# Optimizing a Trainium2 kernel written in Bass

```python
import numpy as np
import jax
import jax.numpy as jnp

def _softmax(x, axis=-1):
    return jax.nn.softmax(x, axis=axis)

def _gelu(x):
    return jax.nn.gelu(x, approximate=True)

def _silu(x):
    return jax.nn.silu(x)

def _sigmoid(x):
    return jax.nn.sigmoid(x)

def _layernorm(x, axis=-1, eps=1e-05):
    m = jnp.mean(x, axis=axis, keepdims=True)
    v = jnp.var(x, axis=axis, keepdims=True)
    return (x - m) / jnp.sqrt(v + eps)

def _scatter_add(tgt, idx, src, axis=0):
    return tgt.at[idx].add(src)

def _segment_sum(src, seg, n):
    return jax.ops.segment_sum(src, seg, n)
kernel_name = 'mk_pixart_resid_d1_seqx_r4_7ef65d'

def setup_inputs(seed: int=0):
    np.random.seed(seed)
    _w = jnp.asarray

    def _rec_inputs():
        import jax
        import jax.numpy as jnp
        _rk = jax.random.key(seed)
        x = -0.0005146 + 1 * jax.random.normal(jax.random.fold_in(_rk, 1), (16, 128, 256), jnp.float32)
        _lenS = 128 - jax.random.randint(jax.random.fold_in(_rk, 7), (16,), 0, max(1, 128 // 4) + 1, jnp.int32)
        _lenS2 = 128 - jax.random.randint(jax.random.fold_in(_rk, 8), (16,), 0, max(1, 128 // 4) + 1, jnp.int32)
        _ctx_1024P = jax.random.normal(jax.random.fold_in(_rk, 11), (16, 16, 256), jnp.float32)
        _ctx_1024c = jax.random.dirichlet(jax.random.fold_in(_rk, 511), 0.3 * jnp.ones((16,), jnp.float32), (16, 128))
        _ctx_1024t = jnp.einsum('bsk,bkd->bsd', _ctx_1024c, _ctx_1024P)
        _ctx_1024t = _ctx_1024t * jax.lax.rsqrt(jnp.mean(jnp.square(_ctx_1024t)) + 1e-12) * 0.953939
        ctx_1024 = -0.000125008 + 0.999885 * (_ctx_1024t + 0.3 * jax.random.normal(jax.random.fold_in(_rk, 611), (16, 128, 256), jnp.float32))
        cond_1024 = -0.00920427 + 1.00102 * jax.random.normal(jax.random.fold_in(_rk, 12), (16, 256), jnp.float32)
        return (x, ctx_1024, cond_1024)
    x, ctx_1024, cond_1024 = _rec_inputs()

    def _L0_xcond_setup():
        import jax, jax.numpy as jnp
        import numpy as np
        DIM = 256
        DIM_HEAD = 64
        HEADS = 16
        INNER = DIM_HEAD * HEADS
        B, N1, N2 = (8, 1024, 64)
        EPS = 1e-05

        def layer_norm(x, w, b):
            mu = jnp.mean(x, axis=-1, keepdims=True)
            var = jnp.var(x, axis=-1, keepdims=True)
            return (x - mu) * jax.lax.rsqrt(var + EPS) * w + b
        key = jax.random.key(seed)
        ks = jax.random.split(key, 10)
        return {'x': jax.random.normal(ks[0], (B, N1, DIM), jnp.float32), 'latents': jax.random.normal(ks[1], (B, N2, DIM), jnp.float32), 'shift': jax.random.normal(ks[2], (B, DIM), jnp.float32), 'scale': jax.random.normal(ks[3], (B, DIM), jnp.float32), 'ln1_w': jnp.ones((DIM,), jnp.float32), 'ln1_b': jnp.zeros((DIM,), jnp.float32), 'ln2_w': jnp.ones((DIM,), jnp.float32), 'ln2_b': jnp.zeros((DIM,), jnp.float32), 'Wq': jax.random.normal(ks[4], (INNER, DIM), jnp.float32) * 0.02, 'Wkv': jax.random.normal(ks[5], (2 * INNER, DIM), jnp.float32) * 0.02, 'Wo': jax.random.normal(ks[6], (DIM, INNER), jnp.float32) * 0.02}
    _L0_xcond_all = _L0_xcond_setup()
    _L0_xcond_in = {k: v for k, v in _L0_xcond_all.items() if k in ('ln1_w', 'ln1_b', 'ln2_w', 'ln2_b', 'Wq', 'Wkv', 'Wo')}
    del _L0_xcond_all

    def _L0_ffn_setup():
        import jax, jax.numpy as jnp
        import numpy as np
        B, S, D, E, F, K = (4, 256, 256, 8, 704, 1)
        key = jax.random.key(seed)
        ks = jax.random.split(key, 8)
        sc = 0.02
        return {'x_bsD': jax.random.normal(ks[0], (B, S, D), jnp.float32), 'router_DE': jax.random.normal(ks[1], (D, E), jnp.float32) * sc, 'w1_eDF': jax.random.normal(ks[2], (E, D, F), jnp.float32) * sc, 'w3_eDF': jax.random.normal(ks[3], (E, D, F), jnp.float32) * sc, 'w2_eFD': jax.random.normal(ks[4], (E, F, D), jnp.float32) * sc, 'ws1_DF': jax.random.normal(ks[5], (D, F), jnp.float32) * sc, 'ws3_DF': jax.random.normal(ks[6], (D, F), jnp.float32) * sc, 'ws2_FD': jax.random.normal(ks[7], (F, D), jnp.float32) * sc}
    _L0_ffn_all = _L0_ffn_setup()
    _L0_ffn_in = {k: v for k, v in _L0_ffn_all.items() if k in ('router_DE', 'w1_eDF', 'w3_eDF', 'w2_eFD', 'ws1_DF', 'ws3_DF', 'ws2_FD')}
    del _L0_ffn_all
    return {'x': x, 'ctx_1024': ctx_1024, 'cond_1024': cond_1024, 'L0_xcond_ln1_w': _L0_xcond_in['ln1_w'], 'L0_xcond_ln1_b': _L0_xcond_in['ln1_b'], 'L0_xcond_ln2_w': _L0_xcond_in['ln2_w'], 'L0_xcond_ln2_b': _L0_xcond_in['ln2_b'], 'L0_xcond_Wq': _L0_xcond_in['Wq'], 'L0_xcond_Wkv': _L0_xcond_in['Wkv'], 'L0_xcond_Wo': _L0_xcond_in['Wo'], 'L0_ffn_router_DE': _L0_ffn_in['router_DE'], 'L0_ffn_w1_eDF': _L0_ffn_in['w1_eDF'], 'L0_ffn_w3_eDF': _L0_ffn_in['w3_eDF'], 'L0_ffn_w2_eFD': _L0_ffn_in['w2_eFD'], 'L0_ffn_ws1_DF': _L0_ffn_in['ws1_DF'], 'L0_ffn_ws3_DF': _L0_ffn_in['ws3_DF'], 'L0_ffn_ws2_FD': _L0_ffn_in['ws2_FD']}

def reference(x, ctx_1024, cond_1024, L0_xcond_ln1_w, L0_xcond_ln1_b, L0_xcond_ln2_w, L0_xcond_ln2_b, L0_xcond_Wq, L0_xcond_Wkv, L0_xcond_Wo, L0_ffn_router_DE, L0_ffn_w1_eDF, L0_ffn_w3_eDF, L0_ffn_w2_eFD, L0_ffn_ws1_DF, L0_ffn_ws3_DF, L0_ffn_ws2_FD):
    import jax
    import jax.numpy as jnp

    def _L0_xcond_ref(x, latents, shift, scale, ln1_w, ln1_b, ln2_w, ln2_b, Wq, Wkv, Wo):
        import jax, jax.numpy as jnp
        import numpy as np
        DIM = 256
        DIM_HEAD = 64
        HEADS = 16
        INNER = DIM_HEAD * HEADS
        B, N1, N2 = (8, 1024, 64)
        EPS = 1e-05

        def layer_norm(x, w, b):
            mu = jnp.mean(x, axis=-1, keepdims=True)
            var = jnp.var(x, axis=-1, keepdims=True)
            return (x - mu) * jax.lax.rsqrt(var + EPS) * w + b
        x = layer_norm(x, ln1_w, ln1_b)
        lat = layer_norm(latents, ln2_w, ln2_b)
        lat = lat * (1.0 + scale[:, None, :]) + shift[:, None, :]
        b, n2, _ = lat.shape
        q = jnp.einsum('bld,ed->ble', lat, Wq)
        kv_in = jnp.concatenate((x, lat), axis=-2)
        kv = jnp.einsum('bld,ed->ble', kv_in, Wkv)
        k, v = jnp.split(kv, 2, axis=-1)

        def to_heads(t):
            bsz, L, _ = t.shape
            return t.reshape(bsz, L, HEADS, DIM_HEAD).transpose(0, 2, 1, 3)
        q, k, v = (to_heads(q), to_heads(k), to_heads(v))
        attn_scale = 1.0 / np.sqrt(np.sqrt(DIM_HEAD)).astype(np.float32)
        logits = jnp.einsum('bhqd,bhkd->bhqk', q * attn_scale, k * attn_scale)
        w = jax.nn.softmax(logits.astype(jnp.float32), axis=-1).astype(logits.dtype)
        out = jnp.einsum('bhqk,bhkd->bhqd', w, v)
        out = out.transpose(0, 2, 1, 3).reshape(b, n2, INNER)
        return jnp.einsum('ble,de->bld', out, Wo)

    def _L0_ffn_ref(x_bsD, router_DE, w1_eDF, w3_eDF, w2_eFD, ws1_DF, ws3_DF, ws2_FD):
        import jax, jax.numpy as jnp
        import numpy as np
        B, S, D, E, F, K = (4, 256, 256, 8, 704, 1)
        b, s, d = x_bsD.shape
        a = b * s
        x_aD = x_bsD.reshape(a, d)
        scores_aE = x_aD @ router_DE
        vals_aK, idx_aK = jax.lax.top_k(scores_aE, K)
        masked_aE = jnp.full_like(scores_aE, -jnp.inf).at[jnp.arange(a)[:, None], idx_aK].set(vals_aK)
        gates_Ea = jax.nn.sigmoid(masked_aE).T
        routed_in_EaD = jax.lax.stop_gradient(gates_Ea[:, :, None] * x_aD[None, :, :])
        mid_EaF = jax.nn.silu(jnp.einsum('ead,edf->eaf', routed_in_EaD, w1_eDF)) * jnp.einsum('ead,edf->eaf', routed_in_EaD, w3_eDF)
        routed_out_EaD = jnp.einsum('eaf,efd->ead', mid_EaF, w2_eFD)
        shared_aD = jax.nn.silu(x_aD @ ws1_DF) * (x_aD @ ws3_DF) @ ws2_FD
        out_aD = shared_aD + routed_out_EaD.sum(axis=0)
        return out_aD.reshape(b, s, d)
    x = x + _L0_xcond_ref(ctx_1024, _layernorm(x, axis=-1), cond_1024, cond_1024, L0_xcond_ln1_w, L0_xcond_ln1_b, L0_xcond_ln2_w, L0_xcond_ln2_b, L0_xcond_Wq, L0_xcond_Wkv, L0_xcond_Wo)
    x = x + _L0_ffn_ref(_layernorm(x, axis=-1), L0_ffn_router_DE, L0_ffn_w1_eDF, L0_ffn_w3_eDF, L0_ffn_w2_eFD, L0_ffn_ws1_DF, L0_ffn_ws3_DF, L0_ffn_ws2_FD)
    return x

_drawn_inputs = setup_inputs


def setup_inputs(seed=0):
    import zlib

    import numpy as np

    out = dict(_drawn_inputs(seed))
    spreads = {'L0_xcond_ln1_w': (1.0, 0.6),
     'L0_xcond_ln1_b': (0.0, 0.796),
     'L0_xcond_ln2_w': (1.0, 0.6),
     'L0_xcond_ln2_b': (0.0, 0.513)}
    factors = {'L0_xcond_Wq': 3.956,
     'L0_ffn_router_DE': 5.817,
     'L0_ffn_w1_eDF': 5.424,
     'L0_ffn_w3_eDF': 5.393,
     'L0_ffn_w2_eFD': 5.406,
     'L0_ffn_ws1_DF': 8.0,
     'L0_ffn_ws3_DF': 8.0,
     'L0_ffn_ws2_FD': 8.0}
    for name, (base, spread) in spreads.items():
        noise = np.random.default_rng([zlib.crc32(name.encode()), seed]).standard_normal(out[name].shape)
        drawn = base * np.exp(spread * noise) if base else spread * noise
        out[name] = jnp.asarray(drawn.astype(out[name].dtype))
    for name, factor in factors.items():
        out[name] = (out[name] * factor).astype(out[name].dtype)
    return out
```

```python
from contextlib import ExitStack

import concourse.bass as bass
from concourse import mybir

FP32 = mybir.dt.float32
FP32R = mybir.dt.float32r
I32 = mybir.dt.int32
ALU = mybir.AluOpType
ACT = mybir.ActivationFunctionType
AX = mybir.AxisListType

NB = 16
P = 128
D = 256
KD = D // 128
NH = 16
DH = 64
INNER = NH * DH
NP = NH // 2
KC = INNER // 128
KEYS = 2 * P
HP = NP // 2
EPS = 1e-5
QSCALE = 1.0 / DH ** 0.5

NE = 8
F = 704
FT = (F + 127) // 128
FM = (FT - 1) * 128
FL = F - FM
TOK = NB * P
NT = TOK // P + NE - 1
GT = 512
NG = TOK // GT
UNITS = 10


def fwidth(f):
    return FL if f == FT - 1 else 128


def build(nc, a, out):
    ctx = ExitStack()
    with ctx:
        def dram(name, shape):
            return nc.dram_tensor(name, shape, FP32, kind="Internal").ap()

        mem = {
            "X": ctx.enter_context(nc.sbuf_tensor("X", [128, NB, D], FP32)),
            "C": ctx.enter_context(nc.sbuf_tensor("C", [128, NB, D], FP32)),
            "IDENT": ctx.enter_context(nc.sbuf_tensor("IDENT", [128, 128], FP32)),
            "PS": ctx.enter_context(nc.psum_tensor("PS", [128, 8, 512], FP32)),
            "xs": dram("xs_sorted", [NT * P, D]),
            "ys": dram("ys_sorted", [NT * P, D]),
        }
        attention_part(nc, a, mem)
        experts_part(nc, a, mem, out)


def attention_part(nc, a, mem):
    X, C, IDENT, PS = mem["X"], mem["C"], mem["IDENT"], mem["PS"]
    ctx = ExitStack()
    with ctx:
        def sb(name, shape, dt=FP32):
            return ctx.enter_context(nc.sbuf_tensor(name, shape, dt))

        def sem(name):
            return ctx.enter_context(nc.semaphore(name))

        WQ = sb("WQ", [128, KD, INNER])
        WKVF = sb("WKVF", [128, KD, 2 * INNER])
        WKVH = sb("WKVH", [128, KD, 2 * INNER], FP32R)
        WKVL = sb("WKVL", [128, KD, 2 * INNER], FP32R)
        WOF = sb("WOF", [128, KC, D])
        WOH = sb("WOH", [128, KC, D], FP32R)
        WOL = sb("WOL", [128, KC, D], FP32R)
        LNP = sb("LNP", [128, 4, KD])
        COND = sb("COND", [128, KD, NB])
        LATA = sb("LATA", [128, KD, NB])
        LATC = sb("LATC", [128, KD, NB])
        AFF = sb("AFF", [128, 2, KD])
        CN = sb("CN", [128, D])
        XN = sb("XN", [128, D])
        ST = sb("ST", [128, 4, 6])
        MV = sb("MV", [128, 4, 2])
        VE = sb("VE", [128, 4])
        RS = sb("RS", [128, 4])
        MHALF = sb("MHALF", [128, 2])
        EPST = sb("EPST", [128, 2])
        RC = sb("RC", [128, D])
        RX = sb("RX", [128, D])
        X2 = sb("X2", [128, D])
        ZERO = sb("ZERO", [128, D])
        KVF = sb("KVF", [128, KD, KEYS])
        KVH = sb("KVH", [128, KD, KEYS], FP32R)
        KVL = sb("KVL", [128, KD, KEYS], FP32R)
        QT = [sb(f"QT{i}", [128, NP, P]) for i in range(2)]
        KT = [sb(f"KT{i}", [128, NP, KEYS]) for i in range(2)]
        V = [sb(f"V{i}", [128, 2, INNER]) for i in range(2)]
        PR = [sb(f"PR{i}", [128, 2, KEYS]) for i in range(2)]
        PT = [sb(f"PT{i}", [128, 4, P]) for i in range(2)]
        NMX = sb("NMX", [128, 2, 2])
        SUM = sb("SUM", [128, 2, 2])
        RINV = sb("RINV", [128, 2, 2])
        OTH = sb("OTH", [128, KC, P], FP32R)
        OTL = sb("OTL", [128, KC, P], FP32R)

        PROJ = [0, 1]
        LG = 2
        PTB = [4, 5]
        OB = 6
        MISC = 7

        d_small = sem("d_small")
        d_first = sem("d_first")
        d_rest = sem("d_rest")
        d_wq = sem("d_wq")
        d_wk = sem("d_wk")
        d_wv = sem("d_wv")
        d_wo = sem("d_wo")
        d_zero = sem("d_zero")
        p_const = sem("p_const")
        p_ident = sem("p_ident")
        p_wo = sem("p_wo")
        p_woh = sem("p_woh")
        a_kv_hi = sem("a_kv_hi")
        v_kv_lo = sem("v_kv_lo")
        v_cond = sem("v_cond")
        v_aff = sem("v_aff")
        v_rows = sem("v_rows")
        v_st = sem("v_st")
        v_mv = sem("v_mv")
        p_ve = sem("p_ve")
        p_rs = sem("p_rs")
        v_xn1 = sem("v_xn1")
        v_xn = sem("v_xn")
        v_st2 = sem("v_st2")
        v_mv2 = sem("v_mv2")
        p_ve2 = sem("p_ve2")
        p_rs2 = sem("p_rs2")
        t_in = sem("t_in")
        v_kvf = sem("v_kvf")
        a_kvh = sem("a_kvh")
        p_kvl = sem("p_kvl")
        t_unit = sem("t_unit")
        a_unit = sem("a_unit")
        t_lg = sem("t_lg")
        v_mx = sem("v_mx")
        a_exp = sem("a_exp")
        v_rinv = sem("v_rinv")
        v_pr = sem("v_pr")
        t_pt = sem("t_pt")
        v_pt = sem("v_pt")
        a_pt = sem("a_pt")
        t_pv = sem("t_pv")
        a_oh = sem("a_oh")
        v_ol = sem("v_ol")
        t_wo = sem("t_wo")
        v_res = sem("v_res")
        v_st3 = sem("v_st3")
        v_mv3 = sem("v_mv3")
        p_ve3 = sem("p_ve3")
        p_rs3 = sem("p_rs3")
        v_x2 = sem("v_x2")

        block = ctx.enter_context(nc.Block())

        @block.sync
        def _(sp):
            def rows(t, lo, hi):
                return t[lo:hi, :, :].rearrange("b p d -> p b d")

            sp.dma_start(C[:, 0:1, :], rows(a["ctx"], 0, 1)).then_inc(d_first, 16)
            sp.dma_start(X[:, 0:1, :], rows(a["x"], 0, 1)).then_inc(d_first, 16)
            sp.dma_start(LNP[:, :, :], a["ln"]).then_inc(d_small, 16)
            sp.dma_start(COND[:, :, :], a["cond"]).then_inc(d_small, 16)
            sp.dma_start(WQ[:, :, :], a["wq_t"].rearrange("(k p) e -> p k e", p=128)).then_inc(d_wq, 16)
            wkv = a["wkv_t"].rearrange("(k p) e -> p k e", p=128)
            sp.dma_start(WKVF[:, :, 0:INNER], wkv[:, :, 0:INNER]).then_inc(d_wk, 16)
            sp.dma_start(WKVF[:, :, INNER:], wkv[:, :, INNER:]).then_inc(d_wv, 16)
            sp.dma_start(C[:, 1:NB, :], rows(a["ctx"], 1, NB)).then_inc(d_rest, 16)
            sp.dma_start(X[:, 1:NB, :], rows(a["x"], 1, NB)).then_inc(d_rest, 16)
            sp.dma_start(WOF[:, :, :], a["wo_t"].rearrange("(k p) d -> p k d", p=128)).then_inc(d_wo, 16)
            sp.wait_ge(p_const, 3)
            for t in range(NT):
                sp.dma_start(mem["xs"][t * P:(t + 1) * P, :], ZERO[:, :]).then_inc(d_zero, 16)
            sp.wait_ge(d_zero, 16 * NT)

        @block.gpsimd
        def _(pool):
            pool.memset(MHALF[:, :], -0.5).then_inc(p_const, 1)
            pool.memset(ZERO[:, :], 0.0).then_inc(p_const, 1)
            pool.memset(EPST[:, :], EPS).then_inc(p_const, 1)
            pool.memset(IDENT[:, :], 0.0).then_inc(p_ident, 1)
            pool.wait_ge(p_ident, 1)
            pool.affine_select(out=IDENT[:, :], in_=IDENT[:, :], compare_op=ALU.not_equal, fill=1.0,
                               base=0, pattern=[[-1, 128]], channel_multiplier=1).then_inc(p_ident, 1)
            pool.wait_ge(p_const, 3)

            def rstd(lo, n, var_ready, ve_sem, done, count):
                pool.wait_ge(var_ready, count)
                pool.tensor_tensor(VE[:, lo:lo + n], MV[:, lo:lo + n, 1], EPST[:, 0:n], ALU.add).then_inc(ve_sem, 1)
                pool.wait_ge(ve_sem, count)
                pool.tensor_tensor(RS[:, lo:lo + n], VE[:, lo:lo + n], MHALF[:, 0:n], ALU.pow).then_inc(done, 1)

            def kv_lo(n):
                pool.wait_ge(a_kvh, n + 1)
                pool.tensor_tensor(KVL[:, :, :], KVF[:, :, :], KVH[:, :, :].bitcast(FP32),
                                   ALU.subtract).then_inc(p_kvl, 1)

            def batch(b, first=False, last=False):
                if not last:
                    rstd(0, 2, v_mv, p_ve, p_rs, b + 2)
                    rstd(2, 1, v_mv2, p_ve2, p_rs2, b + 2)
                    kv_lo(b + 1)
                if not first:
                    rstd(3, 1, v_mv3, p_ve3, p_rs3, b)

            rstd(0, 2, v_mv, p_ve, p_rs, 1)
            rstd(2, 1, v_mv2, p_ve2, p_rs2, 1)
            kv_lo(0)
            batch(0, first=True)
            pool.wait_ge(d_wo, 16)
            pool.tensor_copy(WOH[:, :, :], WOF[:, :, :]).then_inc(p_woh, 1)
            pool.wait_ge(p_woh, 1)
            pool.tensor_tensor(WOL[:, :, :], WOF[:, :, :], WOH[:, :, :].bitcast(FP32), ALU.subtract).then_inc(p_wo, 1)
            with pool.Fori(0, NB // 2 - 1) as i:
                batch(2 * i + 1)
                batch(2 * i + 2)
            batch(NB - 1, last=True)
            rstd(3, 1, v_mv3, p_ve3, p_rs3, NB)

        def row(t, b):
            return t[:, b, :] if isinstance(b, int) else t[:, bass.ds(b, 1), :].rearrange("p a d -> p (a d)")

        def col(t, b):
            return t[:, :, b] if isinstance(b, int) else t[:, :, bass.ds(b, 1)].rearrange("p k a -> p (k a)")

        @block.scalar
        def _(act):
            def kv_hi(n):
                act.wait_ge(v_kvf, n + 1)
                act.activation(KVH[:, :, :], KVF[:, :, :], ACT.Copy).then_inc(a_kvh, 1)

            def unit(n, k, par, waits=True):
                act.wait_ge(t_unit, UNITS * n + k + 1)
                src = PS[:, PROJ[k % 2], :]
                if k < 2:
                    if k == 0 and waits:
                        act.wait_ge(t_pv, NP * (n - 1))
                    act.activation(QT[par][:, 4 * k:4 * k + 4, :], src.rearrange("p (j q) -> p j q", j=4),
                                   ACT.Copy, scale=QSCALE).then_inc(a_unit, 1)
                elif k < 6:
                    j = 2 * (k - 2)
                    act.activation(KT[par][:, j:j + 2, :], src.rearrange("p (j q) -> p j q", j=2),
                                   ACT.Copy).then_inc(a_unit, 1)
                else:
                    half, tile = (k - 6) // 2, (k - 6) % 2
                    act.activation(V[par][:, tile, 512 * half:512 * half + 512], src, ACT.Copy).then_inc(a_unit, 1)

            def exps(b, j):
                for h in range(2):
                    if h == 0:
                        act.wait_ge(v_mx, NP * b + j + 1)
                        if not (isinstance(b, int) and NP * b + j < 2):
                            act.wait_ge(t_pt, NP * b + j - 1)
                    act.activation(PR[j % 2][:, h, :], PS[:, LG + h, 0:KEYS], ACT.Exp, bias=NMX[:, j % 2, h:h + 1],
                                   accum_out=SUM[:, j % 2, h:h + 1]).then_inc(a_exp, 1)

            def copy_pt(b, j):
                act.wait_ge(t_pt, NP * b + j + 1)
                if not (isinstance(b, int) and NP * b + j < 2):
                    act.wait_ge(t_pv, NP * b + j - 1)
                act.activation(PT[j % 2][:, :, :], PS[:, PTB[j % 2], :].rearrange("p (c q) -> p c q", c=4),
                               ACT.Copy).then_inc(a_pt, 1)

            def o_hi(b, half):
                act.wait_ge(t_pv, NP * b + HP * (half + 1))
                if half == 0 and not (isinstance(b, int) and b == 0):
                    act.wait_ge(t_wo, b)
                act.activation(OTH[:, HP * half:HP * half + HP, :], PS[:, OB, :].rearrange("p (j q) -> p j q", j=HP),
                               ACT.Copy).then_inc(a_oh, 1)

            def batch(b, par, first=False, last=False):
                for j in range(NP):
                    if j > 0 and j % 2 == 0:
                        copy_pt(b, j - 1)
                    if j == 0 and not first:
                        copy_pt(b - 1, NP - 1)
                    if j == 1 and not first:
                        o_hi(b - 1, 1)
                    exps(b, j)
                    if j == HP + 1:
                        o_hi(b, 0)
                    for n, k in filler(b, j, last):
                        unit(n, k, par if k >= 8 else 1 - par)
                    if j == 3 and not last:
                        kv_hi(b + 1)

            for half, ready in ((0, d_wk), (1, d_wv)):
                act.wait_ge(ready, 16)
                act.activation(WKVH[:, :, INNER * half:INNER * (half + 1)],
                               WKVF[:, :, INNER * half:INNER * (half + 1)], ACT.Copy).then_inc(a_kv_hi, 1)
                if half == 0:
                    kv_hi(0)
                    for k in range(2):
                        unit(0, k, 0, waits=False)
            for k in range(2, 8):
                unit(0, k, 0, waits=False)
            batch(0, 0, first=True)
            with act.Fori(0, NB // 2 - 1) as i:
                batch(2 * i + 1, 1)
                batch(2 * i + 2, 0)
            batch(NB - 1, 1, last=True)
            copy_pt(NB - 1, NP - 1)
            o_hi(NB - 1, 1)

        @block.vector
        def _(dve):
            def norm_stats(n):
                dve.tensor_copy(RC[:, :], row(C, n))
                dve.tensor_copy(RX[:, :], row(X, n)).then_inc(v_rows, 1)
                dve.wait_ge(v_rows, n + 1)
                dve.bn_stats(ST[:, 0, :], RC[:, :])
                dve.bn_stats(ST[:, 1, :], RX[:, :]).then_inc(v_st, 1)
                dve.wait_ge(v_st, n + 1)
                dve.nop(nofuse=True)
                dve.bn_aggr(MV[:, 0, :], ST[:, 0, :])
                dve.bn_aggr(MV[:, 1, :], ST[:, 1, :]).then_inc(v_mv, 1)

            def norm_rows(n, guard=True):
                dve.wait_ge(p_rs, n + 1)
                if guard:
                    dve.wait_ge(t_in, n)
                dve.tensor_scalar(CN[:, :], RC[:, :], MV[:, 0, 0:1], RS[:, 0:1], ALU.subtract, ALU.mult)
                dve.tensor_scalar(XN[:, :], RX[:, :], MV[:, 1, 0:1], RS[:, 1:2], ALU.subtract, ALU.mult)\
                   .then_inc(v_xn1, 1)
                dve.wait_ge(v_xn1, n + 1)
                dve.bn_stats(ST[:, 2, :], XN[:, :]).then_inc(v_st2, 1)
                dve.wait_ge(v_st2, n + 1)
                dve.nop(nofuse=True)
                dve.bn_aggr(MV[:, 2, :], ST[:, 2, :]).then_inc(v_mv2, 1)

            def norm_again(n):
                dve.tensor_copy(AFF[:, 0, :], col(LATA, n))
                dve.tensor_copy(AFF[:, 1, :], col(LATC, n)).then_inc(v_aff, 1)
                dve.wait_ge(p_rs2, n + 1)
                dve.tensor_scalar(XN[:, :], XN[:, :], MV[:, 2, 0:1], RS[:, 2:3], ALU.subtract, ALU.mult)\
                   .then_inc(v_xn, 1)

            def modulate(n, guard=True):
                dve.wait_ge(t_in, n + 1)
                dve.wait_ge(v_aff, n + 1)
                if guard:
                    dve.wait_ge(p_kvl, n)
                for k in range(KD):
                    src = PS[:, MISC, KEYS * k:KEYS * (k + 1)]
                    dve.tensor_scalar(KVF[:, k, 0:P], src[:, 0:P], LNP[:, 0, k:k + 1], LNP[:, 1, k:k + 1],
                                      ALU.mult, ALU.add)
                    last = dve.tensor_scalar(KVF[:, k, P:KEYS], src[:, P:KEYS], AFF[:, 0, k:k + 1],
                                             AFF[:, 1, k:k + 1], ALU.mult, ALU.add)
                last.then_inc(v_kvf, 1)

            def row_max(b, j):
                dve.wait_ge(t_lg, NP * b + j + 1)
                if not (isinstance(b, int) and NP * b + j < 2):
                    dve.wait_ge(a_exp, 2 * (NP * b + j - 1))
                dve.tensor_reduce(NMX[:, j % 2, :], PS[:, LG:LG + 2, 0:KEYS], AX.X, ALU.max, negate=True)\
                   .then_inc(v_mx, 1)

            def normalise(b, j):
                dve.wait_ge(a_exp, 2 * (NP * b + j + 1))
                dve.reciprocal(RINV[:, j % 2, :], SUM[:, j % 2, :]).then_inc(v_rinv, 1)
                dve.wait_ge(v_rinv, NP * b + j + 1)
                for h in range(2):
                    last = dve.tensor_scalar(PR[j % 2][:, h, :], PR[j % 2][:, h, :], RINV[:, j % 2, h:h + 1], None,
                                             ALU.mult)
                last.then_inc(v_pr, 1)

            def copy_pt(b, j):
                dve.wait_ge(t_pt, NP * b + j + 1)
                if not (isinstance(b, int) and NP * b + j < 2):
                    dve.wait_ge(t_pv, NP * b + j - 1)
                dve.tensor_copy(PT[j % 2][:, :, :], PS[:, PTB[j % 2], :].rearrange("p (c q) -> p c q", c=4))\
                   .then_inc(v_pt, 1)

            def o_lo(b, half):
                dve.wait_ge(a_oh, 2 * b + half + 1)
                lo, hi = HP * half, HP * half + HP
                dve.tensor_tensor(OTL[:, lo:hi, :], PS[:, OB, :].rearrange("p (j q) -> p j q", j=HP),
                                  OTH[:, lo:hi, :].bitcast(FP32), ALU.subtract).then_inc(v_ol, 1)

            def residual(b):
                dve.wait_ge(t_wo, b + 1)
                dve.tensor_tensor(X2[:, :], PS[:, MISC, 0:D], row(X, b), ALU.add).then_inc(v_res, 1)
                dve.wait_ge(v_res, b + 1)
                dve.bn_stats(ST[:, 3, :], X2[:, :]).then_inc(v_st3, 1)
                dve.tensor_copy(row(X, b), X2[:, :])
                dve.wait_ge(v_st3, b + 1)
                dve.nop(nofuse=True)
                dve.bn_aggr(MV[:, 3, :], ST[:, 3, :]).then_inc(v_mv3, 1)

            def expert_input(b):
                dve.wait_ge(p_rs3, b + 1)
                dve.tensor_scalar(row(C, b), X2[:, :], MV[:, 3, 0:1], RS[:, 3:4], ALU.subtract, ALU.mult)\
                   .then_inc(v_x2, 1)

            def batch(b, first=False, last=False):
                for j in range(NP):
                    row_max(b, j)
                    if j % 2:
                        copy_pt(b, j - 1)
                    if j == 1 and not first:
                        o_lo(b - 1, 1)
                    normalise(b, j)
                    if j == HP + 1:
                        o_lo(b, 0)
                    if not last:
                        if j == 0:
                            if first:
                                dve.wait_ge(d_rest, 32)
                            norm_stats(b + 1)
                        elif j == 1:
                            norm_rows(b + 1)
                        elif j == 2:
                            norm_again(b + 1)
                        elif j == 3:
                            if not first:
                                residual(b - 1)
                            modulate(b + 1)
                    elif j == 3:
                        residual(b - 1)
                    if j == 5 and not first:
                        expert_input(b - 1)

            dve.wait_ge(d_first, 32)
            norm_stats(0)
            dve.wait_ge(d_small, 16 * 2)
            dve.tensor_scalar(LATA[:, :, :], COND[:, :, :], 1.0, None, ALU.add).then_inc(v_cond, 1)
            dve.wait_ge(v_cond, 1)
            for k in range(KD):
                dve.tensor_scalar(LATC[:, k, :], LATA[:, k, :], LNP[:, 3, k:k + 1], None, ALU.mult).then_inc(v_cond, 1)
            dve.wait_ge(v_cond, 3)
            for k in range(KD):
                dve.tensor_scalar(LATA[:, k, :], LATA[:, k, :], LNP[:, 2, k:k + 1], None, ALU.mult)
            dve.tensor_tensor(LATC[:, :, :], LATC[:, :, :], COND[:, :, :], ALU.add).then_inc(v_cond, 1)
            dve.wait_ge(v_cond, 4)
            norm_rows(0, guard=False)
            norm_again(0)
            modulate(0, guard=False)
            for half in range(2):
                dve.wait_ge(a_kv_hi, half + 1)
                part = slice(INNER * half, INNER * (half + 1))
                dve.tensor_tensor(WKVL[:, :, part], WKVF[:, :, part], WKVH[:, :, part].bitcast(FP32),
                                  ALU.subtract).then_inc(v_kv_lo, 1)
            batch(0, first=True)
            with dve.Fori(0, NB // 2 - 1) as i:
                batch(2 * i + 1)
                batch(2 * i + 2)
            batch(NB - 1, last=True)
            o_lo(NB - 1, 1)
            residual(NB - 1)
            expert_input(NB - 1)

        @block.tensor
        def _(pe):
            def transpose_inputs(n, guard=True):
                pe.wait_ge(v_xn, n + 1)
                if guard:
                    pe.wait_ge(v_res, n - 1)
                for k in range(KD):
                    for i, src in enumerate((CN, XN)):
                        last = pe.transpose(PS[:, MISC, KEYS * k + P * i:KEYS * k + P * (i + 1)],
                                            src[:, 128 * k:128 * (k + 1)], IDENT[:, :])
                last.then_inc(t_in, 1)

            def split3(dst, stat, mov, steps):
                todo = [(k, s, m) for k in range(steps) for s, m in ((0, 0), (0, 1), (1, 0))]
                for n, (k, s, m) in enumerate(todo):
                    last = pe.matmul(dst, stat(s, k), mov(m, k), start=n == 0, stop=n == len(todo) - 1)
                return last

            kv = (KVH, KVL)
            wkv = (WKVH, WKVL)
            oT = (OTH, OTL)
            wo = (WOH, WOL)

            def unit(n, k, free=True):
                if free:
                    pe.wait_ge(a_unit, UNITS * n + k - 1)
                dst = PS[:, PROJ[k % 2], :]
                if k < 2:
                    if k == 0:
                        pe.wait_ge(v_kvf, n + 1)
                    for j in range(4):
                        e = 128 * (4 * k + j)
                        for c in range(KD):
                            last = pe.matmul(dst[:, P * j:P * (j + 1)], WQ[:, c, e:e + 128], KVF[:, c, P:KEYS],
                                             start=c == 0, stop=c == KD - 1)
                elif k < 6:
                    if k == 2:
                        pe.wait_ge(a_kvh, n + 1)
                        pe.wait_ge(p_kvl, n + 1)
                    for j in range(2):
                        e = 128 * (2 * (k - 2) + j)
                        last = split3(dst[:, KEYS * j:KEYS * (j + 1)], lambda s, c: wkv[s][:, c, e:e + 128],
                                      lambda m, c: kv[m][:, c, :], KD)
                else:
                    half, tile = (k - 6) // 2, (k - 6) % 2
                    e = INNER + 512 * half
                    last = split3(dst, lambda s, c: kv[s][:, c, P * tile:P * (tile + 1)],
                                  lambda m, c: wkv[m][:, c, e:e + 512], KD)
                last.then_inc(t_unit, 1)

            def logits(b, j, par):
                pe.wait_ge(a_unit, UNITS * b + 3 + j // 2)
                if not (isinstance(b, int) and NP * b + j < 1):
                    pe.wait_ge(a_exp, 2 * (NP * b + j))
                for h in range(2):
                    part = slice(DH * h, DH * (h + 1))
                    last = pe.matmul(PS[:, LG + h, 0:KEYS], QT[par][part, j, :], KT[par][part, j, :],
                                     start=True, stop=True)
                last.then_inc(t_lg, 1)

            def transpose_probs(b, j):
                pe.wait_ge(v_pr, NP * b + j + 1)
                if not (isinstance(b, int) and NP * b + j < 2):
                    pe.wait_ge(a_pt if j % 2 else v_pt, HP * b + j // 2)
                for h in range(2):
                    for t in range(2):
                        c = 2 * h + t
                        last = pe.transpose(PS[:, PTB[j % 2], P * c:P * (c + 1)], PR[j % 2][:, h, P * t:P * (t + 1)],
                                            IDENT[:, :])
                last.then_inc(t_pt, 1)

            def times_v(b, j, par):
                pe.wait_ge(a_unit, UNITS * b + (8 if j < HP else 10))
                pe.wait_ge(a_pt if j % 2 else v_pt, HP * b + j // 2 + 1)
                if j % HP == 0 and not (isinstance(b, int) and b == 0 and j == 0):
                    pe.wait_ge(v_ol, 2 * b + j // HP)
                for t in range(2):
                    for h in range(2):
                        e = 128 * j + DH * h
                        last = pe.matmul(PS[DH * h:DH * (h + 1), OB, P * (j % HP):P * (j % HP + 1)],
                                         V[par][:, t, e:e + DH], PT[j % 2][:, 2 * h + t, :],
                                         start=t == 0, stop=t == 1)
                last.then_inc(t_pv, 1)

            def output_projection(b):
                pe.wait_ge(v_ol, 2 * b + 2)
                pe.wait_ge(v_kvf, b + 2 if not (isinstance(b, int) and b == NB - 1) else NB)
                split3(PS[:, MISC, 0:D], lambda s, c: oT[s][:, c, :], lambda m, c: wo[m][:, c, :], KC)\
                    .then_inc(t_wo, 1)

            def batch(b, par, first=False, last=False):
                for j in range(NP):
                    logits(b, j, par)
                    if j:
                        transpose_probs(b, j - 1)
                    elif not first:
                        transpose_probs(b - 1, NP - 1)
                    if j == 2 and not first:
                        output_projection(b - 1)
                    if j == 3 and not last:
                        transpose_inputs(b + 1)
                    for n, k in filler(b, j, last):
                        unit(n, k)
                    if j:
                        times_v(b, j - 1, par)
                    elif not first:
                        times_v(b - 1, NP - 1, 1 - par)

            pe.wait_ge(p_ident, 2)
            transpose_inputs(0, guard=False)
            pe.wait_ge(d_wq, 16)
            for k in range(8):
                if k == 2:
                    pe.wait_ge(v_kv_lo, 1)
                if k == 6:
                    pe.wait_ge(v_kv_lo, 2)
                unit(0, k, free=k > 1)
            batch(0, 0, first=True)
            pe.wait_ge(p_wo, 1)
            with pe.Fori(0, NB // 2 - 1) as i:
                batch(2 * i + 1, 1)
                batch(2 * i + 2, 0)
            batch(NB - 1, 1, last=True)
            transpose_probs(NB - 1, NP - 1)
            times_v(NB - 1, NP - 1, 1)
            output_projection(NB - 1)


def filler(b, j, last):
    own = {0: [8], 1: [9]}
    following = {4: [0, 1], 5: [2, 3], 6: [4, 5], 7: [6, 7]}
    return [(b, k) for k in own.get(j, [])] + ([] if last else [(b + 1, k) for k in following.get(j, [])])


def experts_part(nc, a, mem, out):
    X, C, IDENT, PS = mem["X"], mem["C"], mem["IDENT"], mem["PS"]
    xs, ys = mem["xs"], mem["ys"]
    ctx = ExitStack()
    with ctx:
        def sb(name, shape, dt=FP32):
            return ctx.enter_context(nc.sbuf_tensor(name, shape, dt))

        def sem(name):
            return ctx.enter_context(nc.semaphore(name))

        W13 = [sb(f"W13_{i}", [128, KD, 2 * F]) for i in range(2)]
        W2 = [sb(f"W2_{i}", [128, FT, D]) for i in range(2)]
        WS13 = [sb(f"WS13{p}", [128, KD, 2 * F], FP32R) for p in "HL"]
        WS2 = [sb(f"WS2{p}", [128, FT, D], FP32R) for p in "HL"]
        RT = sb("RT", [128, KD, NE])
        XTF = [sb(f"XTF{i}", [128, KD, P]) for i in range(2)]
        XT = [sb(f"XT{p}", [128, KD, TOK], FP32R) for p in "HL"]
        MIDF = [sb(f"MIDF{i}", [128, GT]) for i in range(2)]
        MID = [sb(f"MID{p}", [128, FT, GT], FP32R) for p in "HL"]
        SC = sb("SC", [128, NB, NE])
        BEST = sb("BEST", [128, NB])
        ONE = sb("ONE", [128, NB, NE])
        CAND = sb("CAND", [128, NB, NE])
        IDX = sb("IDX", [128, NB])
        IOTA_I = sb("IOTA_I", [128, NE + NE * NB + NT * NE], I32)
        IOTA = sb("IOTA", [128, NE + NE * NB + NT * NE])
        UPPER = sb("UPPER", [128, 128])
        ONES = sb("ONES", [128, 128])
        GATE = sb("GATE", [128, NB])
        RANK = sb("RANK", [128, NB, NE])
        CNT = sb("CNT", [128, NB + 1, NE])
        NTE = sb("NTE", [128, NE])
        HIT = sb("HIT", [128, NE, NB])
        ENDT = sb("ENDT", [128, NE + 1])
        OWN = sb("OWN", [128, NT, NE])
        ETF = sb("ETF", [128, NT])
        ETI = sb("ETI", [1, NT], I32)
        POSF = sb("POSF", [128, NB])
        POSI = sb("POSI", [128, NB], I32)
        XS = [sb(f"XS{i}", [128, D]) for i in range(2)]
        XST = [sb(f"XST{i}", [128, KD, P]) for i in range(2)]
        SIL = sb("SIL", [128, F])
        MR = sb("MR", [128, F])
        MRT = sb("MRT", [128, FT, P])
        YS = [sb(f"YS{i}", [128, D]) for i in range(2)]
        G = [sb(f"G{i}", [128, D]) for i in range(2)]

        TRB = [0, 1]
        RTB = 2
        HB = [(3, 4), (5, 6)]
        OUTB = [7, 0]
        EH = 1
        EM = 4
        EX = 6
        EY = 7

        d_ws = sem("d_ws")
        d_rt = sem("d_rt")
        a_wsh = sem("a_wsh")
        v_wsl = sem("v_wsl")
        p_iota = sem("p_iota")
        p_mask = sem("p_mask")
        v_iota = sem("v_iota")
        t_xt = sem("t_xt")
        a_xtf = sem("a_xtf")
        a_xth = sem("a_xth")
        p_xtl = sem("p_xtl")
        t_sc = sem("t_sc")
        v_rt = sem("v_rt")
        a_gate = sem("a_gate")
        t_rank = sem("t_rank")
        v_xg = sem("v_xg")
        v_pos = sem("v_pos")
        v_et = sem("v_et")
        d_sc = sem("d_sc")
        t_h = sem("t_h")
        a_sil = sem("a_sil")
        v_mid = sem("v_mid")
        a_midh = sem("a_midh")
        p_midl = sem("p_midl")
        t_so = sem("t_so")
        v_so = sem("v_so")
        d_xs = [sem(f"d_xs{i}") for i in range(2)]
        d_w13 = [sem(f"d_w13{i}") for i in range(2)]
        d_w2 = [sem(f"d_w2{i}") for i in range(2)]
        d_y = [sem(f"d_y{i}") for i in range(2)]
        t_ex = sem("t_ex")
        a_ex = sem("a_ex")
        t_eh = sem("t_eh")
        a_es = sem("a_es")
        v_em = sem("v_em")
        t_em = sem("t_em")
        v_et1 = sem("v_et1")
        a_et2 = sem("a_et2")
        t_ey = sem("t_ey")
        v_ey = sem("v_ey")
        d_g = [sem(f"d_g{i}") for i in range(2)]
        v_out = sem("v_out")
        d_out = sem("d_out")

        block = ctx.enter_context(nc.Block())

        def tile_rows(t, n):
            return t[n * P:(n + 1) * P, :] if isinstance(n, int) else t[bass.ds(n * P, P), :]

        def load_w2(sp, dst, src, done):
            sp.dma_start(dst[:, 0:FT - 1, :], src[0:128 * (FT - 1), :].rearrange("(k p) d -> p k d", p=128))\
              .then_inc(done, 16)
            sp.dma_start(dst[0:FL, FT - 1, :], src[128 * (FT - 1):F, :]).then_inc(done, 16)

        @block.sync
        def _(sp):
            for i, n in enumerate(("ws1", "ws3")):
                src = a[n].rearrange("(k p) f -> p k f", p=128)
                sp.dma_start(W13[0][:, :, FM * i:FM * (i + 1)], src[:, :, 0:FM]).then_inc(d_ws, 16)
                sp.dma_start(W13[0][:, :, 2 * FM + FL * i:2 * FM + FL * (i + 1)], src[:, :, FM:F]).then_inc(d_ws, 16)
            load_w2(sp, W2[0], a["ws2"], d_ws)
            sp.dma_start(RT[:, :, :], a["router"].rearrange("(k p) e -> p k e", p=128)).then_inc(d_rt, 16)

            def load_expert(t, par, first=False):
                e = sp.value_load(ETI[0:1, t:t + 1] if isinstance(t, int) else ETI[0:1, bass.ds(t, 1)],
                                  min_val=0, max_val=NE - 1)
                if not first:
                    sp.wait_ge(t_ex, t - 1)
                sp.dma_start(XS[par][:, :], tile_rows(xs, t)).then_inc(d_xs[par], 16)
                if not first:
                    sp.wait_ge(t_eh, t - 1)
                for i, n in enumerate(("w1", "w3")):
                    sp.dma_start(W13[par][:, :, F * i:F * (i + 1)],
                                 a[n][bass.ds(e, 1), :, :].rearrange("a (k p) f -> p (a k) f", p=128))\
                      .then_inc(d_w13[par], 16)
                if not first:
                    sp.wait_ge(t_ey, t - 1)
                load_w2(sp, W2[par], a["w2"][bass.ds(e, 1), :, :].rearrange("a f d -> (a f) d"), d_w2[par])

            def store(t, par):
                sp.wait_ge(v_ey, t + 1)
                sp.dma_start(tile_rows(ys, t), YS[par][:, :]).then_inc(d_y[par], 16)

            sp.wait_ge(v_et, 1)
            sp.wait_ge(v_wsl, 2)
            sp.wait_ge(d_sc, 16 * NB)
            load_expert(0, 0, first=True)
            load_expert(1, 1, first=True)
            with sp.Fori(0, (NT - 3) // 2) as i:
                load_expert(2 * i + 2, 0)
                store(2 * i, 0)
                load_expert(2 * i + 3, 1)
                store(2 * i + 1, 1)
            load_expert(NT - 1, 0)
            for t in range(NT - 3, NT):
                store(t, t % 2)
            for b in range(NB):
                sp.wait_ge(v_out, b + 1)
                sp.dma_start(out[b], X[:, b, :]).then_inc(d_out, 16)
            sp.wait_ge(d_out, 16 * NB)

        @block.gpsimd
        def _(pool):
            pool.iota(IOTA_I[:, 0:NE], pattern=[[1, NE]], base=0, channel_multiplier=0).then_inc(p_iota, 1)
            pool.iota(IOTA_I[:, NE:NE + NE * NB], pattern=[[0, NE], [P, NB]], base=0, channel_multiplier=0)\
                .then_inc(p_iota, 1)
            pool.iota(IOTA_I[:, NE + NE * NB:], pattern=[[1, NT], [0, NE]], base=0, channel_multiplier=0)\
                .then_inc(p_iota, 1)
            pool.memset(ONES[:, :], 1.0).then_inc(p_mask, 1)
            pool.wait_ge(p_mask, 1)
            pool.affine_select(out=UPPER[:, :], in_=ONES[:, :], compare_op=ALU.is_gt, fill=0.0,
                               base=0, pattern=[[1, 128]], channel_multiplier=-1).then_inc(p_mask, 1)

            def x_lo(t, par):
                pool.wait_ge(a_xth, t + 1)
                dst = XT[1][:, :, t * P:(t + 1) * P] if isinstance(t, int) else XT[1][:, :, bass.ds(t * P, P)]
                hi = XT[0][:, :, t * P:(t + 1) * P] if isinstance(t, int) else XT[0][:, :, bass.ds(t * P, P)]
                pool.tensor_tensor(dst, XTF[par][:, :, :], hi.bitcast(FP32), ALU.subtract).then_inc(p_xtl, 1)

            with pool.Fori(0, NB // 2) as i:
                x_lo(2 * i, 0)
                x_lo(2 * i + 1, 1)

            pool.wait_ge(v_xg, 1)
            pool.wait_ge(v_pos, 1)
            for b in range(NB):
                pool.indirect_dma_start(out=xs, out_offset=bass.IndirectOffsetOnAxis(ap=POSI[:, b:b + 1], axis=0),
                                        in_=C[:, b, :], in_offset=None).then_inc(d_sc, 16)

            def mid_lo(g, f):
                pool.wait_ge(a_midh, FT * g + f + 1)
                w = fwidth(f)
                pool.tensor_tensor(MID[1][0:w, f, :], MIDF[f % 2][0:w, :], MID[0][0:w, f, :].bitcast(FP32),
                                   ALU.subtract).then_inc(p_midl, 1)

            with pool.Fori(0, NG) as g:
                for f in range(FT):
                    mid_lo(g, f)

            for par in range(2):
                pool.wait_ge(d_y[par], 16 * ((NT + 1 - par) // 2))
            for b in range(NB):
                if b >= 2:
                    pool.wait_ge(v_out, b - 1)
                pool.indirect_dma_start(out=G[b % 2][:, :], out_offset=None, in_=ys,
                                        in_offset=bass.IndirectOffsetOnAxis(ap=POSI[:, b:b + 1], axis=0))\
                    .then_inc(d_g[b % 2], 16)

        @block.scalar
        def _(act):
            act.wait_ge(d_ws, 16 * 6)
            act.activation(WS13[0][:, :, :], W13[0][:, :, :], ACT.Copy).then_inc(a_wsh, 1)
            act.activation(WS2[0][:, 0:FT - 1, :], W2[0][:, 0:FT - 1, :], ACT.Copy)
            act.activation(WS2[0][0:FL, FT - 1, :], W2[0][0:FL, FT - 1, :], ACT.Copy).then_inc(a_wsh, 1)

            def x_hi(t, par, free=True):
                act.wait_ge(t_xt, t + 1)
                if free:
                    act.wait_ge(p_xtl, t - 1)
                    act.wait_ge(t_sc, t - 1)
                act.activation(XTF[par][:, :, :], PS[:, TRB[par], 0:KD * P].rearrange("p (k q) -> p k q", k=KD),
                               ACT.Copy).then_inc(a_xtf, 1)
                act.wait_ge(a_xtf, t + 1)
                dst = XT[0][:, :, t * P:(t + 1) * P] if isinstance(t, int) else XT[0][:, :, bass.ds(t * P, P)]
                act.activation(dst, XTF[par][:, :, :], ACT.Copy).then_inc(a_xth, 1)

            x_hi(0, 0, free=False)
            x_hi(1, 1, free=False)
            with act.Fori(1, NB // 2) as i:
                x_hi(2 * i, 0)
                x_hi(2 * i + 1, 1)

            act.wait_ge(v_rt, 1)
            act.activation(GATE[:, :], BEST[:, :], ACT.Exp, scale=-1.0).then_inc(a_gate, 1)

            def shared_act(g, f):
                w = fwidth(f)
                n = FT * g + f
                act.wait_ge(t_h, n + 1)
                if not (isinstance(n, int) and n == 0):
                    act.wait_ge(p_midl, n)
                act.activation(SIL[0:w, 0:GT], PS[0:w, HB[f % 2][0], :], ACT.Silu).then_inc(a_sil, 1)
                act.wait_ge(v_mid, n + 1)
                if f == 0 and not (isinstance(g, int) and g == 0):
                    act.wait_ge(t_so, 4 * g)
                act.activation(MID[0][0:w, f, :], MIDF[f % 2][0:w, :], ACT.Copy).then_inc(a_midh, 1)

            for f in range(FT):
                shared_act(0, f)
            with act.Fori(1, NG) as g:
                for f in range(FT):
                    shared_act(g, f)

            def copy_x(t, par, free=True):
                act.wait_ge(t_ex, t + 1)
                if free:
                    act.wait_ge(t_eh, t - 1)
                act.activation(XST[par][:, :, :], PS[:, EX, 0:KD * P].rearrange("p (k q) -> p k q", k=KD),
                               ACT.Copy).then_inc(a_ex, 1)

            def routed_act(t, par, copy_next):
                if not (isinstance(t, int) and t == 0):
                    act.wait_ge(t_em, t)
                    act.activation(MRT[:, FT - 2, :], PS[:, EM + 1, 0:P], ACT.Copy)
                    act.activation(MRT[0:FL, FT - 1, :], PS[0:FL, EM + 1, P:2 * P], ACT.Copy).then_inc(a_et2, 1)
                if copy_next:
                    copy_x(t + 1, 1 - par, free=not (isinstance(t, int) and t == 0))
                act.wait_ge(t_eh, t + 1)
                if not (isinstance(t, int) and t == 0):
                    act.wait_ge(v_em, t)
                act.activation(SIL[:, :], PS[:, EH:EH + 3, :].rearrange("p b f -> p (b f)")[:, 0:F], ACT.Silu)\
                   .then_inc(a_es, 1)

            copy_x(0, 0, free=False)
            routed_act(0, 0, True)
            with act.Fori(0, (NT - 3) // 2) as i:
                routed_act(2 * i + 1, 1, True)
                routed_act(2 * i + 2, 0, True)
            routed_act(NT - 2, 1, True)
            routed_act(NT - 1, 0, False)
            act.wait_ge(t_em, NT)
            act.activation(MRT[:, FT - 2, :], PS[:, EM + 1, 0:P], ACT.Copy)
            act.activation(MRT[0:FL, FT - 1, :], PS[0:FL, EM + 1, P:2 * P], ACT.Copy).then_inc(a_et2, 1)

        @block.vector
        def _(dve):
            done = [0]

            def step(ins):
                done[0] += 1
                ins.then_inc(v_rt, 1)
                dve.wait_ge(v_rt, done[0])

            def over_tiles(t):
                return t.rearrange("p (a e) -> p a e", a=1).to_broadcast([128, NB, NE])

            dve.wait_ge(p_iota, 3)
            dve.tensor_copy(IOTA[:, :], IOTA_I[:, :]).then_inc(v_iota, 1)
            dve.wait_ge(a_wsh, 1)
            dve.tensor_tensor(WS13[1][:, :, :], W13[0][:, :, :], WS13[0][:, :, :].bitcast(FP32), ALU.subtract)\
               .then_inc(v_wsl, 1)
            dve.wait_ge(a_wsh, 2)
            dve.tensor_tensor(WS2[1][:, 0:FT - 1, :], W2[0][:, 0:FT - 1, :], WS2[0][:, 0:FT - 1, :].bitcast(FP32),
                              ALU.subtract)
            dve.tensor_tensor(WS2[1][0:FL, FT - 1, :], W2[0][0:FL, FT - 1, :],
                              WS2[0][0:FL, FT - 1, :].bitcast(FP32), ALU.subtract).then_inc(v_wsl, 1)

            dve.wait_ge(t_sc, NB)
            scores = PS[:, RTB, 0:NB * NE].rearrange("p (b e) -> p b e", b=NB)
            dve.tensor_copy(SC[:, :, :], scores)
            step(dve.tensor_reduce(BEST[:, :], scores, AX.X, ALU.max))
            best = BEST[:, :].rearrange("p (b a) -> p b a", a=1).to_broadcast([128, NB, NE])
            step(dve.tensor_tensor(CAND[:, :, :], SC[:, :, :], best, ALU.is_lt))
            experts = over_tiles(IOTA[:, 0:NE])
            step(dve.tensor_scalar(CAND[:, :, :], CAND[:, :, :], float(NE), None, ALU.mult))
            step(dve.tensor_tensor(CAND[:, :, :], CAND[:, :, :], experts, ALU.add))
            step(dve.tensor_reduce(IDX[:, :], CAND[:, :, :], AX.X, ALU.min))
            idx = IDX[:, :].rearrange("p (b a) -> p b a", a=1).to_broadcast([128, NB, NE])
            step(dve.tensor_tensor(ONE[:, :, :], experts, idx, ALU.is_equal))
            dve.wait_ge(a_gate, 1)
            step(dve.tensor_scalar(GATE[:, :], GATE[:, :], 1.0, None, ALU.add))
            step(dve.reciprocal(GATE[:, :], GATE[:, :]))
            for b in range(NB):
                last = dve.tensor_scalar(C[:, b, :], C[:, b, :], GATE[:, b:b + 1], None, ALU.mult)
            last.then_inc(v_xg, 1)
            dve.wait_ge(t_rank, 1)
            dve.tensor_copy(RANK[:, :, :], PS[:, RTB, 0:NB * NE].rearrange("p (b e) -> p b e", b=NB))
            dve.memset(CNT[:, 0, :], 0.0)
            step(dve.tensor_copy(CNT[:, 1:NB + 1, :],
                                 PS[:, RTB, NB * NE:2 * NB * NE].rearrange("p (b e) -> p b e", b=NB)))
            for b in range(2, NB + 1):
                step(dve.tensor_tensor(CNT[:, b, :], CNT[:, b, :], CNT[:, b - 1, :], ALU.add))
            total = CNT[:, NB, :].rearrange("p (e a) -> p e a", a=1).to_broadcast([128, NE, NB])
            step(dve.tensor_tensor(HIT[:, :, :], IOTA[:, NE:NE + NE * NB].rearrange("p (e j) -> p e j", e=NE), total,
                                   ALU.is_lt))
            step(dve.tensor_reduce(NTE[:, :], HIT[:, :, :], AX.X, ALU.add))
            step(dve.memset(ENDT[:, 0:1], 0.0))
            for e in range(NE):
                step(dve.tensor_tensor(ENDT[:, e + 1:e + 2], ENDT[:, e:e + 1], NTE[:, e:e + 1], ALU.add))
            ends = ENDT[:, 1:NE + 1].rearrange("p (a e) -> p a e", a=1).to_broadcast([128, NT, NE])
            step(dve.tensor_tensor(OWN[:, :, :], IOTA[:, NE + NE * NB:].rearrange("p (t e) -> p t e", t=NT), ends,
                                   ALU.is_ge))
            step(dve.tensor_reduce(ETF[:, :], OWN[:, :, 0:NE - 1], AX.X, ALU.add))
            dve.tensor_copy(ETI[:, :], ETF[0:1, :]).then_inc(v_et, 1)
            step(dve.tensor_scalar(NTE[:, :], ENDT[:, 0:NE], float(P), None, ALU.mult))
            step(dve.tensor_tensor(RANK[:, :, :], RANK[:, :, :], CNT[:, 0:NB, :], ALU.add))
            step(dve.tensor_tensor(RANK[:, :, :], RANK[:, :, :], over_tiles(NTE[:, :]), ALU.add))
            step(dve.tensor_tensor(RANK[:, :, :], RANK[:, :, :], ONE[:, :, :], ALU.mult))
            step(dve.tensor_reduce(POSF[:, :], RANK[:, :, :], AX.X, ALU.add))
            dve.tensor_copy(POSI[:, :], POSF[:, :]).then_inc(v_pos, 1)

            def hidden(g, f):
                n = FT * g + f
                w = fwidth(f)
                dve.wait_ge(a_sil, n + 1)
                gate = PS[:, HB[f % 2][1], :] if w == 128 else PS[FL:2 * FL, HB[f % 2][0], :]
                dve.tensor_tensor(MIDF[f % 2][0:w, :], gate, SIL[0:w, 0:GT], ALU.mult)\
                   .then_inc(v_mid, 1)

            def add_shared(g, q):
                dve.wait_ge(t_so, 4 * g + q + 1)
                b = 4 * g + q
                row = X[:, b, :] if isinstance(b, int) else X[:, bass.ds(b, 1), :].rearrange("p a d -> p (a d)")
                dve.tensor_tensor(row, PS[:, OUTB[q % 2], 0:D], row, ALU.add).then_inc(v_so, 1)

            for f in range(FT):
                hidden(0, f)
            with dve.Fori(1, NG) as g:
                for q in range(4):
                    add_shared(g - 1, q)
                for f in range(FT):
                    hidden(g, f)
            for q in range(4):
                add_shared(NG - 1, q)

            def routed(t, par, before):
                if before:
                    dve.wait_ge(t_em, t)
                    dve.tensor_copy(MRT[:, 0:FT - 2, :], PS[:, EM, :].rearrange("p (c q) -> p c q", c=4))\
                       .then_inc(v_et1, 1)
                dve.wait_ge(a_es, t + 1)
                flat = PS[:, EH:EH + 3, :].rearrange("p b f -> p (b f)")
                dve.tensor_tensor(MR[:, :], flat[:, F:2 * F], SIL[:, :], ALU.mult).then_inc(v_em, 1)
                if before:
                    output(t - 1, 1 - par)

            def output(t, par):
                dve.wait_ge(t_ey, t + 1)
                if not (isinstance(t, int) and t < 2):
                    dve.wait_ge(d_y[par], 16 * ((t - par) // 2) if isinstance(t, int) else 16 * (t - par) // 2)
                dve.tensor_copy(YS[par][:, :], PS[:, EY, 0:D]).then_inc(v_ey, 1)

            routed(0, 0, False)
            routed(1, 1, True)
            routed(2, 0, True)
            with dve.Fori(1, (NT - 1) // 2) as i:
                for par, t in ((1, 2 * i + 1), (0, 2 * i + 2)):
                    dve.wait_ge(t_em, t)
                    dve.tensor_copy(MRT[:, 0:FT - 2, :], PS[:, EM, :].rearrange("p (c q) -> p c q", c=4))\
                       .then_inc(v_et1, 1)
                    dve.wait_ge(a_es, t + 1)
                    flat = PS[:, EH:EH + 3, :].rearrange("p b f -> p (b f)")
                    dve.tensor_tensor(MR[:, :], flat[:, F:2 * F], SIL[:, :], ALU.mult).then_inc(v_em, 1)
                    dve.wait_ge(t_ey, t)
                    dve.wait_ge(d_y[1 - par], 16 * i if par else 16 * i)
                    dve.tensor_copy(YS[1 - par][:, :], PS[:, EY, 0:D]).then_inc(v_ey, 1)
            dve.wait_ge(t_em, NT)
            dve.tensor_copy(MRT[:, 0:FT - 2, :], PS[:, EM, :].rearrange("p (c q) -> p c q", c=4)).then_inc(v_et1, 1)
            output(NT - 1, 0)

            for b in range(NB):
                dve.wait_ge(d_g[b % 2], 16 * (b // 2 + 1))
                dve.tensor_tensor(X[:, b, :], X[:, b, :], G[b % 2][:, :], ALU.add).then_inc(v_out, 1)

        @block.tensor
        def _(pe):
            def tr_x(t, par, free=True):
                if free:
                    pe.wait_ge(a_xtf, t - 1)
                for k in range(KD):
                    src = C[:, t, 128 * k:128 * (k + 1)] if isinstance(t, int) else \
                        C[:, bass.ds(t, 1), 128 * k:128 * (k + 1)].rearrange("p a d -> p (a d)")
                    last = pe.transpose(PS[:, TRB[par], P * k:P * (k + 1)], src, IDENT[:, :])
                last.then_inc(t_xt, 1)

            def score(t, par):
                pe.wait_ge(a_xtf, t + 1)
                dst = PS[:, RTB, NE * t:NE * (t + 1)]
                for k in range(KD):
                    last = pe.matmul(dst, XTF[par][:, k, :], RT[:, k, :], start=k == 0, stop=k == KD - 1)
                last.then_inc(t_sc, 1)

            for t in range(NB + 1):
                if t < NB:
                    tr_x(t, t % 2, free=t > 1)
                if t == 0:
                    pe.wait_ge(d_rt, 16)
                if t:
                    score(t - 1, (t - 1) % 2)

            def split3(dst, stat, mov, steps):
                todo = [(k, s, m) for k in range(steps) for s, m in ((0, 0), (0, 1), (1, 0))]
                for n, (k, s, m) in enumerate(todo):
                    last = pe.matmul(dst, stat(s, k), mov(m, k), start=n == 0, stop=n == len(todo) - 1)
                return last

            def shared_hidden(g, f):
                w = fwidth(f)
                n = FT * g + f
                if not (isinstance(n, int) and n < 2):
                    pe.wait_ge(v_mid, n - 1)
                for i in range(2 if w == 128 else 1):
                    lo = FM * i + 128 * f if w == 128 else 2 * FM
                    last = split3(PS[:, HB[f % 2][i], :], lambda s, k: WS13[s][:, k, lo:lo + 128],
                                  lambda m, k: XT[m][:, k, GT * g:GT * (g + 1)] if isinstance(g, int) else
                                  XT[m][:, k, bass.ds(g * GT, GT)], KD)
                last.then_inc(t_h, 1)

            def shared_out(g):
                pe.wait_ge(p_midl, FT * (g + 1))
                pe.wait_ge(v_wsl, 2)
                for q in range(4):
                    if not (isinstance(g, int) and 4 * g + q < 2):
                        pe.wait_ge(v_so, 4 * g + q - 1)
                    todo = [(f, s, m) for f in range(FT) for s, m in ((0, 0), (0, 1), (1, 0))]
                    for n, (f, s, m) in enumerate(todo):
                        w = fwidth(f)
                        last = pe.matmul(PS[:, OUTB[q % 2], 0:D], MID[s][0:w, f, P * q:P * (q + 1)],
                                         WS2[m][0:w, f, :], start=n == 0, stop=n == len(todo) - 1)
                    last.then_inc(t_so, 1)

            pe.wait_ge(v_wsl, 1)
            pe.wait_ge(p_xtl, GT // P)
            shared_hidden(0, 0)
            pe.wait_ge(v_rt, 6)
            pe.wait_ge(p_mask, 2)
            one = ONE[:, :, :].rearrange("p b e -> p (b e)")
            pe.matmul(PS[:, RTB, 0:NB * NE], UPPER[:, :], one, start=True, stop=True)
            pe.matmul(PS[:, RTB, NB * NE:2 * NB * NE], ONES[:, :], one, start=True, stop=True).then_inc(t_rank, 1)
            for f in range(1, FT):
                shared_hidden(0, f)
            pe.wait_ge(p_xtl, NB)

            def shared_group(g):
                shared_hidden(g, 0)
                shared_out(g - 1)
                for f in range(1, FT):
                    shared_hidden(g, f)

            shared_group(1)
            with pe.Fori(2, NG) as g:
                shared_group(g)
            shared_out(NG - 1)

            def ex(t, par):
                pe.wait_ge(d_xs[par], 16 * (t // 2 + 1) if isinstance(t, int) else 8 * (t - par) + 16)
                if isinstance(t, int) and t == 0:
                    pe.wait_ge(v_mid, FT * NG)
                else:
                    pe.wait_ge(a_ex, t)
                for k in range(KD):
                    last = pe.transpose(PS[:, EX, P * k:P * (k + 1)], XS[par][:, 128 * k:128 * (k + 1)], IDENT[:, :])
                last.then_inc(t_ex, 1)

            def eh(t, par):
                pe.wait_ge(a_ex, t + 1)
                pe.wait_ge(d_w13[par], 32 * (t // 2 + 1) if isinstance(t, int) else 16 * (t - par) + 32)
                if not (isinstance(t, int) and t == 0):
                    pe.wait_ge(v_em, t)
                for c in range(3):
                    hi = min(512 * (c + 1), 2 * F)
                    for k in range(KD):
                        last = pe.matmul(PS[:, EH + c, 0:hi - 512 * c], XST[par][:, k, :], W13[par][:, k, 512 * c:hi],
                                         start=k == 0, stop=k == KD - 1)
                last.then_inc(t_eh, 1)

            def em(t):
                pe.wait_ge(v_em, t + 1)
                if not (isinstance(t, int) and t == 0):
                    pe.wait_ge(v_et1, t)
                    pe.wait_ge(a_et2, t)
                for f in range(FT):
                    w = fwidth(f)
                    last = pe.transpose(PS[0:w, EM + f // 4, P * (f % 4):P * (f % 4 + 1)],
                                        MR[:, 128 * f:128 * f + w], IDENT[:, :])
                last.then_inc(t_em, 1)

            def ey(t, par):
                pe.wait_ge(v_et1, t + 1)
                pe.wait_ge(a_et2, t + 1)
                pe.wait_ge(d_w2[par], 32 * (t // 2 + 1) if isinstance(t, int) else 16 * (t - par) + 32)
                if isinstance(t, int) and t == 0:
                    pe.wait_ge(v_so, TOK // P)
                else:
                    pe.wait_ge(v_ey, t)
                for f in range(FT):
                    w = fwidth(f)
                    last = pe.matmul(PS[:, EY, 0:D], MRT[0:w, f, :], W2[par][0:w, f, :], start=f == 0,
                                     stop=f == FT - 1)
                last.then_inc(t_ey, 1)

            def routed(t, par, following=True):
                em(t - 1)
                if following:
                    ex(t + 1, 1 - par)
                eh(t, par)
                ey(t - 1, 1 - par)

            ex(0, 0)
            ex(1, 1)
            pe.wait_ge(v_so, TOK // P)
            eh(0, 0)
            with pe.Fori(0, (NT - 3) // 2) as i:
                routed(2 * i + 1, 1)
                routed(2 * i + 2, 0)
            routed(NT - 2, 1)
            routed(NT - 1, 0, following=False)
            em(NT - 1)
            ey(NT - 1, 0)


def kernel(x, ctx_1024, cond_1024, L0_xcond_ln1_w, L0_xcond_ln1_b, L0_xcond_ln2_w, L0_xcond_ln2_b, L0_xcond_Wq,
           L0_xcond_Wkv, L0_xcond_Wo, L0_ffn_router_DE, L0_ffn_w1_eDF, L0_ffn_w3_eDF, L0_ffn_w2_eFD, L0_ffn_ws1_DF,
           L0_ffn_ws3_DF, L0_ffn_ws2_FD):
    import numpy as np
    import concourse.bacc as bacc
    from concourse.bass_utils import run_bass_kernel_spmd

    def on_partitions(v):
        v = np.asarray(v)
        return np.moveaxis(v.reshape(v.shape[:-1] + (KD, 128)), -1, 0)

    norms = np.stack([np.asarray(v) for v in (L0_xcond_ln1_w, L0_xcond_ln1_b, L0_xcond_ln2_w, L0_xcond_ln2_b)])
    given = {
        "x": x, "ctx": ctx_1024, "cond": np.moveaxis(on_partitions(cond_1024), 1, 2), "ln": on_partitions(norms),
        "wq_t": np.asarray(L0_xcond_Wq).T, "wkv_t": np.asarray(L0_xcond_Wkv).T, "wo_t": np.asarray(L0_xcond_Wo).T,
        "router": L0_ffn_router_DE, "w1": L0_ffn_w1_eDF, "w3": L0_ffn_w3_eDF, "w2": L0_ffn_w2_eFD,
        "ws1": L0_ffn_ws1_DF, "ws3": L0_ffn_ws3_DF, "ws2": L0_ffn_ws2_FD,
    }
    nc = bacc.Bacc("TRN2", target_bir_lowering=False, num_devices=1)
    arrays, aps = {}, {}
    for name, value in given.items():
        value = np.ascontiguousarray(value)
        arrays[f"in_{name}"] = value
        aps[name] = nc.dram_tensor(f"in_{name}", value.shape, mybir.dt.from_np(value.dtype), kind="ExternalInput").ap()
    result = nc.dram_tensor("out_x", (NB, P, D), FP32, kind="ExternalOutput").ap()
    build(nc, aps, result)
    r = run_bass_kernel_spmd(nc, [arrays], core_ids=[0])
    return r.results[0]["out_x"]
```

```python
from contextlib import ExitStack

import concourse.bass as bass
from concourse import mybir

FP32 = mybir.dt.float32
FP32R = mybir.dt.float32r
I32 = mybir.dt.int32
ALU = mybir.AluOpType
ACT = mybir.ActivationFunctionType
AX = mybir.AxisListType

NB = 16
P = 128
D = 256
KD = D // 128
NH = 16
DH = 64
INNER = NH * DH
NP = NH // 2
KC = INNER // 128
KEYS = 2 * P
HP = NP // 2
LOOPS = (NB - 4) // 2
EPS = 1e-5
QSCALE = 1.0 / DH ** 0.5

NE = 8
F = 704
FT = (F + 127) // 128
FM = (FT - 1) * 128
FL = F - FM
TOK = NB * P
NT = TOK // P + NE - 1
DI = D + 1
NOBODY = 2.0 * TOK
GT = 512
NG = TOK // GT
UNITS = 10


def fwidth(f):
    return FL if f == FT - 1 else 128


def build(nc, a, out):
    ctx = ExitStack()
    with ctx:
        def dram(name, shape):
            return nc.dram_tensor(name, shape, FP32, kind="Internal").ap()

        def sb(name, shape):
            return ctx.enter_context(nc.sbuf_tensor(name, shape, FP32))

        mem = {
            "X": sb("X", [128, NB, D]),
            "C": sb("C", [128, NB, DI]),
            "IDENT": sb("IDENT", [128, 128]),
            "W13": [sb(f"W13_{i}", [128, KD, 2 * F]) for i in range(1)],
            "W2": [sb(f"W2_{i}", [128, FT, D]) for i in range(1)],
            "RT": sb("RT", [128, KD, NE]),
            "PS": ctx.enter_context(nc.psum_tensor("PS", [128, 8, 512], FP32)),
            "xs": dram("xs_sorted", [NT * P, DI]),
            "base": dram("base", [TOK, D]),
            "d_ws": ctx.enter_context(nc.semaphore("d_ws")),
        }
        attention_part(nc, a, mem)
        experts_part(nc, a, mem, out.rearrange("b p d -> (b p) d"))


def attention_part(nc, a, mem):
    X, C, IDENT, PS = mem["X"], mem["C"], mem["IDENT"], mem["PS"]
    ctx = ExitStack()
    with ctx:
        def sb(name, shape, dt=FP32):
            return ctx.enter_context(nc.sbuf_tensor(name, shape, dt))

        def sem(name):
            return ctx.enter_context(nc.semaphore(name))

        WQ = sb("WQ", [128, KD, INNER])
        WKVF = sb("WKVF", [128, KD, 2 * INNER])
        WKVH = sb("WKVH", [128, KD, 2 * INNER], FP32R)
        WKVL = sb("WKVL", [128, KD, 2 * INNER], FP32R)
        WOF = sb("WOF", [128, KC, D])
        WOH = sb("WOH", [128, KC, D], FP32R)
        WOL = sb("WOL", [128, KC, D], FP32R)
        LNP = sb("LNP", [128, 4, KD])
        COND = sb("COND", [128, KD, NB])
        LATA = sb("LATA", [128, KD, NB])
        LATC = sb("LATC", [128, KD, NB])
        AFF = sb("AFF", [128, 2, KD])
        CN = sb("CN", [128, D])
        XN = sb("XN", [128, D])
        ST = sb("ST", [128, 4, 6])
        MV = sb("MV", [128, 4, 2])
        VE = sb("VE", [128, 4])
        RS = sb("RS", [128, 4])
        MHALF = sb("MHALF", [128, 2])
        EPST = sb("EPST", [128, 2])
        RC = sb("RC", [128, D])
        RX = sb("RX", [128, D])
        RR = sb("RR", [128, D])
        X2 = sb("X2", [128, D])
        ZERO = sb("ZERO", [128, DI])
        KVF = sb("KVF", [128, KD, KEYS])
        KVH = sb("KVH", [128, KD, KEYS], FP32R)
        KVL = sb("KVL", [128, KD, KEYS], FP32R)
        QT = [sb(f"QT{i}", [128, NP, P]) for i in range(2)]
        KT = [sb(f"KT{i}", [128, NP, KEYS]) for i in range(2)]
        V = [sb(f"V{i}", [128, 2, INNER]) for i in range(2)]
        PR = [sb(f"PR{i}", [128, 2, KEYS]) for i in range(2)]
        PT = [sb(f"PT{i}", [128, 4, P]) for i in range(2)]
        NMX = sb("NMX", [128, 2, 2])
        SUM = sb("SUM", [128, 2, 2])
        RINV = sb("RINV", [128, 2, 2])
        OTH = sb("OTH", [128, KC, P], FP32R)
        OTL = sb("OTL", [128, KC, P], FP32R)

        PROJ = [0, 1]
        LG = 2
        PTB = [4, 5]
        OB = 6
        MISC = 7

        d_small = sem("d_small")
        d_rows = sem("d_rows")
        d_rr = sem("d_rr")
        d_wq = sem("d_wq")
        d_wk = sem("d_wk")
        d_wv = sem("d_wv")
        d_wo = sem("d_wo")
        d_zero = sem("d_zero")
        p_const = sem("p_const")
        p_ident = sem("p_ident")
        p_wo = sem("p_wo")
        p_woh = sem("p_woh")
        a_kv_hi = sem("a_kv_hi")
        v_kv_lo = sem("v_kv_lo")
        v_cond = sem("v_cond")
        v_aff = sem("v_aff")
        v_st = sem("v_st")
        v_mv = sem("v_mv")
        p_ve = sem("p_ve")
        p_rs = sem("p_rs")
        v_xn1 = sem("v_xn1")
        v_xn = sem("v_xn")
        v_st2 = sem("v_st2")
        v_mv2 = sem("v_mv2")
        p_ve2 = sem("p_ve2")
        p_rs2 = sem("p_rs2")
        t_in = sem("t_in")
        v_kvf = sem("v_kvf")
        a_kvh = sem("a_kvh")
        p_kvl = sem("p_kvl")
        t_unit = sem("t_unit")
        a_unit = sem("a_unit")
        t_lg = sem("t_lg")
        v_mx = sem("v_mx")
        a_exp = sem("a_exp")
        v_rinv = sem("v_rinv")
        v_pr = sem("v_pr")
        t_pt = sem("t_pt")
        v_pt = sem("v_pt")
        a_pt = sem("a_pt")
        t_pv = sem("t_pv")
        a_oh = sem("a_oh")
        v_ol = sem("v_ol")
        t_wo = sem("t_wo")
        v_res = sem("v_res")
        v_st3 = sem("v_st3")
        v_mv3 = sem("v_mv3")
        p_ve3 = sem("p_ve3")
        p_rs3 = sem("p_rs3")
        v_x2 = sem("v_x2")

        block = ctx.enter_context(nc.Block())

        @block.sync
        def _(sp):
            def one(t, n):
                return t[n] if isinstance(n, int) else t[bass.ds(n, 1), :, :].rearrange("a p d -> (a p) d")

            def load_rows(n):
                if not isinstance(n, int) or n:
                    sp.wait_ge(v_xn1, n)
                sp.dma_start(RC[:, :], one(a["ctx"], n)).then_inc(d_rows, 16)
                sp.dma_start(RX[:, :], one(a["x"], n)).then_inc(d_rows, 16)

            def load_residual(n):
                if not isinstance(n, int) or n:
                    sp.wait_ge(v_res, n)
                sp.dma_start(RR[:, :], one(a["x"], n)).then_inc(d_rr, 16)

            load_rows(0)
            sp.dma_start(LNP[:, :, :], a["ln"]).then_inc(d_small, 16)
            sp.dma_start(COND[:, :, :], a["cond"]).then_inc(d_small, 16)
            sp.dma_start(WQ[:, :, :], a["wq_t"].rearrange("(k p) e -> p k e", p=128)).then_inc(d_wq, 16)
            wkv = a["wkv_t"].rearrange("(k p) e -> p k e", p=128)
            sp.dma_start(WKVF[:, :, 0:INNER], wkv[:, :, 0:INNER]).then_inc(d_wk, 16)
            sp.dma_start(WKVF[:, :, INNER:], wkv[:, :, INNER:]).then_inc(d_wv, 16)
            load_rows(1)
            load_residual(0)
            sp.dma_start(WOF[:, :, :], a["wo_t"].rearrange("(k p) d -> p k d", p=128)).then_inc(d_wo, 16)
            load_rows(2)
            d_ws = mem["d_ws"]
            W13, W2 = mem["W13"][0], mem["W2"][0]
            for i, n in enumerate(("ws1", "ws3")):
                src = a[n].rearrange("(k p) f -> p k f", p=128)
                sp.dma_start(W13[:, :, FM * i:FM * (i + 1)], src[:, :, 0:FM]).then_inc(d_ws, 16)
                sp.dma_start(W13[:, :, 2 * FM + FL * i:2 * FM + FL * (i + 1)], src[:, :, FM:F]).then_inc(d_ws, 16)
            load_w2(sp, W2, a["ws2"], d_ws)
            sp.dma_start(mem["RT"][:, :, :], a["router"].rearrange("(k p) e -> p k e", p=128)).then_inc(d_ws, 16)
            sp.wait_ge(p_const, 4)
            for t in range(NT):
                sp.dma_start(mem["xs"][t * P:(t + 1) * P, :], ZERO[:, :]).then_inc(d_zero, 16)
            with sp.Fori(1, NB - 2) as n:
                load_rows(n + 2)
                load_residual(n)
            load_residual(NB - 2)
            load_residual(NB - 1)
            sp.wait_ge(d_zero, 16 * NT)
            sp.wait_ge(d_ws, 16 * 7)

        @block.gpsimd
        def _(pool):
            pool.memset(MHALF[:, :], -0.5).then_inc(p_const, 1)
            pool.memset(ZERO[:, 0:D], 0.0).then_inc(p_const, 1)
            pool.memset(ZERO[:, D:DI], NOBODY).then_inc(p_const, 1)
            pool.memset(EPST[:, :], EPS).then_inc(p_const, 1)
            pool.memset(IDENT[:, :], 0.0).then_inc(p_ident, 1)
            pool.wait_ge(p_ident, 1)
            pool.affine_select(out=IDENT[:, :], in_=IDENT[:, :], compare_op=ALU.not_equal, fill=1.0,
                               base=0, pattern=[[-1, 128]], channel_multiplier=1).then_inc(p_ident, 1)
            pool.wait_ge(p_const, 4)

            def rstd(lo, n, var_ready, ve_sem, done, count):
                pool.wait_ge(var_ready, count)
                pool.tensor_tensor(VE[:, lo:lo + n], MV[:, lo:lo + n, 1], EPST[:, 0:n], ALU.add).then_inc(ve_sem, 1)
                pool.wait_ge(ve_sem, count)
                pool.tensor_tensor(RS[:, lo:lo + n], VE[:, lo:lo + n], MHALF[:, 0:n], ALU.pow).then_inc(done, 1)

            def kv_lo(n):
                pool.wait_ge(a_kvh, n + 1)
                pool.tensor_tensor(KVL[:, :, :], KVF[:, :, :], KVH[:, :, :].bitcast(FP32),
                                   ALU.subtract).then_inc(p_kvl, 1)

            def norms(n):
                rstd(0, 2, v_mv, p_ve, p_rs, n + 1)
                rstd(2, 1, v_mv2, p_ve2, p_rs2, n + 1)

            def batch(b, first=False, following=True, norm=True):
                if following:
                    kv_lo(b + 1)
                if not first:
                    rstd(3, 1, v_mv3, p_ve3, p_rs3, b)
                if norm:
                    norms(b + 2)

            norms(0)
            kv_lo(0)
            norms(1)
            batch(0, first=True)
            pool.wait_ge(d_wo, 16)
            pool.tensor_copy(WOH[:, :, :], WOF[:, :, :]).then_inc(p_woh, 1)
            pool.wait_ge(p_woh, 1)
            pool.tensor_tensor(WOL[:, :, :], WOF[:, :, :], WOH[:, :, :].bitcast(FP32), ALU.subtract).then_inc(p_wo, 1)
            with pool.Fori(0, LOOPS) as i:
                batch(2 * i + 1)
                batch(2 * i + 2)
            batch(NB - 3)
            batch(NB - 2, norm=False)
            batch(NB - 1, following=False, norm=False)
            rstd(3, 1, v_mv3, p_ve3, p_rs3, NB)

        def row(t, b):
            return t[:, b, 0:D] if isinstance(b, int) else t[:, bass.ds(b, 1), 0:D].rearrange("p a d -> p (a d)")

        def col(t, b):
            return t[:, :, b] if isinstance(b, int) else t[:, :, bass.ds(b, 1)].rearrange("p k a -> p (k a)")

        @block.scalar
        def _(act):
            def kv_hi(n):
                act.wait_ge(v_kvf, n + 1)
                act.activation(KVH[:, :, :], KVF[:, :, :], ACT.Copy).then_inc(a_kvh, 1)

            def unit(n, k, par, waits=True):
                act.wait_ge(t_unit, UNITS * n + k + 1)
                src = PS[:, PROJ[k % 2], :]
                if k < 2:
                    if k == 0 and waits:
                        act.wait_ge(t_pv, NP * (n - 1))
                    act.activation(QT[par][:, 4 * k:4 * k + 4, :], src.rearrange("p (j q) -> p j q", j=4),
                                   ACT.Copy, scale=QSCALE).then_inc(a_unit, 1)
                elif k < 6:
                    j = 2 * (k - 2)
                    act.activation(KT[par][:, j:j + 2, :], src.rearrange("p (j q) -> p j q", j=2),
                                   ACT.Copy).then_inc(a_unit, 1)
                else:
                    half, tile = (k - 6) // 2, (k - 6) % 2
                    act.activation(V[par][:, tile, 512 * half:512 * half + 512], src, ACT.Copy).then_inc(a_unit, 1)

            def exps(b, j):
                for h in range(2):
                    if h == 0:
                        act.wait_ge(v_mx, NP * b + j + 1)
                        if not (isinstance(b, int) and NP * b + j < 2):
                            act.wait_ge(t_pt, NP * b + j - 1)
                    act.activation(PR[j % 2][:, h, :], PS[:, LG + h, 0:KEYS], ACT.Exp, bias=NMX[:, j % 2, h:h + 1],
                                   accum_out=SUM[:, j % 2, h:h + 1]).then_inc(a_exp, 1)

            def copy_pt(b, j):
                act.wait_ge(t_pt, NP * b + j + 1)
                if not (isinstance(b, int) and NP * b + j < 2):
                    act.wait_ge(t_pv, NP * b + j - 1)
                act.activation(PT[j % 2][:, :, :], PS[:, PTB[j % 2], :].rearrange("p (c q) -> p c q", c=4),
                               ACT.Copy).then_inc(a_pt, 1)

            def o_hi(b, half):
                act.wait_ge(t_pv, NP * b + HP * (half + 1))
                if half == 0 and not (isinstance(b, int) and b == 0):
                    act.wait_ge(t_wo, b)
                act.activation(OTH[:, HP * half:HP * half + HP, :], PS[:, OB, :].rearrange("p (j q) -> p j q", j=HP),
                               ACT.Copy).then_inc(a_oh, 1)

            def batch(b, par, first=False, last=False):
                for j in range(NP):
                    if j > 0 and j % 2 == 0:
                        copy_pt(b, j - 1)
                    if j == 0 and not first:
                        copy_pt(b - 1, NP - 1)
                    if j == 1 and not first:
                        o_hi(b - 1, 1)
                    exps(b, j)
                    if j == HP + 1:
                        o_hi(b, 0)
                    for n, k in filler(b, j, last):
                        unit(n, k, par if k >= 8 else 1 - par)
                    if j == 1 and not last:
                        kv_hi(b + 1)

            for half, ready in ((0, d_wk), (1, d_wv)):
                act.wait_ge(ready, 16)
                act.activation(WKVH[:, :, INNER * half:INNER * (half + 1)],
                               WKVF[:, :, INNER * half:INNER * (half + 1)], ACT.Copy).then_inc(a_kv_hi, 1)
                if half == 0:
                    kv_hi(0)
                    for k in range(2):
                        unit(0, k, 0, waits=False)
            for k in range(2, 8):
                unit(0, k, 0, waits=False)
            batch(0, 0, first=True)
            with act.Fori(0, LOOPS) as i:
                batch(2 * i + 1, 1)
                batch(2 * i + 2, 0)
            batch(NB - 3, 1)
            batch(NB - 2, 0)
            batch(NB - 1, 1, last=True)
            copy_pt(NB - 1, NP - 1)
            o_hi(NB - 1, 1)

        @block.vector
        def _(dve):
            def norm_stats(n):
                dve.wait_ge(d_rows, 32 * (n + 1))
                dve.bn_stats(ST[:, 0, :], RC[:, :])
                dve.bn_stats(ST[:, 1, :], RX[:, :]).then_inc(v_st, 1)
                dve.wait_ge(v_st, n + 1)
                dve.nop(nofuse=True)
                dve.bn_aggr(MV[:, 0, :], ST[:, 0, :])
                dve.bn_aggr(MV[:, 1, :], ST[:, 1, :]).then_inc(v_mv, 1)

            def norm_rows(n, guard=True):
                dve.wait_ge(p_rs, n + 1)
                if guard:
                    dve.wait_ge(t_in, n)
                dve.tensor_scalar(CN[:, :], RC[:, :], MV[:, 0, 0:1], RS[:, 0:1], ALU.subtract, ALU.mult)
                dve.tensor_scalar(XN[:, :], RX[:, :], MV[:, 1, 0:1], RS[:, 1:2], ALU.subtract, ALU.mult)\
                   .then_inc(v_xn1, 1)
                dve.wait_ge(v_xn1, n + 1)
                dve.bn_stats(ST[:, 2, :], XN[:, :]).then_inc(v_st2, 1)
                dve.wait_ge(v_st2, n + 1)
                dve.nop(nofuse=True)
                dve.bn_aggr(MV[:, 2, :], ST[:, 2, :]).then_inc(v_mv2, 1)

            def norm_again(n):
                dve.tensor_copy(AFF[:, 0, :], col(LATA, n))
                dve.tensor_copy(AFF[:, 1, :], col(LATC, n)).then_inc(v_aff, 1)
                dve.wait_ge(p_rs2, n + 1)
                dve.tensor_scalar(XN[:, :], XN[:, :], MV[:, 2, 0:1], RS[:, 2:3], ALU.subtract, ALU.mult)\
                   .then_inc(v_xn, 1)

            def modulate(n, guard=True):
                dve.wait_ge(t_in, n + 1)
                dve.wait_ge(v_aff, n + 1)
                if guard:
                    dve.wait_ge(p_kvl, n)
                for k in range(KD):
                    src = PS[:, MISC, KEYS * k:KEYS * (k + 1)]
                    dve.tensor_scalar(KVF[:, k, 0:P], src[:, 0:P], LNP[:, 0, k:k + 1], LNP[:, 1, k:k + 1],
                                      ALU.mult, ALU.add)
                    last = dve.tensor_scalar(KVF[:, k, P:KEYS], src[:, P:KEYS], AFF[:, 0, k:k + 1],
                                             AFF[:, 1, k:k + 1], ALU.mult, ALU.add)
                last.then_inc(v_kvf, 1)

            def row_max(b, j):
                dve.wait_ge(t_lg, NP * b + j + 1)
                if not (isinstance(b, int) and NP * b + j < 2):
                    dve.wait_ge(a_exp, 2 * (NP * b + j - 1))
                dve.tensor_reduce(NMX[:, j % 2, :], PS[:, LG:LG + 2, 0:KEYS], AX.X, ALU.max, negate=True)\
                   .then_inc(v_mx, 1)

            def normalise(b, j):
                dve.wait_ge(a_exp, 2 * (NP * b + j + 1))
                dve.reciprocal(RINV[:, j % 2, :], SUM[:, j % 2, :]).then_inc(v_rinv, 1)
                dve.wait_ge(v_rinv, NP * b + j + 1)
                for h in range(2):
                    last = dve.tensor_scalar(PR[j % 2][:, h, :], PR[j % 2][:, h, :], RINV[:, j % 2, h:h + 1], None,
                                             ALU.mult)
                last.then_inc(v_pr, 1)

            def copy_pt(b, j):
                dve.wait_ge(t_pt, NP * b + j + 1)
                if not (isinstance(b, int) and NP * b + j < 2):
                    dve.wait_ge(t_pv, NP * b + j - 1)
                dve.tensor_copy(PT[j % 2][:, :, :], PS[:, PTB[j % 2], :].rearrange("p (c q) -> p c q", c=4))\
                   .then_inc(v_pt, 1)

            def o_lo(b, half):
                dve.wait_ge(a_oh, 2 * b + half + 1)
                lo, hi = HP * half, HP * half + HP
                dve.tensor_tensor(OTL[:, lo:hi, :], PS[:, OB, :].rearrange("p (j q) -> p j q", j=HP),
                                  OTH[:, lo:hi, :].bitcast(FP32), ALU.subtract).then_inc(v_ol, 1)

            def residual(b):
                dve.wait_ge(t_wo, b + 1)
                dve.wait_ge(d_rr, 16 * (b + 1))
                dve.tensor_tensor(X2[:, :], PS[:, MISC, 0:D], RR[:, :], ALU.add).then_inc(v_res, 1)
                dve.wait_ge(v_res, b + 1)
                dve.bn_stats(ST[:, 3, :], X2[:, :]).then_inc(v_st3, 1)
                dve.tensor_copy(row(X, b), X2[:, :])
                dve.wait_ge(v_st3, b + 1)
                dve.nop(nofuse=True)
                dve.bn_aggr(MV[:, 3, :], ST[:, 3, :]).then_inc(v_mv3, 1)

            def expert_input(b):
                dve.wait_ge(p_rs3, b + 1)
                dve.tensor_scalar(row(C, b), X2[:, :], MV[:, 3, 0:1], RS[:, 3:4], ALU.subtract, ALU.mult)\
                   .then_inc(v_x2, 1)

            def batch(b, first=False, following=True, norm=True):
                for j in range(NP):
                    row_max(b, j)
                    if j % 2:
                        copy_pt(b, j - 1)
                    if j == 1 and not first:
                        o_lo(b - 1, 1)
                    normalise(b, j)
                    if j == HP + 1:
                        o_lo(b, 0)
                    if j == 1 and following:
                        modulate(b + 1)
                    if j == 4 and not first:
                        residual(b - 1)
                    if j == 5 and not first:
                        expert_input(b - 1)
                    if norm and j >= 5:
                        (norm_stats, norm_rows, norm_again)[j - 5](b + 2)

            norm_stats(0)
            dve.wait_ge(d_small, 16 * 2)
            dve.tensor_scalar(LATA[:, :, :], COND[:, :, :], 1.0, None, ALU.add).then_inc(v_cond, 1)
            dve.wait_ge(v_cond, 1)
            for k in range(KD):
                dve.tensor_scalar(LATC[:, k, :], LATA[:, k, :], LNP[:, 3, k:k + 1], None, ALU.mult).then_inc(v_cond, 1)
            dve.wait_ge(v_cond, 3)
            for k in range(KD):
                dve.tensor_scalar(LATA[:, k, :], LATA[:, k, :], LNP[:, 2, k:k + 1], None, ALU.mult)
            dve.tensor_tensor(LATC[:, :, :], LATC[:, :, :], COND[:, :, :], ALU.add).then_inc(v_cond, 1)
            dve.wait_ge(v_cond, 4)
            norm_rows(0, guard=False)
            norm_again(0)
            modulate(0, guard=False)
            for half in range(2):
                dve.wait_ge(a_kv_hi, half + 1)
                part = slice(INNER * half, INNER * (half + 1))
                dve.tensor_tensor(WKVL[:, :, part], WKVF[:, :, part], WKVH[:, :, part].bitcast(FP32),
                                  ALU.subtract).then_inc(v_kv_lo, 1)
            norm_stats(1)
            norm_rows(1)
            norm_again(1)
            batch(0, first=True)
            with dve.Fori(0, LOOPS) as i:
                batch(2 * i + 1)
                batch(2 * i + 2)
            batch(NB - 3)
            batch(NB - 2, norm=False)
            batch(NB - 1, following=False, norm=False)
            o_lo(NB - 1, 1)
            residual(NB - 1)
            expert_input(NB - 1)

        @block.tensor
        def _(pe):
            def transpose_inputs(n):
                pe.wait_ge(v_xn, n + 1)
                for k in range(KD):
                    for i, src in enumerate((CN, XN)):
                        last = pe.transpose(PS[:, MISC, KEYS * k + P * i:KEYS * k + P * (i + 1)],
                                            src[:, 128 * k:128 * (k + 1)], IDENT[:, :])
                last.then_inc(t_in, 1)

            def split3(dst, stat, mov, steps):
                todo = [(k, s, m) for k in range(steps) for s, m in ((0, 0), (0, 1), (1, 0))]
                for n, (k, s, m) in enumerate(todo):
                    last = pe.matmul(dst, stat(s, k), mov(m, k), start=n == 0, stop=n == len(todo) - 1)
                return last

            kv = (KVH, KVL)
            wkv = (WKVH, WKVL)
            oT = (OTH, OTL)
            wo = (WOH, WOL)

            def unit(n, k, free=True):
                if free:
                    pe.wait_ge(a_unit, UNITS * n + k - 1)
                dst = PS[:, PROJ[k % 2], :]
                if k < 2:
                    if k == 0:
                        pe.wait_ge(v_kvf, n + 1)
                    for j in range(4):
                        e = 128 * (4 * k + j)
                        for c in range(KD):
                            last = pe.matmul(dst[:, P * j:P * (j + 1)], WQ[:, c, e:e + 128], KVF[:, c, P:KEYS],
                                             start=c == 0, stop=c == KD - 1)
                elif k < 6:
                    if k == 2:
                        pe.wait_ge(a_kvh, n + 1)
                        pe.wait_ge(p_kvl, n + 1)
                    for j in range(2):
                        e = 128 * (2 * (k - 2) + j)
                        last = split3(dst[:, KEYS * j:KEYS * (j + 1)], lambda s, c: wkv[s][:, c, e:e + 128],
                                      lambda m, c: kv[m][:, c, :], KD)
                else:
                    half, tile = (k - 6) // 2, (k - 6) % 2
                    e = INNER + 512 * half
                    last = split3(dst, lambda s, c: kv[s][:, c, P * tile:P * (tile + 1)],
                                  lambda m, c: wkv[m][:, c, e:e + 512], KD)
                last.then_inc(t_unit, 1)

            def logits(b, j, par):
                pe.wait_ge(a_unit, UNITS * b + 3 + j // 2)
                if not (isinstance(b, int) and NP * b + j < 1):
                    pe.wait_ge(a_exp, 2 * (NP * b + j))
                for h in range(2):
                    part = slice(DH * h, DH * (h + 1))
                    last = pe.matmul(PS[:, LG + h, 0:KEYS], QT[par][part, j, :], KT[par][part, j, :],
                                     start=True, stop=True)
                last.then_inc(t_lg, 1)

            def transpose_probs(b, j):
                pe.wait_ge(v_pr, NP * b + j + 1)
                if not (isinstance(b, int) and NP * b + j < 2):
                    pe.wait_ge(a_pt if j % 2 else v_pt, HP * b + j // 2)
                for h in range(2):
                    for t in range(2):
                        c = 2 * h + t
                        last = pe.transpose(PS[:, PTB[j % 2], P * c:P * (c + 1)], PR[j % 2][:, h, P * t:P * (t + 1)],
                                            IDENT[:, :])
                last.then_inc(t_pt, 1)

            def times_v(b, j, par):
                pe.wait_ge(a_unit, UNITS * b + (8 if j < HP else 10))
                pe.wait_ge(a_pt if j % 2 else v_pt, HP * b + j // 2 + 1)
                if j % HP == 0 and not (isinstance(b, int) and b == 0 and j == 0):
                    pe.wait_ge(v_ol, 2 * b + j // HP)
                for t in range(2):
                    for h in range(2):
                        e = 128 * j + DH * h
                        last = pe.matmul(PS[DH * h:DH * (h + 1), OB, P * (j % HP):P * (j % HP + 1)],
                                         V[par][:, t, e:e + DH], PT[j % 2][:, 2 * h + t, :],
                                         start=t == 0, stop=t == 1)
                last.then_inc(t_pv, 1)

            def output_projection(b):
                pe.wait_ge(v_ol, 2 * b + 2)
                pe.wait_ge(v_kvf, min(b + 3, NB) if isinstance(b, int) else b + 3)
                split3(PS[:, MISC, 0:D], lambda s, c: oT[s][:, c, :], lambda m, c: wo[m][:, c, :], KC)\
                    .then_inc(t_wo, 1)

            def batch(b, par, first=False, last=False):
                for j in range(NP):
                    logits(b, j, par)
                    if j:
                        transpose_probs(b, j - 1)
                    elif not first:
                        transpose_probs(b - 1, NP - 1)
                    if j == 3 and not first:
                        output_projection(b - 1)
                    if j == 1 and not last:
                        transpose_inputs(b + 1)
                    for n, k in filler(b, j, last):
                        unit(n, k)
                    if j:
                        times_v(b, j - 1, par)
                    elif not first:
                        times_v(b - 1, NP - 1, 1 - par)

            pe.wait_ge(p_ident, 2)
            transpose_inputs(0)
            pe.wait_ge(d_wq, 16)
            for k in range(8):
                if k == 2:
                    pe.wait_ge(v_kv_lo, 1)
                if k == 6:
                    pe.wait_ge(v_kv_lo, 2)
                unit(0, k, free=k > 1)
            batch(0, 0, first=True)
            pe.wait_ge(p_wo, 1)
            with pe.Fori(0, LOOPS) as i:
                batch(2 * i + 1, 1)
                batch(2 * i + 2, 0)
            batch(NB - 3, 1)
            batch(NB - 2, 0)
            batch(NB - 1, 1, last=True)
            transpose_probs(NB - 1, NP - 1)
            times_v(NB - 1, NP - 1, 1)
            output_projection(NB - 1)


def filler(b, j, last):
    own = {0: [8], 1: [9]}
    following = {2: [0, 1], 4: [2, 3], 5: [4], 6: [5, 6], 7: [7]}
    return [(b, k) for k in own.get(j, [])] + ([] if last else [(b + 1, k) for k in following.get(j, [])])


def load_w2(sp, dst, src, done):
    sp.dma_start(dst[:, 0:FT - 1, :], src[0:FM, :].rearrange("(k p) d -> p k d", p=128)).then_inc(done, 16)
    sp.dma_start(dst[0:FL, FT - 1, :], src[FM:F, :]).then_inc(done, 16)


def experts_part(nc, a, mem, out):
    X, C, IDENT, PS, RT = mem["X"], mem["C"], mem["IDENT"], mem["PS"], mem["RT"]
    xs, base, d_ws = mem["xs"], mem["base"], mem["d_ws"]
    ctx = ExitStack()
    with ctx:
        def sb(name, shape, dt=FP32):
            return ctx.enter_context(nc.sbuf_tensor(name, shape, dt))

        def sem(name):
            return ctx.enter_context(nc.semaphore(name))

        W13 = mem["W13"] + [sb("W13_1", [128, KD, 2 * F])]
        W2 = mem["W2"] + [sb("W2_1", [128, FT, D])]
        WS13 = [sb(f"WS13{p}", [128, KD, 2 * F], FP32R) for p in "HL"]
        WS2 = [sb(f"WS2{p}", [128, FT, D], FP32R) for p in "HL"]
        XTF = [sb(f"XTF{i}", [128, KD, P]) for i in range(2)]
        XT = [sb(f"XT{p}", [128, KD, TOK], FP32R) for p in "HL"]
        MIDF = [sb(f"MIDF{i}", [128, GT]) for i in range(2)]
        MID = [sb(f"MID{p}", [128, FT, GT], FP32R) for p in "HL"]
        SC = sb("SC", [128, NB, NE])
        BEST = sb("BEST", [128, NB])
        ONE = sb("ONE", [128, NB, NE])
        CAND = sb("CAND", [128, NB, NE])
        IDX = sb("IDX", [128, NB])
        IOTA_I = sb("IOTA_I", [128, NE + NE * NB + NT * NE + NB], I32)
        IOTA = sb("IOTA", [128, NE + NE * NB + NT * NE + NB])
        UPPER = sb("UPPER", [128, 128])
        ONES = sb("ONES", [128, 128])
        GATE = sb("GATE", [128, NB])
        RANK = sb("RANK", [128, NB, NE])
        CNT = [sb(f"CNT{i}", [128, NB + 1, NE]) for i in range(2)]
        NTE = sb("NTE", [128, NE])
        HIT = sb("HIT", [128, NE, NB])
        ENDT = sb("ENDT", [128, NE + 1])
        OWN = sb("OWN", [128, NT, NE])
        ETF = sb("ETF", [128, NT])
        ETI = sb("ETI", [1, NT], I32)
        POSF = sb("POSF", [128, NB])
        POSI = sb("POSI", [128, NB], I32)
        XS = [sb(f"XS{i}", [128, DI]) for i in range(2)]
        WHO = sb("WHO", [128, NT], I32)
        XST = [sb(f"XST{i}", [128, KD, P]) for i in range(2)]
        SIL = sb("SIL", [128, F])
        MR = sb("MR", [128, F])
        MRT = sb("MRT", [128, FT, P])
        YS = [sb(f"YS{i}", [128, D]) for i in range(2)]
        BASE = [sb(f"BASE{i}", [128, D]) for i in range(2)]

        TRB = [0, 1]
        RTB = 2
        HB = [(3, 4), (5, 6)]
        OUTB = [7, 0]
        EH = 1
        EM = 4
        EX = 6
        EY = 7

        v_wsh = sem("v_wsh")
        v_wsl = sem("v_wsl")
        p_iota = sem("p_iota")
        p_mask = sem("p_mask")
        t_xt = sem("t_xt")
        a_xtf = sem("a_xtf")
        a_xth = sem("a_xth")
        p_xtl = sem("p_xtl")
        t_sc = sem("t_sc")
        v_rt = sem("v_rt")
        a_gate = sem("a_gate")
        t_rank = sem("t_rank")
        v_gate = sem("v_gate")
        p_xg = sem("p_xg")
        v_pos = sem("v_pos")
        v_et = sem("v_et")
        d_sc = sem("d_sc")
        t_h = sem("t_h")
        a_sil = sem("a_sil")
        v_mid = sem("v_mid")
        a_midh = sem("a_midh")
        v_midl = sem("v_midl")
        t_so = sem("t_so")
        v_so = sem("v_so")
        d_xs = [sem(f"d_xs{i}") for i in range(2)]
        d_w13 = [sem(f"d_w13{i}") for i in range(2)]
        d_w2 = [sem(f"d_w2{i}") for i in range(2)]
        d_bs = sem("d_bs")
        a_who = sem("a_who")
        v_zero = sem("v_zero")
        d_base = [sem(f"d_base{i}") for i in range(2)]
        d_y = [sem(f"d_y{i}") for i in range(2)]
        t_ex = sem("t_ex")
        a_ex = sem("a_ex")
        t_eh = sem("t_eh")
        a_es = sem("a_es")
        v_em = sem("v_em")
        t_em = sem("t_em")
        v_et1 = sem("v_et1")
        a_et2 = sem("a_et2")
        t_ey = sem("t_ey")
        v_ey = sem("v_ey")

        block = ctx.enter_context(nc.Block())

        def tile_rows(t, n):
            return t[n * P:(n + 1) * P, :] if isinstance(n, int) else t[bass.ds(n * P, P), :]

        @block.sync
        def _(sp):
            def load_expert(t, par, first=False):
                e = sp.value_load(ETI[0:1, t:t + 1] if isinstance(t, int) else ETI[0:1, bass.ds(t, 1)],
                                  min_val=0, max_val=NE - 1)
                if not first:
                    sp.wait_ge(t_eh, t - 1)
                for i, n in enumerate(("w1", "w3")):
                    sp.dma_start(W13[par][:, :, F * i:F * (i + 1)],
                                 a[n][bass.ds(e, 1), :, :].rearrange("a (k p) f -> p (a k) f", p=128))\
                      .then_inc(d_w13[par], 16)
                if not first:
                    sp.wait_ge(t_ey, t - 1)
                load_w2(sp, W2[par], a["w2"][bass.ds(e, 1), :, :].rearrange("a f d -> (a f) d"), d_w2[par])

            sp.wait_ge(v_et, 1)
            sp.wait_ge(v_wsl, 2)
            load_expert(0, 0, first=True)
            load_expert(1, 1, first=True)
            for g in range(NG):
                sp.wait_ge(v_so, 4 * (g + 1))
                sp.dma_start(base[GT * g:GT * (g + 1), :].rearrange("(b p) d -> p b d", p=P),
                             X[:, 4 * g:4 * (g + 1), :]).then_inc(d_bs, 16)
            with sp.Fori(1, (NT - 1) // 2) as i:
                load_expert(2 * i, 0)
                load_expert(2 * i + 1, 1)
            load_expert(NT - 1, 0)
            sp.wait_ge(d_bs, 16 * NG)

        @block.gpsimd
        def _(pool):
            pool.iota(IOTA_I[:, 0:NE], pattern=[[1, NE]], base=0, channel_multiplier=0).then_inc(p_iota, 1)
            pool.iota(IOTA_I[:, NE:NE + NE * NB], pattern=[[0, NE], [P, NB]], base=0, channel_multiplier=0)\
                .then_inc(p_iota, 1)
            pool.iota(IOTA_I[:, NE + NE * NB:NE + NE * NB + NT * NE], pattern=[[1, NT], [0, NE]], base=0,
                      channel_multiplier=0).then_inc(p_iota, 1)
            pool.iota(IOTA_I[:, NE + NE * NB + NT * NE:], pattern=[[P, NB]], base=0, channel_multiplier=1)\
                .then_inc(p_iota, 1)
            pool.memset(ONES[:, :], 1.0).then_inc(p_mask, 1)
            pool.wait_ge(p_mask, 1)
            pool.affine_select(out=UPPER[:, :], in_=ONES[:, :], compare_op=ALU.is_gt, fill=0.0,
                               base=0, pattern=[[1, 128]], channel_multiplier=-1).then_inc(p_mask, 1)

            def x_lo(t, par):
                pool.wait_ge(a_xth, t + 1)
                dst = XT[1][:, :, t * P:(t + 1) * P] if isinstance(t, int) else XT[1][:, :, bass.ds(t * P, P)]
                hi = XT[0][:, :, t * P:(t + 1) * P] if isinstance(t, int) else XT[0][:, :, bass.ds(t * P, P)]
                pool.tensor_tensor(dst, XTF[par][:, :, :], hi.bitcast(FP32), ALU.subtract).then_inc(p_xtl, 1)

            with pool.Fori(0, NB // 2) as i:
                x_lo(2 * i, 0)
                x_lo(2 * i + 1, 1)

            pool.wait_ge(v_gate, 1)
            for b in range(NB):
                pool.tensor_scalar(C[:, b, 0:D], C[:, b, 0:D], GATE[:, b:b + 1], None, ALU.mult).then_inc(p_xg, 1)
            pool.wait_ge(v_pos, 1)
            for b in range(NB):
                pool.wait_ge(p_xg, b + 1)
                pool.indirect_dma_start(out=xs, out_offset=bass.IndirectOffsetOnAxis(ap=POSI[:, b:b + 1], axis=0),
                                        in_=C[:, b, :], in_offset=None).then_inc(d_sc, 16)

            for par in range(2):
                pool.memset(BASE[par][:, :], 0.0).then_inc(v_zero, 1)
            pool.wait_ge(v_zero, 2)
            pool.wait_ge(d_bs, 16 * NG)

            def gather_base(t):
                pool.wait_ge(a_who, t + 1)
                if t >= 2:
                    pool.wait_ge(v_ey, t - 1)
                pool.indirect_dma_start(out=BASE[t % 2][:, :], out_offset=None, in_=base,
                                        in_offset=bass.IndirectOffsetOnAxis(ap=WHO[:, t:t + 1], axis=0),
                                        bounds_check=TOK - 1, oob_is_err=False).then_inc(d_base[t % 2], 16)

            gather_base(0)
            for t in range(NT):
                if t + 1 < NT:
                    gather_base(t + 1)
                pool.wait_ge(v_ey, t + 1)
                pool.indirect_dma_start(out=out, out_offset=bass.IndirectOffsetOnAxis(ap=WHO[:, t:t + 1], axis=0),
                                        in_=YS[t % 2][:, :], in_offset=None,
                                        bounds_check=TOK - 1, oob_is_err=False).then_inc(d_y[t % 2], 16)
            for par in range(2):
                pool.wait_ge(d_y[par], 16 * ((NT + 1 - par) // 2))

        @block.scalar
        def _(act):
            def x_hi(t, par, free=True):
                act.wait_ge(t_xt, t + 1)
                if free:
                    act.wait_ge(p_xtl, t - 1)
                    act.wait_ge(t_sc, t - 1)
                act.activation(XTF[par][:, :, :], PS[:, TRB[par], 0:KD * P].rearrange("p (k q) -> p k q", k=KD),
                               ACT.Copy).then_inc(a_xtf, 1)
                act.wait_ge(a_xtf, t + 1)
                dst = XT[0][:, :, t * P:(t + 1) * P] if isinstance(t, int) else XT[0][:, :, bass.ds(t * P, P)]
                act.activation(dst, XTF[par][:, :, :], ACT.Copy).then_inc(a_xth, 1)

            x_hi(0, 0, free=False)
            x_hi(1, 1, free=False)
            with act.Fori(1, NB // 2) as i:
                x_hi(2 * i, 0)
                x_hi(2 * i + 1, 1)

            act.wait_ge(v_rt, 2)
            act.activation(GATE[:, :], BEST[:, :], ACT.Exp, scale=-1.0).then_inc(a_gate, 1)

            def shared_act(g, f):
                w = fwidth(f)
                n = FT * g + f
                act.wait_ge(t_h, n + 1)
                act.activation(SIL[0:w, 0:GT], PS[0:w, HB[f % 2][0], :], ACT.Silu).then_inc(a_sil, 1)
                act.wait_ge(v_mid, n + 1)
                if f == 0 and not (isinstance(g, int) and g == 0):
                    act.wait_ge(t_so, 4 * g)
                act.activation(MID[0][0:w, f, :], MIDF[f % 2][0:w, :], ACT.Copy).then_inc(a_midh, 1)

            for f in range(FT):
                shared_act(0, f)
            with act.Fori(1, NG) as g:
                for f in range(FT):
                    shared_act(g, f)

            def copy_x(t, par, free=True, load=True):
                act.wait_ge(t_ex, t + 1)
                if free:
                    act.wait_ge(t_eh, t - 1)
                act.activation(XST[par][:, :, :], PS[:, EX, 0:KD * P].rearrange("p (k q) -> p k q", k=KD),
                               ACT.Copy).then_inc(a_ex, 1)
                act.activation(WHO[:, t:t + 1] if isinstance(t, int) else WHO[:, bass.ds(t, 1)],
                               XS[par][:, D:DI], ACT.Copy).then_inc(a_who, 1)
                if load:
                    act.wait_ge(a_who, t + 1)
                    act.dma_start(XS[par][:, :], tile_rows(xs, t + 2)).then_inc(d_xs[par], 16)

            def routed_act(t, par, copy_next):
                if not (isinstance(t, int) and t == 0):
                    act.wait_ge(t_em, t)
                    act.activation(MRT[:, FT - 2, :], PS[:, EM + 1, 0:P], ACT.Copy)
                    act.activation(MRT[0:FL, FT - 1, :], PS[0:FL, EM + 1, P:2 * P], ACT.Copy).then_inc(a_et2, 1)
                if copy_next:
                    copy_x(t + 1, 1 - par, free=not (isinstance(t, int) and t == 0),
                           load=not (isinstance(t, int) and t + 3 >= NT))
                act.wait_ge(t_eh, t + 1)
                if not (isinstance(t, int) and t == 0):
                    act.wait_ge(v_em, t)
                act.activation(SIL[:, :], PS[:, EH:EH + 3, :].rearrange("p b f -> p (b f)")[:, 0:F], ACT.Silu)\
                   .then_inc(a_es, 1)

            act.wait_ge(d_sc, 16 * NB)
            for t in range(2):
                act.dma_start(XS[t][:, :], tile_rows(xs, t)).then_inc(d_xs[t], 16)
            copy_x(0, 0, free=False)
            routed_act(0, 0, True)
            with act.Fori(0, (NT - 5) // 2) as i:
                routed_act(2 * i + 1, 1, True)
                routed_act(2 * i + 2, 0, True)
            routed_act(NT - 4, 1, True)
            routed_act(NT - 3, 0, True)
            routed_act(NT - 2, 1, True)
            routed_act(NT - 1, 0, False)
            act.wait_ge(t_em, NT)
            act.activation(MRT[:, FT - 2, :], PS[:, EM + 1, 0:P], ACT.Copy)
            act.activation(MRT[0:FL, FT - 1, :], PS[0:FL, EM + 1, P:2 * P], ACT.Copy).then_inc(a_et2, 1)

        @block.vector
        def _(dve):
            done = [0]

            def step(ins):
                done[0] += 1
                ins.then_inc(v_rt, 1)
                dve.wait_ge(v_rt, done[0])

            def over_tiles(t):
                return t.rearrange("p (a e) -> p a e", a=1).to_broadcast([128, NB, NE])

            dve.wait_ge(d_ws, 16 * 7)
            dve.tensor_copy(WS13[0][:, :, :], W13[0][:, :, :]).then_inc(v_wsh, 1)
            dve.wait_ge(v_wsh, 1)
            dve.tensor_tensor(WS13[1][:, :, :], W13[0][:, :, :], WS13[0][:, :, :].bitcast(FP32), ALU.subtract)\
               .then_inc(v_wsl, 1)
            dve.tensor_copy(WS2[0][:, 0:FT - 1, :], W2[0][:, 0:FT - 1, :])
            dve.tensor_copy(WS2[0][0:FL, FT - 1, :], W2[0][0:FL, FT - 1, :]).then_inc(v_wsh, 1)
            dve.wait_ge(v_wsh, 2)
            dve.tensor_tensor(WS2[1][:, 0:FT - 1, :], W2[0][:, 0:FT - 1, :], WS2[0][:, 0:FT - 1, :].bitcast(FP32),
                              ALU.subtract)
            dve.tensor_tensor(WS2[1][0:FL, FT - 1, :], W2[0][0:FL, FT - 1, :],
                              WS2[0][0:FL, FT - 1, :].bitcast(FP32), ALU.subtract).then_inc(v_wsl, 1)
            dve.wait_ge(p_iota, 4)
            step(dve.tensor_copy(IOTA[:, :], IOTA_I[:, :]))
            dve.tensor_copy(C[:, :, D:DI].rearrange("p b a -> p (b a)"), IOTA[:, NE + NE * NB + NT * NE:])

            dve.wait_ge(t_sc, NB)
            scores = PS[:, RTB, 0:NB * NE].rearrange("p (b e) -> p b e", b=NB)
            dve.tensor_copy(SC[:, :, :], scores)
            step(dve.tensor_reduce(BEST[:, :], scores, AX.X, ALU.max))
            best = BEST[:, :].rearrange("p (b a) -> p b a", a=1).to_broadcast([128, NB, NE])
            step(dve.tensor_tensor(CAND[:, :, :], SC[:, :, :], best, ALU.is_lt))
            experts = over_tiles(IOTA[:, 0:NE])
            step(dve.tensor_scalar(CAND[:, :, :], CAND[:, :, :], float(NE), None, ALU.mult))
            step(dve.tensor_tensor(CAND[:, :, :], CAND[:, :, :], experts, ALU.add))
            step(dve.tensor_reduce(IDX[:, :], CAND[:, :, :], AX.X, ALU.min))
            idx = IDX[:, :].rearrange("p (b a) -> p b a", a=1).to_broadcast([128, NB, NE])
            step(dve.tensor_tensor(ONE[:, :, :], experts, idx, ALU.is_equal))
            def place_tokens():
                dve.wait_ge(a_gate, 1)
                step(dve.tensor_scalar(GATE[:, :], GATE[:, :], 1.0, None, ALU.add))
                dve.reciprocal(GATE[:, :], GATE[:, :]).then_inc(v_gate, 1)
                dve.wait_ge(t_rank, 1)
                dve.tensor_copy(RANK[:, :, :], PS[:, RTB, 0:NB * NE].rearrange("p (b e) -> p b e", b=NB))
                for half in range(2):
                    dve.memset(CNT[half][:, 0, :], 0.0)
                step(dve.tensor_copy(CNT[0][:, 1:NB + 1, :],
                                     PS[:, RTB, NB * NE:2 * NB * NE].rearrange("p (b e) -> p b e", b=NB)))
                now, ahead = 0, 1
                while ahead < NB:
                    src, dst = CNT[now], CNT[1 - now]
                    dve.tensor_copy(dst[:, 1:ahead + 1, :], src[:, 1:ahead + 1, :])
                    step(dve.tensor_tensor(dst[:, ahead + 1:, :], src[:, ahead + 1:, :], src[:, 1:NB + 1 - ahead, :],
                                           ALU.add))
                    now, ahead = 1 - now, 2 * ahead
                cnt = CNT[now]
                total = cnt[:, NB, :].rearrange("p (e a) -> p e a", a=1).to_broadcast([128, NE, NB])
                step(dve.tensor_tensor(HIT[:, :, :], IOTA[:, NE:NE + NE * NB].rearrange("p (e j) -> p e j", e=NE),
                                       total, ALU.is_lt))
                step(dve.tensor_reduce(NTE[:, :], HIT[:, :, :], AX.X, ALU.add))
                step(dve.memset(ENDT[:, 0:1], 0.0))
                for e in range(NE):
                    step(dve.tensor_tensor(ENDT[:, e + 1:e + 2], ENDT[:, e:e + 1], NTE[:, e:e + 1], ALU.add))
                step(dve.tensor_scalar(NTE[:, :], ENDT[:, 0:NE], float(P), None, ALU.mult))
                step(dve.tensor_tensor(RANK[:, :, :], RANK[:, :, :], cnt[:, 0:NB, :], ALU.add))
                step(dve.tensor_tensor(RANK[:, :, :], RANK[:, :, :], over_tiles(NTE[:, :]), ALU.add))
                step(dve.tensor_tensor(RANK[:, :, :], RANK[:, :, :], ONE[:, :, :], ALU.mult))
                step(dve.tensor_reduce(POSF[:, :], RANK[:, :, :], AX.X, ALU.add))
                dve.tensor_copy(POSI[:, :], POSF[:, :]).then_inc(v_pos, 1)
                ends = ENDT[:, 1:NE + 1].rearrange("p (a e) -> p a e", a=1).to_broadcast([128, NT, NE])
                tiles = IOTA[:, NE + NE * NB:NE + NE * NB + NT * NE].rearrange("p (t e) -> p t e", t=NT)
                step(dve.tensor_tensor(OWN[:, :, :], tiles, ends, ALU.is_ge))
                step(dve.tensor_reduce(ETF[:, :], OWN[:, :, 0:NE - 1], AX.X, ALU.add))
                dve.tensor_copy(ETI[:, :], ETF[0:1, :]).then_inc(v_et, 1)

            def hidden(g, f):
                n = FT * g + f
                w = fwidth(f)
                dve.wait_ge(a_sil, n + 1)
                gate = PS[:, HB[f % 2][1], :] if w == 128 else PS[FL:2 * FL, HB[f % 2][0], :]
                dve.tensor_tensor(MIDF[f % 2][0:w, :], gate, SIL[0:w, 0:GT], ALU.mult)\
                   .then_inc(v_mid, 1)

            def add_shared(g, q):
                dve.wait_ge(t_so, 4 * g + q + 1)
                b = 4 * g + q
                row = X[:, b, :] if isinstance(b, int) else X[:, bass.ds(b, 1), :].rearrange("p a d -> p (a d)")
                dve.tensor_tensor(row, PS[:, OUTB[q % 2], 0:D], row, ALU.add).then_inc(v_so, 1)

            def mid_lo(g, f):
                dve.wait_ge(a_midh, FT * g + f + 1)
                w = fwidth(f)
                dve.tensor_tensor(MID[1][0:w, f, :], MIDF[f % 2][0:w, :], MID[0][0:w, f, :].bitcast(FP32),
                                  ALU.subtract).then_inc(v_midl, 1)

            for f in range(FT):
                hidden(0, f)
                mid_lo(0, f)
                if f == 0:
                    place_tokens()
            with dve.Fori(1, NG) as g:
                for f in range(FT):
                    hidden(g, f)
                    if f == 0:
                        for q in range(4):
                            add_shared(g - 1, q)
                    mid_lo(g, f)
            for q in range(4):
                add_shared(NG - 1, q)

            def copy_hidden(t):
                dve.wait_ge(t_em, t)
                dve.tensor_copy(MRT[:, 0:FT - 2, :], PS[:, EM, :].rearrange("p (c q) -> p c q", c=4))\
                   .then_inc(v_et1, 1)

            def gate_hidden(t):
                dve.wait_ge(a_es, t + 1)
                flat = PS[:, EH:EH + 3, :].rearrange("p b f -> p (b f)")
                dve.tensor_tensor(MR[:, :], flat[:, F:2 * F], SIL[:, :], ALU.mult).then_inc(v_em, 1)

            def output(t, par, n):
                dve.wait_ge(t_ey, t + 1)
                dve.wait_ge(d_base[par], 16 * (n + 1))
                if not (isinstance(t, int) and t < 2):
                    dve.wait_ge(d_y[par], 16 * n)
                dve.tensor_tensor(YS[par][:, :], PS[:, EY, 0:D], BASE[par][:, :], ALU.add).then_inc(v_ey, 1)

            gate_hidden(0)
            for t in (1, 2):
                copy_hidden(t)
                gate_hidden(t)
                output(t - 1, (t - 1) % 2, 0)
            with dve.Fori(1, (NT - 1) // 2) as i:
                copy_hidden(2 * i + 1)
                gate_hidden(2 * i + 1)
                output(2 * i, 0, i)
                copy_hidden(2 * i + 2)
                gate_hidden(2 * i + 2)
                output(2 * i + 1, 1, i)
            copy_hidden(NT)
            output(NT - 1, 0, NT // 2)

        @block.tensor
        def _(pe):
            def tr_x(t, par, free=True):
                if free:
                    pe.wait_ge(a_xtf, t - 1)
                for k in range(KD):
                    src = C[:, t, 128 * k:128 * (k + 1)] if isinstance(t, int) else \
                        C[:, bass.ds(t, 1), 128 * k:128 * (k + 1)].rearrange("p a d -> p (a d)")
                    last = pe.transpose(PS[:, TRB[par], P * k:P * (k + 1)], src, IDENT[:, :])
                last.then_inc(t_xt, 1)

            def score(t, par):
                pe.wait_ge(a_xtf, t + 1)
                dst = PS[:, RTB, NE * t:NE * (t + 1)]
                for k in range(KD):
                    last = pe.matmul(dst, XTF[par][:, k, :], RT[:, k, :], start=k == 0, stop=k == KD - 1)
                last.then_inc(t_sc, 1)

            for t in range(NB + 1):
                if t < NB:
                    tr_x(t, t % 2, free=t > 1)
                if t == 0:
                    pe.wait_ge(d_ws, 16 * 7)
                if t:
                    score(t - 1, (t - 1) % 2)

            def split3(dst, stat, mov, steps):
                todo = [(k, s, m) for k in range(steps) for s, m in ((0, 0), (0, 1), (1, 0))]
                for n, (k, s, m) in enumerate(todo):
                    last = pe.matmul(dst, stat(s, k), mov(m, k), start=n == 0, stop=n == len(todo) - 1)
                return last

            def shared_hidden(g, f):
                w = fwidth(f)
                n = FT * g + f
                if not (isinstance(n, int) and n < 2):
                    pe.wait_ge(v_mid, n - 1)
                for i in range(2 if w == 128 else 1):
                    lo = FM * i + 128 * f if w == 128 else 2 * FM
                    last = split3(PS[:, HB[f % 2][i], :], lambda s, k: WS13[s][:, k, lo:lo + 128],
                                  lambda m, k: XT[m][:, k, GT * g:GT * (g + 1)] if isinstance(g, int) else
                                  XT[m][:, k, bass.ds(g * GT, GT)], KD)
                last.then_inc(t_h, 1)

            def shared_out(g):
                pe.wait_ge(v_midl, FT * (g + 1))
                pe.wait_ge(v_wsl, 2)
                for q in range(4):
                    if not (isinstance(g, int) and 4 * g + q < 2):
                        pe.wait_ge(v_so, 4 * g + q - 1)
                    todo = [(f, s, m) for f in range(FT) for s, m in ((0, 0), (0, 1), (1, 0))]
                    for n, (f, s, m) in enumerate(todo):
                        w = fwidth(f)
                        last = pe.matmul(PS[:, OUTB[q % 2], 0:D], MID[s][0:w, f, P * q:P * (q + 1)],
                                         WS2[m][0:w, f, :], start=n == 0, stop=n == len(todo) - 1)
                    last.then_inc(t_so, 1)

            pe.wait_ge(v_wsl, 1)
            pe.wait_ge(p_xtl, GT // P)
            shared_hidden(0, 0)
            pe.wait_ge(v_rt, 7)
            pe.wait_ge(p_mask, 2)
            one = ONE[:, :, :].rearrange("p b e -> p (b e)")
            pe.matmul(PS[:, RTB, 0:NB * NE], UPPER[:, :], one, start=True, stop=True)
            pe.matmul(PS[:, RTB, NB * NE:2 * NB * NE], ONES[:, :], one, start=True, stop=True).then_inc(t_rank, 1)
            for f in range(1, FT):
                shared_hidden(0, f)
            pe.wait_ge(p_xtl, NB)

            def shared_group(g):
                shared_hidden(g, 0)
                shared_out(g - 1)
                for f in range(1, FT):
                    shared_hidden(g, f)

            shared_group(1)
            with pe.Fori(2, NG) as g:
                shared_group(g)
            shared_out(NG - 1)

            def ex(t, par):
                pe.wait_ge(d_xs[par], 16 * (t // 2 + 1) if isinstance(t, int) else 8 * (t - par) + 16)
                if isinstance(t, int) and t == 0:
                    pe.wait_ge(v_mid, FT * NG)
                else:
                    pe.wait_ge(a_ex, t)
                for k in range(KD):
                    last = pe.transpose(PS[:, EX, P * k:P * (k + 1)], XS[par][:, 128 * k:128 * (k + 1)], IDENT[:, :])
                last.then_inc(t_ex, 1)

            def eh(t, par):
                pe.wait_ge(a_ex, t + 1)
                pe.wait_ge(d_w13[par], 32 * (t // 2 + 1) if isinstance(t, int) else 16 * (t - par) + 32)
                if not (isinstance(t, int) and t == 0):
                    pe.wait_ge(v_em, t)
                for c in range(3):
                    hi = min(512 * (c + 1), 2 * F)
                    for k in range(KD):
                        last = pe.matmul(PS[:, EH + c, 0:hi - 512 * c], XST[par][:, k, :], W13[par][:, k, 512 * c:hi],
                                         start=k == 0, stop=k == KD - 1)
                last.then_inc(t_eh, 1)

            def em(t):
                pe.wait_ge(v_em, t + 1)
                if not (isinstance(t, int) and t == 0):
                    pe.wait_ge(v_et1, t)
                    pe.wait_ge(a_et2, t)
                for f in range(FT):
                    w = fwidth(f)
                    last = pe.transpose(PS[0:w, EM + f // 4, P * (f % 4):P * (f % 4 + 1)],
                                        MR[:, 128 * f:128 * f + w], IDENT[:, :])
                last.then_inc(t_em, 1)

            def ey(t, par):
                pe.wait_ge(v_et1, t + 1)
                pe.wait_ge(a_et2, t + 1)
                pe.wait_ge(d_w2[par], 32 * (t // 2 + 1) if isinstance(t, int) else 16 * (t - par) + 32)
                if isinstance(t, int) and t == 0:
                    pe.wait_ge(v_so, TOK // P)
                else:
                    pe.wait_ge(v_ey, t)
                for f in range(FT):
                    w = fwidth(f)
                    last = pe.matmul(PS[:, EY, 0:D], MRT[0:w, f, :], W2[par][0:w, f, :], start=f == 0,
                                     stop=f == FT - 1)
                last.then_inc(t_ey, 1)

            def routed(t, par, following=True):
                em(t - 1)
                if following:
                    ex(t + 1, 1 - par)
                eh(t, par)
                ey(t - 1, 1 - par)

            ex(0, 0)
            ex(1, 1)
            pe.wait_ge(v_so, TOK // P)
            eh(0, 0)
            with pe.Fori(0, (NT - 3) // 2) as i:
                routed(2 * i + 1, 1)
                routed(2 * i + 2, 0)
            routed(NT - 2, 1)
            routed(NT - 1, 0, following=False)
            em(NT - 1)
            ey(NT - 1, 0)


def kernel(x, ctx_1024, cond_1024, L0_xcond_ln1_w, L0_xcond_ln1_b, L0_xcond_ln2_w, L0_xcond_ln2_b, L0_xcond_Wq,
           L0_xcond_Wkv, L0_xcond_Wo, L0_ffn_router_DE, L0_ffn_w1_eDF, L0_ffn_w3_eDF, L0_ffn_w2_eFD, L0_ffn_ws1_DF,
           L0_ffn_ws3_DF, L0_ffn_ws2_FD):
    import numpy as np
    import concourse.bacc as bacc
    from concourse.bass_utils import run_bass_kernel_spmd

    def on_partitions(v):
        v = np.asarray(v)
        return np.moveaxis(v.reshape(v.shape[:-1] + (KD, 128)), -1, 0)

    norms = np.stack([np.asarray(v) for v in (L0_xcond_ln1_w, L0_xcond_ln1_b, L0_xcond_ln2_w, L0_xcond_ln2_b)])
    given = {
        "x": x, "ctx": ctx_1024, "cond": np.moveaxis(on_partitions(cond_1024), 1, 2), "ln": on_partitions(norms),
        "wq_t": np.asarray(L0_xcond_Wq).T, "wkv_t": np.asarray(L0_xcond_Wkv).T, "wo_t": np.asarray(L0_xcond_Wo).T,
        "router": L0_ffn_router_DE, "w1": L0_ffn_w1_eDF, "w3": L0_ffn_w3_eDF, "w2": L0_ffn_w2_eFD,
        "ws1": L0_ffn_ws1_DF, "ws3": L0_ffn_ws3_DF, "ws2": L0_ffn_ws2_FD,
    }
    nc = bacc.Bacc("TRN2", target_bir_lowering=False, num_devices=1)
    arrays, aps = {}, {}
    for name, value in given.items():
        value = np.ascontiguousarray(value)
        arrays[f"in_{name}"] = value
        aps[name] = nc.dram_tensor(f"in_{name}", value.shape, mybir.dt.from_np(value.dtype), kind="ExternalInput").ap()
    result = nc.dram_tensor("out_x", (NB, P, D), FP32, kind="ExternalOutput").ap()
    build(nc, aps, result)
    r = run_bass_kernel_spmd(nc, [arrays], core_ids=[0])
    return r.results[0]["out_x"]
```

```python
from contextlib import ExitStack

import concourse.bass as bass
from concourse import mybir

FP32 = mybir.dt.float32
FP32R = mybir.dt.float32r
I32 = mybir.dt.int32
ALU = mybir.AluOpType
ACT = mybir.ActivationFunctionType
AX = mybir.AxisListType

NB = 16
P = 128
D = 256
KD = D // 128
NH = 16
DH = 64
INNER = NH * DH
NP = NH // 2
KC = INNER // 128
KEYS = 2 * P
HP = NP // 2
LOOPS = (NB - 4) // 2
EPS = 1e-5
QSCALE = 1.0 / DH ** 0.5

NE = 8
F = 704
FT = (F + 127) // 128
FM = (FT - 1) * 128
FL = F - FM
TOK = NB * P
NT = TOK // P + NE - 1
DI = D + 1
NOBODY = 2.0 * TOK
GT = 512
NG = TOK // GT
TAIL = [0, 2, 4, 6, 9, 12]
AHEAD = TAIL[-1]
assert GT // P <= AHEAD < NB
UNIT = [("q", 0, 0), ("k", 0, 0), ("k", 1, 0), ("v", 0, 0), ("v", 0, 1),
        ("q", 1, 0), ("k", 2, 0), ("k", 3, 0), ("v", 1, 0), ("v", 1, 1)]
NU = len(UNIT)
BANK = [0, 1, 2, 0, 1, 2, 0, 1, 2, 1]
OWN = [slice(0, DH), slice(DH, 2 * DH)]
LOS = sum(u[0] != "v" for u in UNIT)
KUNIT, QUNIT = ([k for k, u in enumerate(UNIT) if u[0] == kind] for kind in "kq")


def eighth(j):
    return slice(2 * F // 8 * j, 2 * F // 8 * (j + 1))


def fwidth(f):
    return FL if f == FT - 1 else 128


def build(nc, a, out):
    ctx = ExitStack()
    with ctx:
        def dram(name, shape):
            return nc.dram_tensor(name, shape, FP32, kind="Internal").ap()

        def sb(name, shape, dt=FP32):
            return ctx.enter_context(nc.sbuf_tensor(name, shape, dt))

        mem = {
            "C": sb("C", [128, NB, DI]),
            "IDENT": sb("IDENT", [128, 128]),
            "WS13": [sb(f"WS13{p}", [128, KD, 2 * F], FP32R) for p in "HL"],
            "WS2": [sb(f"WS2{p}", [128, FT, D], FP32R) for p in "HL"],
            "WKV_XT": [sb(f"WKV_XT{p}", [128, KD, max(2 * INNER, TOK)], FP32R) for p in "HL"],
            "RT": sb("RT", [128, KD, NE]),
            "RTS": sb("RTS", [128, KD, 2, NE], FP32R),
            "PS": ctx.enter_context(nc.psum_tensor("PS", [128, 8, 512], FP32)),
            "xs": dram("xs_sorted", [NT * P, DI]),
            "base": dram("base", [TOK, D]),
        }
        attention_part(nc, a, mem)
        experts_part(nc, a, mem, out.rearrange("b p d -> (b p) d"))


def attention_part(nc, a, mem):
    C, IDENT, PS, base = mem["C"], mem["IDENT"], mem["PS"], mem["base"]
    WS13, WS2 = mem["WS13"], mem["WS2"]
    WKVH, WKVL = XT = mem["WKV_XT"]
    ctx = ExitStack()
    with ctx:
        def sb(name, shape, dt=FP32):
            return ctx.enter_context(nc.sbuf_tensor(name, shape, dt))

        def sem(name):
            return ctx.enter_context(nc.semaphore(name))

        WQ = sb("WQ", [128, KD, INNER])
        STAGE = sb("STAGE", [128, 2, KD * INNER])
        WOH = sb("WOH", [128, KC, D], FP32R)
        WOL = sb("WOL", [128, KC, D], FP32R)
        LNP = sb("LNP", [128, 4, KD])
        COND = sb("COND", [128, KD, NB])
        LATA = sb("LATA", [128, KD, NB])
        LATC = sb("LATC", [128, KD, NB])
        AFF = sb("AFF", [128, 2, KD])
        CN = sb("CN", [128, D])
        XN = sb("XN", [128, D])
        ST = sb("ST", [128, 4, 6])
        MV = sb("MV", [128, 4, 2])
        VE = sb("VE", [128, 4])
        RS = sb("RS", [128, 4])
        MHALF = sb("MHALF", [128, 2])
        EPST = sb("EPST", [128, 2])
        RC = sb("RC", [128, D])
        RX = sb("RX", [128, D])
        RR = sb("RR", [128, D])
        X2 = sb("X2", [128, D])
        ZERO = sb("ZERO", [128, DI])
        KVF = [sb(f"KVF{i}", [128, KD, KEYS]) for i in range(2)]
        KVH = [sb(f"KVH{i}", [128, KD, KEYS], FP32R) for i in range(2)]
        KVL = [sb(f"KVL{i}", [128, KD, KEYS], FP32R) for i in range(2)]
        KT = sb("KT", [128, 2, NP, KEYS], FP32R)
        QT = sb("QT", [128, 2, NP, P], FP32R)
        QTL = sb("QTL", [128, 2, NP, P], FP32R)
        V = sb("V", [128, 2, INNER])
        PR = [sb(f"PR{i}", [128, 2, KEYS]) for i in range(2)]
        PT = [sb(f"PT{i}", [128, 4, P]) for i in range(2)]
        NMX = sb("NMX", [128, 2, 2])
        SUM = sb("SUM", [128, 2, 2])
        RINV = sb("RINV", [128, 2, 2])
        OTH = sb("OTH", [128, KC, P], FP32R)
        OTL = sb("OTL", [128, KC, P], FP32R)

        PROJ = [0, 1, 4]
        LG = [2, 3]
        PTB = 5
        OB = 6
        MISC = 7

        d_small = sem("d_small")
        d_rows = sem("d_rows")
        d_rr = sem("d_rr")
        d_wq = sem("d_wq")
        d_wk = sem("d_wk")
        d_wv = sem("d_wv")
        d_wo = sem("d_wo")
        d_w2 = sem("d_w2")
        d_w13 = [sem(f"d_w13_{k}") for k in range(KD)]
        d_rt = sem("d_rt")
        p_rt = sem("p_rt")
        d_x1 = sem("d_x1")
        d_zero = sem("d_zero")
        p_const = sem("p_const")
        p_ident = sem("p_ident")
        v_zeros = sem("v_zeros")
        p_wo = sem("p_wo")
        a_woh = sem("a_woh")
        a_wsh = sem("a_wsh")
        p_wsl = sem("p_wsl")
        a_kv_hi = sem("a_kv_hi")
        v_kv_lo = sem("v_kv_lo")
        p_kv_lo = sem("p_kv_lo")
        v_cond = sem("v_cond")
        v_aff = sem("v_aff")
        v_st = sem("v_st")
        v_mv = sem("v_mv")
        p_ve = sem("p_ve")
        p_rs = sem("p_rs")
        v_xn1 = sem("v_xn1")
        v_xn = sem("v_xn")
        v_st2 = sem("v_st2")
        v_mv2 = sem("v_mv2")
        p_ve2 = sem("p_ve2")
        p_rs2 = sem("p_rs2")
        t_in = sem("t_in")
        v_kvf = sem("v_kvf")
        a_kvh = sem("a_kvh")
        p_kvl = sem("p_kvl")
        t_unit = sem("t_unit")
        a_unit = sem("a_unit")
        d_twice = sem("d_twice")
        v_unit = sem("v_unit")
        t_lg = sem("t_lg")
        v_mx = sem("v_mx")
        a_exp = sem("a_exp")
        v_rinv = sem("v_rinv")
        v_pr = sem("v_pr")
        p_pr = sem("p_pr")
        t_pt = sem("t_pt")
        a_pt = sem("a_pt")
        t_pv = sem("t_pv")
        a_oh = sem("a_oh")
        v_ol = sem("v_ol")
        t_wo = sem("t_wo")
        v_res = sem("v_res")
        v_st3 = sem("v_st3")
        v_mv3 = sem("v_mv3")
        p_ve3 = sem("p_ve3")
        p_rs3 = sem("p_rs3")
        v_x2 = sem("v_x2")
        t_xt = sem("t_xt")
        a_xth = sem("a_xth")
        v_xtl = sem("v_xtl")

        block = ctx.enter_context(nc.Block())

        @block.sync
        def _(sp):
            def one(t, n):
                return t[n] if isinstance(n, int) else t[bass.ds(n, 1), :, :].rearrange("a p d -> (a p) d")

            def load_rows(n):
                if not isinstance(n, int) or n:
                    sp.wait_ge(v_xn1, n)
                sp.dma_start(RC[:, :], one(a["ctx"], n)).then_inc(d_rows, 16)
                sp.dma_start(RX[:, :], one(a["x"], n)).then_inc(d_rows, 16)

            def load_residual(n):
                if not isinstance(n, int) or n:
                    sp.wait_ge(d_x1, 16 * n)
                sp.dma_start(RR[:, :], one(a["x"], n)).then_inc(d_rr, 16)

            load_rows(0)
            sp.dma_start(LNP[:, :, :], a["ln"]).then_inc(d_small, 16)
            sp.dma_start(COND[:, :, :], a["cond"]).then_inc(d_small, 16)
            wkv = a["wkv_t"].rearrange("(k p) e -> p k e", p=128)

            def load_kv(half, done):
                sp.dma_start(STAGE[:, half, :].rearrange("p (k e) -> p k e", k=KD),
                             wkv[:, :, INNER * half:INNER * (half + 1)]).then_inc(done, 16)

            load_kv(0, d_wk)
            sp.dma_start(WQ[:, :, :], a["wq_t"].rearrange("(k p) e -> p k e", p=128)).then_inc(d_wq, 16)
            load_kv(1, d_wv)
            load_rows(1)
            load_residual(0)
            sp.wait_ge(v_kv_lo, 1)
            sp.wait_ge(p_kv_lo, 1)
            sp.dma_start(STAGE[:, 0, :].rearrange("p (k d) -> p k d", k=KC),
                         a["wo_t"].rearrange("(k p) d -> p k d", p=128)).then_inc(d_wo, 16)
            load_rows(2)
            sp.wait_ge(v_kv_lo, 2)
            sp.wait_ge(p_kv_lo, 2)
            load_w2(sp, STAGE[:, 1, 0:FT * D].rearrange("p (k d) -> p k d", k=FT), a["ws2"], a["ws2_last"], d_w2)
            sp.dma_start(mem["RT"][:, :, :], a["router"].rearrange("(k p) e -> p k e", p=128)).then_inc(d_rt, 16)
            sp.wait_ge(p_const, 4)
            for t in range(NT):
                sp.dma_start(mem["xs"][t * P:(t + 1) * P, :], ZERO[:, :]).then_inc(d_zero, 16)

            def load_w13(k):
                sp.dma_start(STAGE[:, k, 0:2 * F], a["ws13"][:, k, :]).then_inc(d_w13[k], 16)

            def store_sum(n):
                sp.wait_ge(v_res, n + 1)
                dst = base[P * n:P * (n + 1), :] if isinstance(n, int) else base[bass.ds(n * P, P), :]
                sp.dma_start(dst, X2[:, :]).then_inc(d_x1, 16)

            sp.wait_ge(p_wo, KC)
            load_w13(0)
            with sp.Fori(1, NB - 2) as n:
                load_rows(n + 2)
                store_sum(n - 1)
                load_residual(n)
            sp.wait_ge(p_wsl, FT)
            load_w13(1)
            for n in (NB - 2, NB - 1):
                store_sum(n - 1)
                load_residual(n)
            store_sum(NB - 1)
            sp.wait_ge(d_zero, 16 * NT)
            sp.wait_ge(d_rt, 16)
            sp.wait_ge(d_x1, 16 * NB)

        def weights_lo(engine, half, k, done):
            engine.wait_ge(a_kv_hi, KD * half + KD - k)
            part = slice(INNER * half, INNER * (half + 1))
            engine.tensor_tensor(WKVL[:, k, part], STAGE[:, half, INNER * k:INNER * (k + 1)],
                                 WKVH[:, k, part].bitcast(FP32), ALU.subtract).then_inc(done, 1)

        @block.gpsimd
        def _(pool):
            pool.memset(MHALF[:, :], -0.5).then_inc(p_const, 1)
            pool.memset(ZERO[:, 0:D], 0.0).then_inc(p_const, 1)
            pool.memset(ZERO[:, D:DI], NOBODY).then_inc(p_const, 1)
            pool.memset(EPST[:, :], EPS).then_inc(p_const, 1)
            pool.memset(IDENT[:, :], 0.0).then_inc(p_ident, 1)
            pool.wait_ge(p_ident, 1)
            pool.affine_select(out=IDENT[:, :], in_=IDENT[:, :], compare_op=ALU.not_equal, fill=1.0,
                               base=0, pattern=[[-1, 128]], channel_multiplier=1).then_inc(p_ident, 1)
            pool.wait_ge(p_const, 4)

            def rstd(lo, n, var_ready, ve_sem, done, count):
                pool.wait_ge(var_ready, count)
                pool.tensor_tensor(VE[:, lo:lo + n], MV[:, lo:lo + n, 1], EPST[:, 0:n], ALU.add).then_inc(ve_sem, 1)
                pool.wait_ge(ve_sem, count)
                pool.tensor_tensor(RS[:, lo:lo + n], VE[:, lo:lo + n], MHALF[:, 0:n], ALU.pow).then_inc(done, 1)

            def kv_lo(n, par):
                pool.wait_ge(a_kvh, n + 1)
                pool.tensor_tensor(KVL[par][:, :, :], KVF[par][:, :, :], KVH[par][:, :, :].bitcast(FP32),
                                   ALU.subtract).then_inc(p_kvl, 1)

            def norms(n):
                rstd(0, 2, v_mv, p_ve, p_rs, n + 1)
                rstd(2, 1, v_mv2, p_ve2, p_rs2, n + 1)

            def normalise(b, j):
                pool.wait_ge(v_rinv, NP * b + j + 1)
                pr = PR[j % 2][:, 1, :]
                pool.tensor_tensor(pr, pr, RINV[:, j % 2, 1:2].to_broadcast([128, KEYS]), ALU.mult).then_inc(p_pr, 1)

            def batch(b, par, first=False, following=True, norm=True, between=None):
                for j in range(NP):
                    if j == 4 and following:
                        kv_lo(b + 1, 1 - par)
                    if j == 4 and norm:
                        rstd(0, 2, v_mv, p_ve, p_rs, b + 3)
                    if j == 5 and norm:
                        rstd(2, 1, v_mv2, p_ve2, p_rs2, b + 3)
                    if j == NP - 1 and not first:
                        rstd(3, 1, v_mv3, p_ve3, p_rs3, b)
                    normalise(b, j)
                    if between:
                        between(j)

            def wo_lo(j):
                for k in ([0], [1], [2], [], [], [3], [4, 5], [6, 7])[j]:
                    pool.wait_ge(a_woh, k + 1)
                    pool.tensor_tensor(WOL[:, k, :], STAGE[:, 0, D * k:D * (k + 1)], WOH[:, k, :].bitcast(FP32),
                                       ALU.subtract).then_inc(p_wo, 1)

            def w2_lo(j):
                if j < FT:
                    w = fwidth(j)
                    pool.wait_ge(a_wsh, j + 1)
                    pool.tensor_tensor(WS2[1][0:w, j, :], STAGE[0:w, 1, D * j:D * (j + 1)],
                                       WS2[0][0:w, j, :].bitcast(FP32), ALU.subtract).then_inc(p_wsl, 1)

            def w13_lo(k):
                def part(j):
                    pool.wait_ge(a_wsh, FT + NP * k + j + 1)
                    pool.tensor_tensor(WS13[1][:, k, eighth(j)], STAGE[:, k, eighth(j)],
                                       WS13[0][:, k, eighth(j)].bitcast(FP32), ALU.subtract).then_inc(p_wsl, 1)
                return part

            norms(0)
            weights_lo(pool, 0, 1, p_kv_lo)
            kv_lo(0, 0)
            weights_lo(pool, 1, 1, p_kv_lo)
            norms(1)
            batch(0, 0, first=True, between=wo_lo)
            with pool.Fori(0, LOOPS) as i:
                batch(2 * i + 1, 1)
                batch(2 * i + 2, 0)
            pool.wait_ge(d_rt, 16)
            pool.tensor_copy(mem["RTS"][:, :, 0, :], mem["RT"][:, :, :]).then_inc(p_rt, 1)
            pool.wait_ge(p_rt, 1)
            pool.tensor_tensor(mem["RTS"][:, :, 1, :], mem["RT"][:, :, :], mem["RTS"][:, :, 0, :].bitcast(FP32),
                               ALU.subtract).then_inc(p_rt, 1)
            batch(NB - 3, 1, between=w2_lo)
            batch(NB - 2, 0, norm=False, between=w13_lo(0))
            batch(NB - 1, 1, following=False, norm=False, between=w13_lo(1))
            rstd(3, 1, v_mv3, p_ve3, p_rs3, NB)

        def row(t, b):
            return t[:, b, 0:D] if isinstance(b, int) else t[:, bass.ds(b, 1), 0:D].rearrange("p a d -> p (a d)")

        def col(t, b):
            return t[:, :, b] if isinstance(b, int) else t[:, :, bass.ds(b, 1)].rearrange("p k a -> p (k a)")

        @block.scalar
        def _(act):
            def kv_hi(n, par):
                act.wait_ge(v_kvf, n + 1)
                act.activation(KVH[par][:, :, :], KVF[par][:, :, :], ACT.Copy).then_inc(a_kvh, 1)

            def unit(n, k):
                kind, i, tile = UNIT[k]
                act.wait_ge(t_unit, NU * n + k + 1)
                src = PS[:, PROJ[BANK[k]], :]
                later = not isinstance(n, int) or n > 0
                if kind == "q":
                    if later:
                        act.wait_ge(t_lg, NP * (n - 1) + HP * (i + 1))
                    part = slice(HP * i, HP * (i + 1))
                    for own in range(2):
                        last = act.activation(QT[OWN[own], own, part, :],
                                              src[OWN[own], :].rearrange("p (j q) -> p j q", j=HP),
                                              ACT.Copy, scale=QSCALE)
                    last.then_inc(a_unit, 1)
                elif kind == "k":
                    if later:
                        act.wait_ge(t_lg, NP * (n - 1) + 2 * (i + 1))
                    for own in range(2):
                        last = act.activation(KT[OWN[own], own, 2 * i:2 * i + 2, :],
                                              src[OWN[own], :].rearrange("p (j q) -> p j q", j=2), ACT.Copy)
                    last.then_inc(a_unit, 1)
                else:
                    if later:
                        act.wait_ge(t_pv, NP * (n - 1) + HP * (i + 1))
                    act.activation(V[:, tile, 512 * i:512 * (i + 1)], src, ACT.Copy).then_inc(a_unit, 1)

            def twice(n, k):
                kind, i, _ = UNIT[k]
                if kind == "q":
                    act.wait_ge(a_unit, NU * n + k + 1)
                    part = slice(HP * i, HP * (i + 1))
                    for own in range(2):
                        act.dma_start(QT[OWN[1 - own], own, part, :].bitcast(FP32), QT[OWN[own], own, part, :].bitcast(FP32))\
                           .then_inc(d_twice, 16)

            def exps(b, j):
                for h in range(2):
                    if h == 0:
                        act.wait_ge(v_mx, NP * b + j + 1)
                        if not (isinstance(b, int) and NP * b + j < 2):
                            act.wait_ge(t_pt, NP * b + j - 1)
                    act.activation(PR[j % 2][:, h, :], PS[:, LG[j % 2], KEYS * h:KEYS * (h + 1)], ACT.Exp, bias=NMX[:, j % 2, h:h + 1],
                                   accum_out=SUM[:, j % 2, h:h + 1]).then_inc(a_exp, 1)

            def copy_pt(b, j):
                act.wait_ge(t_pt, NP * b + j + 1)
                if not (isinstance(b, int) and NP * b + j < 2):
                    act.wait_ge(t_pv, NP * b + j - 1)
                act.activation(PT[j % 2][:, :, :], PS[:, PTB, :].rearrange("p (c q) -> p c q", c=4),
                               ACT.Copy).then_inc(a_pt, 1)

            def o_hi(b, half):
                act.wait_ge(t_pv, NP * b + HP * (half + 1))
                if half == 0 and not (isinstance(b, int) and b == 0):
                    act.wait_ge(t_wo, b)
                act.activation(OTH[:, HP * half:HP * half + HP, :], PS[:, OB, :].rearrange("p (j q) -> p j q", j=HP),
                               ACT.Copy).then_inc(a_oh, 1)

            def wo_hi(j):
                act.wait_ge(d_wo, 16)
                act.activation(WOH[:, j, :], STAGE[:, 0, D * j:D * (j + 1)], ACT.Copy).then_inc(a_woh, 1)

            def w2_hi(j):
                if j < FT:
                    w = fwidth(j)
                    act.wait_ge(d_w2, 32)
                    act.activation(WS2[0][0:w, j, :], STAGE[0:w, 1, D * j:D * (j + 1)], ACT.Copy).then_inc(a_wsh, 1)

            def w13_hi(k):
                def part(j):
                    act.wait_ge(d_w13[k], 16)
                    act.activation(WS13[0][:, k, eighth(j)], STAGE[:, k, eighth(j)], ACT.Copy).then_inc(a_wsh, 1)
                return part

            def tail_hi(j):
                for t in tail_tokens(j):
                    act.wait_ge(t_xt, t + 1)
                    tokens_hi(act, XT, PS[:, PROJ[t % 3], :], t).then_inc(a_xth, 1)

            def batch(b, par, first=False, last=False, between=None):
                for j in range(NP):
                    exps(b, j)
                    if between:
                        between(j)
                    for n, k in filler(b, j - 1, last, False):
                        twice(n, k)
                    if j == 3 and not last:
                        kv_hi(b + 1, 1 - par)
                    for n, k in filler(b, j, last, False):
                        unit(n, k)
                    if j == 1 and not first:
                        o_hi(b - 1, 1)
                    if j == HP + 1:
                        o_hi(b, 0)
                    for n, k in filler(b, j, last, True):
                        unit(n, k)
                    if not first or j > 0:
                        copy_pt(*at(b, j - 1))
                    if last:
                        tail_hi(j)

            def weights_hi(half, ready):
                act.wait_ge(ready, 16)
                for k in (1, 0):
                    act.activation(WKVH[:, k, INNER * half:INNER * (half + 1)],
                                   STAGE[:, half, INNER * k:INNER * (k + 1)], ACT.Copy).then_inc(a_kv_hi, 1)

            weights_hi(0, d_wk)
            kv_hi(0, 0)
            weights_hi(1, d_wv)
            for k in range(NU // 2):
                unit(0, k)
                if k == 0:
                    twice(0, 0)
            batch(0, 0, first=True, between=wo_hi)
            with act.Fori(0, LOOPS) as i:
                batch(2 * i + 1, 1)
                batch(2 * i + 2, 0)
            batch(NB - 3, 1, between=w2_hi)
            batch(NB - 2, 0, between=w13_hi(0))
            batch(NB - 1, 1, last=True, between=w13_hi(1))
            copy_pt(NB - 1, NP - 1)
            tail_hi(NP)
            o_hi(NB - 1, 1)
            tail_hi(NP + 1)
            tail_hi(NP + 2)
            act.activation(NMX[:, 0, :], MHALF[:, :], ACT.Silu)

        @block.vector
        def _(dve):
            def norm_stats(n):
                dve.wait_ge(d_rows, 32 * (n + 1))
                dve.bn_stats(ST[:, 0, :], RC[:, :])
                dve.bn_stats(ST[:, 1, :], RX[:, :]).then_inc(v_st, 1)
                dve.wait_ge(v_st, n + 1)
                dve.nop(nofuse=True)
                dve.bn_aggr(MV[:, 0, :], ST[:, 0, :])
                dve.bn_aggr(MV[:, 1, :], ST[:, 1, :]).then_inc(v_mv, 1)

            def norm_rows(n, guard=True):
                dve.wait_ge(p_rs, n + 1)
                if guard:
                    dve.wait_ge(t_in, n)
                dve.tensor_scalar(CN[:, :], RC[:, :], MV[:, 0, 0:1], RS[:, 0:1], ALU.subtract, ALU.mult)
                dve.tensor_scalar(XN[:, :], RX[:, :], MV[:, 1, 0:1], RS[:, 1:2], ALU.subtract, ALU.mult)\
                   .then_inc(v_xn1, 1)
                dve.wait_ge(v_xn1, n + 1)
                dve.bn_stats(ST[:, 2, :], XN[:, :]).then_inc(v_st2, 1)
                dve.wait_ge(v_st2, n + 1)
                dve.nop(nofuse=True)
                dve.bn_aggr(MV[:, 2, :], ST[:, 2, :]).then_inc(v_mv2, 1)

            def norm_again(n):
                dve.tensor_copy(AFF[:, 0, :], col(LATA, n))
                dve.tensor_copy(AFF[:, 1, :], col(LATC, n)).then_inc(v_aff, 1)
                dve.wait_ge(p_rs2, n + 1)
                dve.tensor_scalar(XN[:, :], XN[:, :], MV[:, 2, 0:1], RS[:, 2:3], ALU.subtract, ALU.mult)\
                   .then_inc(v_xn, 1)

            def modulate(n, par):
                dve.wait_ge(t_in, n + 1)
                dve.wait_ge(v_aff, n + 1)
                if not isinstance(n, int) or n > 1:
                    dve.wait_ge(p_kvl, n - 1)
                for k in range(KD):
                    src = PS[:, MISC, KEYS * k:KEYS * (k + 1)]
                    dve.tensor_scalar(KVF[par][:, k, 0:P], src[:, 0:P], LNP[:, 0, k:k + 1], LNP[:, 1, k:k + 1],
                                      ALU.mult, ALU.add)
                    last = dve.tensor_scalar(KVF[par][:, k, P:KEYS], src[:, P:KEYS], AFF[:, 0, k:k + 1],
                                             AFF[:, 1, k:k + 1], ALU.mult, ALU.add)
                last.then_inc(v_kvf, 1)

            def unit_lo(n, k):
                kind, i, _ = UNIT[k]
                src = PS[:, PROJ[BANK[k]], :]
                dve.wait_ge(a_unit, NU * n + k + 1)
                if kind == "q":
                    part = slice(HP * i, HP * (i + 1))
                    for own in range(2):
                        last = dve.scalar_tensor_tensor(
                            QTL[OWN[own], own, part, :], src[OWN[own], :].rearrange("p (j q) -> p j q", j=HP), QSCALE,
                            QT[OWN[own], own, part, :].bitcast(FP32), ALU.mult, ALU.subtract)
                    last.then_inc(v_unit, 1)
                elif kind == "k":
                    part = slice(2 * i, 2 * i + 2)
                    for own in range(2):
                        last = dve.tensor_tensor(KT[OWN[1 - own], own, part, :],
                                                 src[OWN[own], :].rearrange("p (j q) -> p j q", j=2),
                                                 KT[OWN[own], own, part, :].bitcast(FP32), ALU.subtract)
                    last.then_inc(v_unit, 1)

            def row_max(b, j):
                dve.wait_ge(t_lg, NP * b + j + 1)
                if not (isinstance(b, int) and NP * b + j < 2):
                    dve.wait_ge(a_exp, 2 * (NP * b + j - 1))
                dve.tensor_reduce(NMX[:, j % 2, :], PS[:, LG[j % 2], :].rearrange("p (h k) -> p h k", h=2), AX.X,
                                  ALU.max, negate=True)\
                   .then_inc(v_mx, 1)

            def normalise(b, j):
                n = NP * b + j + 1
                dve.wait_ge(a_exp, 2 * n)
                dve.reciprocal(RINV[:, j % 2, :], SUM[:, j % 2, :]).then_inc(v_rinv, 1)
                dve.wait_ge(v_rinv, n)
                dve.tensor_scalar(PR[j % 2][:, 0, :], PR[j % 2][:, 0, :], RINV[:, j % 2, 0:1], None, ALU.mult)\
                   .then_inc(v_pr, 1)

            def o_lo(b, half):
                dve.wait_ge(a_oh, 2 * b + half + 1)
                lo, hi = HP * half, HP * half + HP
                dve.tensor_tensor(OTL[:, lo:hi, :], PS[:, OB, :].rearrange("p (j q) -> p j q", j=HP),
                                  OTH[:, lo:hi, :].bitcast(FP32), ALU.subtract).then_inc(v_ol, 1)

            def residual(b):
                dve.wait_ge(t_wo, b + 1)
                dve.wait_ge(d_rr, 16 * (b + 1))
                dve.tensor_tensor(X2[:, :], PS[:, MISC, 0:D], RR[:, :], ALU.add).then_inc(v_res, 1)
                dve.wait_ge(v_res, b + 1)
                dve.bn_stats(ST[:, 3, :], X2[:, :]).then_inc(v_st3, 1)
                dve.wait_ge(v_st3, b + 1)
                dve.nop(nofuse=True)
                dve.bn_aggr(MV[:, 3, :], ST[:, 3, :]).then_inc(v_mv3, 1)

            def expert_input(b):
                dve.wait_ge(p_rs3, b + 1)
                dve.tensor_scalar(row(C, b), X2[:, :], MV[:, 3, 0:1], RS[:, 3:4], ALU.subtract, ALU.mult)\
                   .then_inc(v_x2, 1)

            def tail_lo(j):
                for t in tail_tokens(j):
                    dve.wait_ge(a_xth, t + 1)
                    tokens_lo(dve, XT, PS[:, PROJ[t % 3], :], t).then_inc(v_xtl, 1)

            def batch(b, par, first=False, following=True, norm=True):
                for j in range(NP):
                    row_max(b, j)
                    if not following:
                        tail_lo(j - 1)
                    for n, k in late_lo(b, j - 1, not following):
                        unit_lo(n, k)
                    if j == 2 and following:
                        modulate(b + 1, 1 - par)
                    if norm and j in (3, 4, 6):
                        {3: norm_stats, 4: norm_rows, 6: norm_again}[j](b + 2)
                    if j == 7 and not first:
                        residual(b - 1)
                    normalise(b, j)
                    for n, k in early_lo(b, j, not following):
                        unit_lo(n, k)
                    if j == 1 and not first:
                        o_lo(b - 1, 1)
                    if j == HP + 1:
                        o_lo(b, 0)
                    if j == 7 and not first:
                        expert_input(b - 1)

            dve.wait_ge(p_const, 2)
            for h in range(2):
                for j in range(0, NP, D // P):
                    last = dve.tensor_copy(QTL[OWN[1 - h], h, j:j + D // P, :],
                                            ZERO[OWN[1 - h], 0:D].rearrange("p (j q) -> p j q", q=P))
                last.then_inc(v_zeros, 1)
            norm_stats(0)
            dve.wait_ge(d_small, 16 * 2)
            dve.tensor_scalar(LATA[:, :, :], COND[:, :, :], 1.0, None, ALU.add).then_inc(v_cond, 1)
            dve.wait_ge(v_cond, 1)
            for k in range(KD):
                dve.tensor_scalar(LATC[:, k, :], LATA[:, k, :], LNP[:, 3, k:k + 1], None, ALU.mult).then_inc(v_cond, 1)
            dve.wait_ge(v_cond, 3)
            for k in range(KD):
                dve.tensor_scalar(LATA[:, k, :], LATA[:, k, :], LNP[:, 2, k:k + 1], None, ALU.mult)
            dve.tensor_tensor(LATC[:, :, :], LATC[:, :, :], COND[:, :, :], ALU.add).then_inc(v_cond, 1)
            dve.wait_ge(v_cond, 4)
            norm_rows(0, guard=False)
            norm_again(0)
            modulate(0, 0)
            weights_lo(dve, 0, 0, v_kv_lo)
            weights_lo(dve, 1, 0, v_kv_lo)
            unit_lo(0, 0)
            norm_stats(1)
            unit_lo(0, 1)
            norm_rows(1)
            unit_lo(0, 2)
            norm_again(1)
            batch(0, 0, first=True)
            with dve.Fori(0, LOOPS) as i:
                batch(2 * i + 1, 1)
                batch(2 * i + 2, 0)
            batch(NB - 3, 1)
            batch(NB - 2, 0, norm=False)
            batch(NB - 1, 1, following=False, norm=False)
            for j in (NP - 1, NP):
                tail_lo(j)
            o_lo(NB - 1, 1)
            tail_lo(NP + 1)
            residual(NB - 1)
            tail_lo(NP + 2)
            expert_input(NB - 1)

        @block.tensor
        def _(pe):
            def transpose_inputs(n):
                pe.wait_ge(v_xn, n + 1)
                for k in range(KD):
                    for i, src in enumerate((CN, XN)):
                        last = pe.transpose(PS[:, MISC, KEYS * k + P * i:KEYS * k + P * (i + 1)],
                                            src[:, 128 * k:128 * (k + 1)], IDENT[:, :])
                last.then_inc(t_in, 1)

            def split3(dst, stat, mov, steps, begin=True, end=True):
                todo = [(k, s, m) for k in steps for s, m in ((0, 0), (0, 1), (1, 0))]
                for n, (k, s, m) in enumerate(todo):
                    last = pe.matmul(dst, stat(s, k), mov(m, k), start=begin and n == 0,
                                     stop=end and n == len(todo) - 1)
                return last

            wkv = (WKVH, WKVL)
            oT = (OTH, OTL)
            wo = (WOH, WOL)

            def unit(n, k, par):
                kind, i, tile = UNIT[k]
                kv = (KVH[par], KVL[par])
                dst = PS[:, PROJ[BANK[k]], :]
                pk = max(i for i in range(k - NU, k) if BANK[i % NU] == BANK[k])
                if pk >= 0 or not isinstance(n, int) or n > 0:
                    before, pk = (n, pk) if pk >= 0 else (n - 1, pk + NU)
                    if UNIT[pk][0] == "v":
                        pe.wait_ge(a_unit, NU * before + pk + 1)
                    else:
                        pe.wait_ge(v_unit, lo_count(before, pk))
                if kind == "q":
                    if i == 0:
                        pe.wait_ge(v_kvf, n + 1)
                    for j in range(HP):
                        e = 128 * (HP * i + j)
                        for c in range(KD):
                            last = pe.matmul(dst[:, P * j:P * (j + 1)], WQ[:, c, e:e + 128], KVF[par][:, c, P:KEYS],
                                             start=c == 0, stop=c == KD - 1)
                elif kind == "k":
                    if i == 0:
                        pe.wait_ge(a_kvh, n + 1)
                        pe.wait_ge(p_kvl, n + 1)
                    for j in range(2):
                        e = 128 * (2 * i + j)
                        last = split3(dst[:, KEYS * j:KEYS * (j + 1)], lambda s, c: wkv[s][:, c, e:e + 128],
                                      lambda m, c: kv[m][:, c, :], range(KD))
                else:
                    e = INNER + 512 * i
                    last = split3(dst, lambda s, c: kv[s][:, c, P * tile:P * (tile + 1)],
                                  lambda m, c: wkv[m][:, c, e:e + 512], range(KD))
                last.then_inc(t_unit, 1)

            def logits(b, j):
                pe.wait_ge(v_unit, lo_count(b, max(KUNIT[j // 2], QUNIT[j // HP])))
                pe.wait_ge(d_twice, 32 * (2 * b + j // HP + 1))
                if not (isinstance(b, int) and NP * b + j < 2):
                    pe.wait_ge(a_exp, 2 * (NP * b + j - 1))
                for h in range(2):
                    dst = PS[:, LG[j % 2], KEYS * h:KEYS * (h + 1)]
                    pe.matmul(dst, QT[:, h, j, :], KT[:, h, j, :], start=True, stop=False)
                    last = pe.matmul(dst, QTL[:, h, j, :], KT[:, h, j, :], start=False, stop=True)
                last.then_inc(t_lg, 1)

            def transpose_probs(b, j):
                pe.wait_ge(v_pr, NP * b + j + 1)
                pe.wait_ge(p_pr, NP * b + j + 1)
                if not (isinstance(b, int) and NP * b + j < 1):
                    pe.wait_ge(a_pt, NP * b + j)
                for h in range(2):
                    for t in range(2):
                        c = 2 * h + t
                        last = pe.transpose(PS[:, PTB, P * c:P * (c + 1)], PR[j % 2][:, h, P * t:P * (t + 1)],
                                            IDENT[:, :])
                last.then_inc(t_pt, 1)

            def times_v(b, j):
                pe.wait_ge(a_unit, NU * b + (NU if j >= HP else NU // 2))
                pe.wait_ge(a_pt, NP * b + j + 1)
                if j % HP == 0 and not (isinstance(b, int) and b == 0 and j == 0):
                    pe.wait_ge(v_ol, 2 * b + j // HP)
                for t in range(2):
                    for h in range(2):
                        e = 128 * j + DH * h
                        last = pe.matmul(PS[DH * h:DH * (h + 1), OB, P * (j % HP):P * (j % HP + 1)],
                                         V[:, t, e:e + DH], PT[j % 2][:, 2 * h + t, :],
                                         start=t == 0, stop=t == 1)
                last.then_inc(t_pv, 1)

            def output_projection(b, half):
                pe.wait_ge(v_ol, 2 * b + 1 + half)
                if half == 0:
                    pe.wait_ge(p_wo, KC)
                pe.wait_ge(v_kvf, min(b + 3, NB) if isinstance(b, int) else b + 3)
                last = split3(PS[:, MISC, 0:D], lambda s, c: oT[s][:, c, :], lambda m, c: wo[m][:, c, :],
                              range(HP * half, HP * half + HP), begin=half == 0, end=half == 1)
                if half == 1:
                    last.then_inc(t_wo, 1)

            def batch(b, par, first=False, last=False):
                for j in range(NP):
                    logits(b, j)
                    if j == 2 and not last:
                        transpose_inputs(b + 1)
                    if j == HP + 1 and not first:
                        output_projection(b - 1, 1)
                    for n, k in filler(b, j, last, False):
                        unit(n, k, par if k >= NU // 2 else 1 - par)
                    if not first or j > 1:
                        times_v(*at(b, j - 2))
                    if j == 3 and not first:
                        output_projection(b - 1, 0)
                    for n, k in filler(b, j, last, True):
                        unit(n, k, par if k >= NU // 2 else 1 - par)
                    if not first or j > 0:
                        transpose_probs(*at(b, j - 1))
                    if last:
                        tail_transposes(j)

            def tail_transposes(j):
                for t in tail_tokens(j):
                    if t == 0:
                        pe.wait_ge(v_x2, AHEAD)
                        pe.wait_ge(a_unit, NU * NB)
                        pe.wait_ge(v_unit, LOS * NB)
                    if t >= 3:
                        pe.wait_ge(v_xtl, t - 2)
                    transpose_tokens(pe, PS[:, PROJ[t % 3], :], C, IDENT, t).then_inc(t_xt, 1)

            pe.wait_ge(p_ident, 2)
            transpose_inputs(0)
            pe.wait_ge(d_wq, 16)
            for k in range(NU // 2):
                if k == 1:
                    pe.wait_ge(v_kv_lo, 1)
                    pe.wait_ge(p_kv_lo, 1)
                if k == 3:
                    pe.wait_ge(v_kv_lo, 2)
                    pe.wait_ge(p_kv_lo, 2)
                unit(0, k, 0)
            pe.wait_ge(v_zeros, 2)
            batch(0, 0, first=True)
            with pe.Fori(0, LOOPS) as i:
                batch(2 * i + 1, 1)
                batch(2 * i + 2, 0)
            batch(NB - 3, 1)
            batch(NB - 2, 0)
            batch(NB - 1, 1, last=True)
            times_v(NB - 1, NP - 2)
            transpose_probs(NB - 1, NP - 1)
            tail_transposes(NP)
            pe.wait_ge(v_res, NB - 1)
            output_projection(NB - 1, 0)
            times_v(NB - 1, NP - 1)
            tail_transposes(NP + 1)
            output_projection(NB - 1, 1)
            tail_transposes(NP + 2)


def filler(b, j, last, behind):
    if j < 0:
        ks = []
    elif last:
        ks = [] if behind else {0: [5], 1: [6], 2: [7], 4: [8], 5: [9]}.get(j, [])
    else:
        ks = ({1: [7], 5: [11], 6: [13]} if behind else {0: [5], 1: [6], 2: [8], 3: [9], 4: [10], 6: [12], 7: [14]})\
            .get(j, [])
    return [(b, k) if k < NU else (b + 1, k - NU) for k in ks]


def scored(f):
    return range(3 * f - 3, 3 * f if f < FT - 1 else NB) if f else range(0)


def early_lo(b, j, last):
    return [(n, k) for n, k in filler(b, j, last, False) if UNIT[k][0] == "k"]


def late_lo(b, j, last):
    return [(n, k) for n, k in filler(b, j, last, False) if UNIT[k][0] == "q"] + filler(b, j, last, True)


def at(b, j):
    return (b, j) if j >= 0 else (b - 1, NP + j)


def between(f):
    return range(AHEAD + 2 * f, AHEAD + 2 * f + 2) if 0 <= f < (NB - AHEAD) // 2 else range(0)


def tokens_hi(act, XT, bank, t):
    return act.activation(XT[0][:, :, t * P:(t + 1) * P], bank[:, 0:KD * P].rearrange("p (k q) -> p k q", k=KD),
                          ACT.Copy)


def tokens_lo(dve, XT, bank, t):
    return dve.tensor_tensor(XT[1][:, :, t * P:(t + 1) * P], bank[:, 0:KD * P].rearrange("p (k q) -> p k q", k=KD),
                             XT[0][:, :, t * P:(t + 1) * P].bitcast(FP32), ALU.subtract)


def transpose_tokens(pe, bank, C, IDENT, t):
    for k in range(KD):
        last = pe.transpose(bank[:, P * k:P * (k + 1)], C[:, t, 128 * k:128 * (k + 1)], IDENT[:, :])
    return last


def tail_tokens(j):
    n = j - NP + 2
    return range(TAIL[n], TAIL[n + 1]) if n >= 0 else range(0)


def lo_count(n, k):
    return LOS * n + sum(UNIT[i][0] != "v" for i in range(k + 1))


def load_w2(sp, dst, tiles, last, done):
    sp.dma_start(dst[:, 0:FT - 1, :], tiles).then_inc(done, 16)
    sp.dma_start(dst[0:FL, FT - 1, :], last).then_inc(done, 16)


def experts_part(nc, a, mem, out):
    C, IDENT, PS, RTS = mem["C"], mem["IDENT"], mem["PS"], mem["RTS"]
    WS13, WS2, xs, base, XT = mem["WS13"], mem["WS2"], mem["xs"], mem["base"], mem["WKV_XT"]
    ctx = ExitStack()
    with ctx:
        def sb(name, shape, dt=FP32):
            return ctx.enter_context(nc.sbuf_tensor(name, shape, dt))

        def sem(name):
            return ctx.enter_context(nc.semaphore(name))

        X = sb("X", [128, NB, D])
        W13 = [sb(f"W13_{i}", [128, KD, 2 * F]) for i in range(2)]
        W2 = [sb(f"W2_{i}", [128, FT, D]) for i in range(2)]
        MIDF = [sb(f"MIDF{i}", [128, GT]) for i in range(2)]
        MID = [sb(f"MID{p}", [128, FT, GT], FP32R) for p in "HL"]
        SC = sb("SC", [128, NB, NE])
        BEST = sb("BEST", [128, NB])
        ONE = sb("ONE", [128, NB, NE])
        CAND = sb("CAND", [128, NB, NE])
        IDX = sb("IDX", [128, NB])
        IOTA_I = sb("IOTA_I", [128, NE + NE * NB + NT * NE + NB], I32)
        IOTA = sb("IOTA", [128, NE + NE * NB + NT * NE + NB])
        UPPER = sb("UPPER", [128, 128])
        ONES = sb("ONES", [128, 128])
        GATE = sb("GATE", [128, NB])
        RANK = sb("RANK", [128, NB, NE])
        CNT = [sb(f"CNT{i}", [128, NB + 1, NE]) for i in range(2)]
        NTE = sb("NTE", [128, NE])
        HIT = sb("HIT", [128, NE, NB])
        ENDT = sb("ENDT", [128, NE + 1])
        OWN = sb("OWN", [128, NT, NE])
        ETF = sb("ETF", [128, NT])
        ETI = sb("ETI", [1, NT], I32)
        POSF = sb("POSF", [128, NB])
        POSI = sb("POSI", [128, NB], I32)
        XS = [sb(f"XS{i}", [128, DI]) for i in range(2)]
        WHO = sb("WHO", [128, NT], I32)
        XST = [sb(f"XST{i}", [128, KD, P]) for i in range(2)]
        SIL = sb("SIL", [128, FT * P])
        MRT = [sb(f"MRT{i}", [128, FT * P]) for i in range(2)]
        YS = [sb(f"YS{i}", [128, D]) for i in range(2)]
        BASE = [sb(f"BASE{i}", [128, D]) for i in range(2)]

        TRB = [0, 1]
        RTB = 2
        HB = [(3, 4), (5, 6)]
        OUTB = [7, 0]
        OUTB_LAST = [3, 7]
        EH = [0, 3]
        EX = 6
        EY = 7

        d_x = sem("d_x")
        p_iota = sem("p_iota")
        p_mask = sem("p_mask")
        t_xt = sem("t_xt")
        a_xth = sem("a_xth")
        v_xtl = sem("v_xtl")
        t_sc = sem("t_sc")
        v_rt = sem("v_rt")
        a_gate = sem("a_gate")
        t_rank = sem("t_rank")
        v_gate = sem("v_gate")
        p_xg = sem("p_xg")
        v_pos = sem("v_pos")
        v_et = sem("v_et")
        d_sc = sem("d_sc")
        t_h = sem("t_h")
        a_sil = sem("a_sil")
        v_mid = sem("v_mid")
        a_midh = sem("a_midh")
        v_midl = sem("v_midl")
        t_so = sem("t_so")
        v_so = sem("v_so")
        d_xs = [sem(f"d_xs{i}") for i in range(2)]
        d_w13 = [sem(f"d_w13{i}") for i in range(2)]
        d_w2 = [sem(f"d_w2{i}") for i in range(2)]
        d_bs = sem("d_bs")
        a_who = sem("a_who")
        v_zero = sem("v_zero")
        d_base = [sem(f"d_base{i}") for i in range(2)]
        d_y = [sem(f"d_y{i}") for i in range(2)]
        t_ex = sem("t_ex")
        a_ex = sem("a_ex")
        t_eh = sem("t_eh")
        a_es = sem("a_es")
        v_em = sem("v_em")
        t_ey = sem("t_ey")
        v_ey = sem("v_ey")

        block = ctx.enter_context(nc.Block())

        def hidden_of(par):
            return PS[:, EH[par]:EH[par] + 3, :].rearrange("p b f -> p (b f)")

        def lhs13(w, k, i):
            lo = FM if i == 2 * (FT - 1) else 128 * i if i < FT - 1 else F + FL + 128 * (i - FT + 1)
            return w[:, k, lo:lo + 128]

        def tile_rows(t, n):
            return t[n * P:(n + 1) * P, :] if isinstance(n, int) else t[bass.ds(n * P, P), :]

        @block.sync
        def _(sp):
            def expert_of(t):
                return sp.value_load(ETI[0:1, t:t + 1] if isinstance(t, int) else ETI[0:1, bass.ds(t, 1)],
                                     min_val=0, max_val=NE - 1)

            def load_hidden(t, par, first=False):
                e = expert_of(t)
                if not first:
                    sp.wait_ge(t_eh, t - 1)
                sp.dma_start(W13[par][:, :, :], a["w13"][bass.ds(e, 1), :, :, :].rearrange("a p k f -> p (a k) f"))\
                  .then_inc(d_w13[par], 16)

            def load_output(t, par, first=False):
                e = expert_of(t)
                if not first:
                    sp.wait_ge(t_ey, t - 1)
                load_w2(sp, W2[par], a["w2"][bass.ds(e, 1), :, :, :].rearrange("a p k d -> p (a k) d"),
                        a["w2_last"][bass.ds(e, 1), :, :].rearrange("a p d -> (a p) d"), d_w2[par])

            sp.dma_start(X[:, :, :], base.rearrange("(b p) d -> p b d", p=P)).then_inc(d_x, 16)
            sp.wait_ge(v_et, 1)
            for t in range(2):
                load_hidden(t, t, first=True)
                load_output(t, t, first=True)
            sp.wait_ge(d_sc, 16 * NB)
            for t in range(2):
                sp.dma_start(XS[t][:, :], tile_rows(xs, t)).then_inc(d_xs[t], 16)
            for g in range(NG):
                sp.wait_ge(v_so, 4 * (g + 1))
                sp.dma_start(base[GT * g:GT * (g + 1), :].rearrange("(b p) d -> p b d", p=P),
                             X[:, 4 * g:4 * (g + 1), :]).then_inc(d_bs, 16)
            load_hidden(2, 0)
            with sp.Fori(1, (NT - 1) // 2) as i:
                load_hidden(2 * i + 1, 1)
                load_output(2 * i, 0)
                load_hidden(2 * i + 2, 0)
                load_output(2 * i + 1, 1)
            load_output(NT - 1, 0)
            sp.wait_ge(d_bs, 16 * NG)

        @block.gpsimd
        def _(pool):
            pool.iota(IOTA_I[:, 0:NE], pattern=[[1, NE]], base=0, channel_multiplier=0).then_inc(p_iota, 1)
            pool.iota(IOTA_I[:, NE:NE + NE * NB], pattern=[[0, NE], [P, NB]], base=0, channel_multiplier=0)\
                .then_inc(p_iota, 1)
            pool.iota(IOTA_I[:, NE + NE * NB:NE + NE * NB + NT * NE], pattern=[[1, NT], [0, NE]], base=0,
                      channel_multiplier=0).then_inc(p_iota, 1)
            pool.iota(IOTA_I[:, NE + NE * NB + NT * NE:], pattern=[[P, NB]], base=0, channel_multiplier=1)\
                .then_inc(p_iota, 1)
            pool.memset(ONES[:, :], 1.0).then_inc(p_mask, 1)
            pool.wait_ge(p_mask, 1)
            pool.affine_select(out=UPPER[:, :], in_=ONES[:, :], compare_op=ALU.is_gt, fill=0.0,
                               base=0, pattern=[[1, 128]], channel_multiplier=-1).then_inc(p_mask, 1)

            pool.wait_ge(v_gate, 1)
            for b in range(NB):
                pool.tensor_scalar(C[:, b, 0:D], C[:, b, 0:D], GATE[:, b:b + 1], None, ALU.mult).then_inc(p_xg, 1)
            pool.wait_ge(v_pos, 1)
            for b in range(NB):
                pool.wait_ge(p_xg, b + 1)
                pool.indirect_dma_start(out=xs, out_offset=bass.IndirectOffsetOnAxis(ap=POSI[:, b:b + 1], axis=0),
                                        in_=C[:, b, :], in_offset=None).then_inc(d_sc, 16)

            for par in range(2):
                pool.memset(BASE[par][:, :], 0.0).then_inc(v_zero, 1)
            pool.wait_ge(v_zero, 2)
            pool.wait_ge(d_bs, 16 * NG)

            def gather_base(t):
                pool.wait_ge(a_who, t + 1)
                if t >= 2:
                    pool.wait_ge(v_ey, t - 1)
                pool.indirect_dma_start(out=BASE[t % 2][:, :], out_offset=None, in_=base,
                                        in_offset=bass.IndirectOffsetOnAxis(ap=WHO[:, t:t + 1], axis=0),
                                        bounds_check=TOK - 1, oob_is_err=False).then_inc(d_base[t % 2], 16)

            gather_base(0)
            for t in range(NT):
                if t + 1 < NT:
                    gather_base(t + 1)
                pool.wait_ge(v_ey, t + 1)
                pool.indirect_dma_start(out=out, out_offset=bass.IndirectOffsetOnAxis(ap=WHO[:, t:t + 1], axis=0),
                                        in_=YS[t % 2][:, :], in_offset=None,
                                        bounds_check=TOK - 1, oob_is_err=False).then_inc(d_y[t % 2], 16)
            for par in range(2):
                pool.wait_ge(d_y[par], 16 * ((NT + 1 - par) // 2))

        @block.scalar
        def _(act):
            def x_hi(t):
                act.wait_ge(t_xt, t - AHEAD + 1)
                tokens_hi(act, XT, PS[:, TRB[t % 2], :], t).then_inc(a_xth, 1)

            def shared_silu(g, f):
                w = fwidth(f)
                n = FT * g + f
                act.wait_ge(t_h, n + 1)
                if f == 1:
                    act.wait_ge(v_mid, n)
                act.activation(SIL[0:w, 0:GT], PS[0:w, HB[f % 2][0], :], ACT.Silu).then_inc(a_sil, 1)

            def shared_mid(g, f):
                w = fwidth(f)
                act.wait_ge(v_mid, FT * g + f + 1)
                if f == 0 and not (isinstance(g, int) and g == 0):
                    act.wait_ge(t_so, 4 * g)
                act.activation(MID[0][0:w, f, :], MIDF[f % 2][0:w, :], ACT.Copy).then_inc(a_midh, 1)

            for f in range(FT):
                shared_silu(0, f)
                shared_mid(0, f)
                for t in between(f):
                    x_hi(t)

            def shared_group(g, gate=False, last=False):
                for f in range(2):
                    shared_silu(g, f)
                if gate:
                    act.wait_ge(v_rt, 4)
                    act.activation(GATE[:, :], BEST[:, :], ACT.Exp, scale=-1.0).then_inc(a_gate, 1)
                for f in range(2):
                    shared_mid(g, f)
                for f in range(2, FT):
                    shared_silu(g, f)
                    if last and f == FT - 2:
                        copy_x(0, 0, free=False)
                    shared_mid(g, f)

            def copy_x(t, par, free=True, load=True):
                act.wait_ge(t_ex, t + 1)
                if free:
                    act.wait_ge(t_eh, t - 1)
                act.activation(XST[par][:, :, :], PS[:, EX, 0:KD * P].rearrange("p (k q) -> p k q", k=KD),
                               ACT.Copy).then_inc(a_ex, 1)
                act.activation(WHO[:, t:t + 1] if isinstance(t, int) else WHO[:, bass.ds(t, 1)],
                               XS[par][:, D:DI], ACT.Copy).then_inc(a_who, 1)
                if load:
                    act.wait_ge(a_who, t + 1)
                    act.dma_start(XS[par][:, :], tile_rows(xs, t + 2)).then_inc(d_xs[par], 16)

            def routed_act(t, par, copy_next):
                if copy_next:
                    copy_x(t + 1, 1 - par, free=not (isinstance(t, int) and t == 0),
                           load=not (isinstance(t, int) and t + 3 >= NT))
                act.wait_ge(t_eh, t + 1)
                if not (isinstance(t, int) and t == 0):
                    act.wait_ge(v_em, t)
                h = hidden_of(par)
                act.activation(SIL[:, 0:FM], h[:, 0:FM], ACT.Silu)
                act.activation(SIL[0:FL, FM:FM + P], h[0:FL, 2 * FM:2 * FM + P], ACT.Silu).then_inc(a_es, 1)

            for g in range(1, NG):
                shared_group(g, gate=g == 1, last=g == NG - 1)
            routed_act(0, 0, True)
            with act.Fori(0, (NT - 5) // 2) as i:
                routed_act(2 * i + 1, 1, True)
                routed_act(2 * i + 2, 0, True)
            routed_act(NT - 4, 1, True)
            routed_act(NT - 3, 0, True)
            routed_act(NT - 2, 1, True)
            routed_act(NT - 1, 0, False)

        @block.vector
        def _(dve):
            done = [0]

            def step(ins):
                done[0] += 1
                ins.then_inc(v_rt, 1)
                dve.wait_ge(v_rt, done[0])

            def over_tiles(t):
                return t.rearrange("p (a e) -> p a e", a=1).to_broadcast([128, NB, NE])

            def x_lo(t):
                dve.wait_ge(a_xth, t - AHEAD + 1)
                tokens_lo(dve, XT, PS[:, TRB[t % 2], :], t).then_inc(v_xtl, 1)

            dve.wait_ge(p_iota, 4)
            step(dve.tensor_copy(IOTA[:, :], IOTA_I[:, :]))
            dve.tensor_copy(C[:, :, D:DI].rearrange("p b a -> p (b a)"), IOTA[:, NE + NE * NB + NT * NE:])

            def choose_experts():
                dve.wait_ge(t_sc, NB)
                scores = PS[:, RTB, 0:NB * 2 * NE].rearrange("p (b m e) -> p b m e", b=NB, m=2)
                step(dve.tensor_copy(SC[:, :, :], scores[:, :, 1, :]))
                step(dve.tensor_tensor(SC[:, :, :], scores[:, :, 0, :], SC[:, :, :], ALU.add))
                step(dve.tensor_reduce(BEST[:, :], SC[:, :, :], AX.X, ALU.max))
                best = BEST[:, :].rearrange("p (b a) -> p b a", a=1).to_broadcast([128, NB, NE])
                step(dve.tensor_tensor(CAND[:, :, :], SC[:, :, :], best, ALU.is_lt))
                experts = over_tiles(IOTA[:, 0:NE])
                step(dve.tensor_scalar(CAND[:, :, :], CAND[:, :, :], float(NE), None, ALU.mult))
                step(dve.tensor_tensor(CAND[:, :, :], CAND[:, :, :], experts, ALU.add))
                step(dve.tensor_reduce(IDX[:, :], CAND[:, :, :], AX.X, ALU.min))
                idx = IDX[:, :].rearrange("p (b a) -> p b a", a=1).to_broadcast([128, NB, NE])
                step(dve.tensor_tensor(ONE[:, :, :], experts, idx, ALU.is_equal))

            def counts():
                dve.wait_ge(a_gate, 1)
                step(dve.tensor_scalar(GATE[:, :], GATE[:, :], 1.0, None, ALU.add))
                dve.reciprocal(GATE[:, :], GATE[:, :]).then_inc(v_gate, 1)
                dve.wait_ge(t_rank, 1)
                dve.tensor_copy(RANK[:, :, :], PS[:, RTB, 0:NB * NE].rearrange("p (b e) -> p b e", b=NB))
                for half in range(2):
                    dve.memset(CNT[half][:, 0, :], 0.0)
                step(dve.tensor_copy(CNT[0][:, 1:NB + 1, :],
                                     PS[:, RTB, NB * NE:2 * NB * NE].rearrange("p (b e) -> p b e", b=NB)))

            def running_sums(rounds):
                for n in rounds:
                    src, dst, ahead = CNT[n % 2], CNT[1 - n % 2], 1 << n
                    dve.tensor_copy(dst[:, 1:ahead + 1, :], src[:, 1:ahead + 1, :])
                    step(dve.tensor_tensor(dst[:, ahead + 1:, :], src[:, ahead + 1:, :], src[:, 1:NB + 1 - ahead, :],
                                           ALU.add))

            rounds = (NB - 1).bit_length()
            cnt = CNT[rounds % 2]

            def tiles_needed():
                total = cnt[:, NB, :].rearrange("p (e a) -> p e a", a=1).to_broadcast([128, NE, NB])
                step(dve.tensor_tensor(HIT[:, :, :], IOTA[:, NE:NE + NE * NB].rearrange("p (e j) -> p e j", e=NE),
                                       total, ALU.is_lt))
                step(dve.tensor_reduce(NTE[:, :], HIT[:, :, :], AX.X, ALU.add))
                step(dve.memset(ENDT[:, 0:1], 0.0))

            def first_tiles(experts):
                for e in experts:
                    step(dve.tensor_tensor(ENDT[:, e + 1:e + 2], ENDT[:, e:e + 1], NTE[:, e:e + 1], ALU.add))

            def slots():
                step(dve.tensor_scalar(NTE[:, :], ENDT[:, 0:NE], float(P), None, ALU.mult))
                step(dve.tensor_tensor(RANK[:, :, :], RANK[:, :, :], cnt[:, 0:NB, :], ALU.add))
                step(dve.tensor_tensor(RANK[:, :, :], RANK[:, :, :], over_tiles(NTE[:, :]), ALU.add))

            def own_slots():
                step(dve.tensor_tensor(RANK[:, :, :], RANK[:, :, :], ONE[:, :, :], ALU.mult))
                step(dve.tensor_reduce(POSF[:, :], RANK[:, :, :], AX.X, ALU.add))
                dve.tensor_copy(POSI[:, :], POSF[:, :]).then_inc(v_pos, 1)

            def experts_of_tiles():
                ends = ENDT[:, 1:NE + 1].rearrange("p (a e) -> p a e", a=1).to_broadcast([128, NT, NE])
                tiles = IOTA[:, NE + NE * NB:NE + NE * NB + NT * NE].rearrange("p (t e) -> p t e", t=NT)
                step(dve.tensor_tensor(OWN[:, :, :], tiles, ends, ALU.is_ge))
                step(dve.tensor_reduce(ETF[:, :], OWN[:, :, 0:NE - 1], AX.X, ALU.add))
                dve.tensor_copy(ETI[:, :], ETF[0:1, :]).then_inc(v_et, 1)

            def hidden(g, f):
                n = FT * g + f
                w = fwidth(f)
                if not (isinstance(g, int) and n < 2):
                    dve.wait_ge(v_midl, n - 1)
                dve.wait_ge(a_sil, n + 1)
                gate = PS[:, HB[f % 2][1], :] if w == 128 else PS[FL:2 * FL, HB[f % 2][0], :]
                dve.tensor_tensor(MIDF[f % 2][0:w, :], gate, SIL[0:w, 0:GT], ALU.mult)\
                   .then_inc(v_mid, 1)

            def add_shared(g, q, banks=OUTB):
                dve.wait_ge(t_so, 4 * g + q + 1)
                b = 4 * g + q
                row = X[:, b, :] if isinstance(b, int) else X[:, bass.ds(b, 1), :].rearrange("p a d -> p (a d)")
                dve.tensor_tensor(row, PS[:, banks[q % 2], 0:D], row, ALU.add).then_inc(v_so, 1)

            def mid_lo(g, f):
                dve.wait_ge(a_midh, FT * g + f + 1)
                w = fwidth(f)
                dve.tensor_tensor(MID[1][0:w, f, :], MIDF[f % 2][0:w, :], MID[0][0:w, f, :].bitcast(FP32),
                                  ALU.subtract).then_inc(v_midl, 1)

            def shared_group(g, route=False):
                for f in range(2):
                    hidden(g, f)
                if route:
                    choose_experts()
                    dve.wait_ge(d_x, 16)
                for q in range(4):
                    add_shared(g - 1, q)
                    if route and q == 2:
                        counts()
                    if route and q == 3:
                        running_sums(range(2))
                for f in range(2):
                    mid_lo(g, f)
                for f in range(2, FT):
                    hidden(g, f)
                    if route and f == 2:
                        running_sums(range(2, rounds))
                    if route and f == 3:
                        tiles_needed()
                        first_tiles(range(2))
                    if route and f == 4:
                        first_tiles(range(2, NE))
                    if route and f == 5:
                        slots()
                        own_slots()
                        experts_of_tiles()
                    mid_lo(g, f)

            for f in range(FT):
                hidden(0, f)
                mid_lo(0, f)
                for t in between(f):
                    x_lo(t)
            for g in range(1, NG):
                shared_group(g, route=g == 1)
            for q in range(4):
                add_shared(NG - 1, q, OUTB_LAST)

            def gate_hidden(t, par):
                dve.wait_ge(a_es, t + 1)
                if not (isinstance(t, int) and t < 2):
                    dve.wait_ge(t_ey, t - 1)
                h = hidden_of(par)
                dve.tensor_tensor(MRT[par][:, 0:FM], h[:, FM:2 * FM], SIL[:, 0:FM], ALU.mult)
                dve.tensor_tensor(MRT[par][0:FL, FM:FM + P], h[FL:2 * FL, 2 * FM:2 * FM + P], SIL[0:FL, FM:FM + P],
                                  ALU.mult).then_inc(v_em, 1)

            def output(t, par, n):
                dve.wait_ge(t_ey, t + 1)
                dve.wait_ge(d_base[par], 16 * (n + 1))
                if not (isinstance(t, int) and t < 2):
                    dve.wait_ge(d_y[par], 16 * n)
                dve.tensor_tensor(YS[par][:, :], PS[:, EY, 0:D], BASE[par][:, :], ALU.add).then_inc(v_ey, 1)

            gate_hidden(0, 0)
            for t in (1, 2):
                gate_hidden(t, t % 2)
                output(t - 1, (t - 1) % 2, 0)
            with dve.Fori(1, (NT - 1) // 2) as i:
                gate_hidden(2 * i + 1, 1)
                output(2 * i, 0, i)
                gate_hidden(2 * i + 2, 0)
                output(2 * i + 1, 1, i)
            output(NT - 1, 0, NT // 2)

        @block.tensor
        def _(pe):
            def tr_x(t):
                if t >= AHEAD + 2:
                    pe.wait_ge(v_xtl, t - AHEAD - 1)
                transpose_tokens(pe, PS[:, TRB[t % 2], :], C, IDENT, t).then_inc(t_xt, 1)

            def score(t):
                if t >= AHEAD:
                    pe.wait_ge(v_xtl, t - AHEAD + 1)
                todo = [(k, m) for k in range(KD) for m in range(2)]
                for n, (k, m) in enumerate(todo):
                    last = pe.matmul(PS[:, RTB, 2 * NE * t:2 * NE * (t + 1)], XT[m][:, k, P * t:P * (t + 1)],
                                     RTS[:, k, :, :].rearrange("p m e -> p (m e)"), start=n == 0,
                                     stop=n == len(todo) - 1)
                last.then_inc(t_sc, 1)

            def split3(dst, stat, mov, steps):
                todo = [(k, s, m) for k in range(steps) for s, m in ((0, 0), (0, 1), (1, 0))]
                for n, (k, s, m) in enumerate(todo):
                    last = pe.matmul(dst, stat(s, k), mov(m, k), start=n == 0, stop=n == len(todo) - 1)
                return last

            def shared_hidden(g, f):
                n = FT * g + f
                if not (isinstance(n, int) and n < 2):
                    pe.wait_ge(v_mid, n - 1)
                for i in range(2 if f < FT - 1 else 1):
                    c = (FT - 1) * i + f if f < FT - 1 else 2 * (FT - 1)
                    last = split3(PS[:, HB[f % 2][i], :], lambda s, k: lhs13(WS13[s], k, c),
                                  lambda m, k: XT[m][:, k, GT * g:GT * (g + 1)] if isinstance(g, int) else
                                  XT[m][:, k, bass.ds(g * GT, GT)], KD)
                last.then_inc(t_h, 1)

            def shared_out(g, banks=OUTB, ranks=False):
                pe.wait_ge(v_midl, FT * (g + 1))
                for q in range(4):
                    if q == 2 and ranks:
                        pe.wait_ge(v_rt, 9)
                        pe.wait_ge(p_mask, 2)
                        one = ONE[:, :, :].rearrange("p b e -> p (b e)")
                        pe.matmul(PS[:, RTB, 0:NB * NE], UPPER[:, :], one, start=True, stop=True)
                        pe.matmul(PS[:, RTB, NB * NE:2 * NB * NE], ONES[:, :], one, start=True, stop=True)\
                            .then_inc(t_rank, 1)
                    if not (isinstance(g, int) and 4 * g + q < 2):
                        pe.wait_ge(v_so, 4 * g + q - 1)
                    todo = [(f, s, m) for f in range(FT) for s, m in ((0, 0), (0, 1), (1, 0))]
                    for n, (f, s, m) in enumerate(todo):
                        w = fwidth(f)
                        last = pe.matmul(PS[:, banks[q % 2], 0:D], MID[s][0:w, f, P * q:P * (q + 1)],
                                         WS2[m][0:w, f, :], start=n == 0, stop=n == len(todo) - 1)
                    last.then_inc(t_so, 1)

            for f in range(FT):
                shared_hidden(0, f)
                for t in scored(f):
                    score(t)
                for t in between(f):
                    tr_x(t)

            def shared_group(g, ranks=False, last=False):
                if GT // P * (g + 1) > AHEAD:
                    pe.wait_ge(v_xtl, GT // P * (g + 1) - AHEAD)
                for f in range(2):
                    shared_hidden(g, f)
                shared_out(g - 1, ranks=ranks)
                for f in range(2, FT):
                    if last and f == FT - 1:
                        ex(0, 0)
                    shared_hidden(g, f)

            def ex(t, par):
                pe.wait_ge(d_xs[par], 16 * (t // 2 + 1) if isinstance(t, int) else 8 * (t - par) + 16)
                if isinstance(t, int) and t == 0:
                    pe.wait_ge(v_mid, FT * NG - 2)
                else:
                    pe.wait_ge(a_ex, t)
                for k in range(KD):
                    last = pe.transpose(PS[:, EX, P * k:P * (k + 1)], XS[par][:, 128 * k:128 * (k + 1)], IDENT[:, :])
                last.then_inc(t_ex, 1)

            def eh(t, par):
                pe.wait_ge(a_ex, t + 1)
                pe.wait_ge(d_w13[par], 16 * (t // 2 + 1) if isinstance(t, int) else 8 * (t - par) + 16)
                if not (isinstance(t, int) and t < 2):
                    pe.wait_ge(v_em, t - 1)
                h = hidden_of(par)
                for c in range(2 * FT - 1):
                    for k in range(KD):
                        last = pe.matmul(h[:, P * c:P * (c + 1)], lhs13(W13[par], k, c), XST[par][:, k, :],
                                         start=k == 0, stop=k == KD - 1)
                last.then_inc(t_eh, 1)

            def ey(t, par):
                pe.wait_ge(v_em, t + 1)
                pe.wait_ge(d_w2[par], 32 * (t // 2 + 1) if isinstance(t, int) else 16 * (t - par) + 32)
                if isinstance(t, int) and t == 0:
                    pe.wait_ge(v_so, TOK // P)
                else:
                    pe.wait_ge(v_ey, t)
                for f in range(FT):
                    w = fwidth(f)
                    last = pe.matmul(PS[:, EY, 0:D], MRT[par][0:w, P * f:P * (f + 1)], W2[par][0:w, f, :], start=f == 0,
                                     stop=f == FT - 1)
                last.then_inc(t_ey, 1)

            def routed(t, par, following=True):
                if following:
                    ex(t + 1, 1 - par)
                eh(t, par)
                ey(t - 1, 1 - par)

            for g in range(1, NG):
                shared_group(g, ranks=g == 1, last=g == NG - 1)
            pe.wait_ge(v_so, 4 * (NG - 1))
            pe.wait_ge(v_pos, 1)
            eh(0, 0)
            ex(1, 1)
            shared_out(NG - 1, OUTB_LAST)
            pe.wait_ge(v_so, 4 * NG - 1)
            routed(1, 1)
            routed(2, 0)
            with pe.Fori(1, (NT - 3) // 2) as i:
                routed(2 * i + 1, 1)
                routed(2 * i + 2, 0)
            routed(NT - 2, 1)
            routed(NT - 1, 0, following=False)
            ey(NT - 1, 0)


def kernel(x, ctx_1024, cond_1024, L0_xcond_ln1_w, L0_xcond_ln1_b, L0_xcond_ln2_w, L0_xcond_ln2_b, L0_xcond_Wq,
           L0_xcond_Wkv, L0_xcond_Wo, L0_ffn_router_DE, L0_ffn_w1_eDF, L0_ffn_w3_eDF, L0_ffn_w2_eFD, L0_ffn_ws1_DF,
           L0_ffn_ws3_DF, L0_ffn_ws2_FD):
    import numpy as np
    import concourse.bacc as bacc
    from concourse.bass_utils import run_bass_kernel_spmd

    def on_partitions(v):
        v = np.asarray(v)
        return np.moveaxis(v.reshape(v.shape[:-1] + (KD, 128)), -1, 0)

    def hidden_columns(w1, w3):
        w1, w3 = np.asarray(w1), np.asarray(w3)
        w = np.concatenate([w1, w3[..., FM:], w3[..., :FM]], axis=-1)
        return np.swapaxes(w.reshape(w.shape[:-2] + (KD, 128, 2 * F)), -3, -2)

    def hidden_rows(w2):
        w2 = np.asarray(w2)
        return np.swapaxes(w2[..., :FM, :].reshape(w2.shape[:-2] + (FT - 1, 128, D)), -3, -2), w2[..., FM:, :]

    w2, w2_last = hidden_rows(L0_ffn_w2_eFD)
    ws2, ws2_last = hidden_rows(L0_ffn_ws2_FD)
    norms = np.stack([np.asarray(v) for v in (L0_xcond_ln1_w, L0_xcond_ln1_b, L0_xcond_ln2_w, L0_xcond_ln2_b)])
    given = {
        "x": x, "ctx": ctx_1024, "cond": np.moveaxis(on_partitions(cond_1024), 1, 2), "ln": on_partitions(norms),
        "wq_t": np.asarray(L0_xcond_Wq).T, "wkv_t": np.asarray(L0_xcond_Wkv).T, "wo_t": np.asarray(L0_xcond_Wo).T,
        "router": L0_ffn_router_DE, "w13": hidden_columns(L0_ffn_w1_eDF, L0_ffn_w3_eDF), "w2": w2, "w2_last": w2_last,
        "ws13": hidden_columns(L0_ffn_ws1_DF, L0_ffn_ws3_DF), "ws2": ws2, "ws2_last": ws2_last,
    }
    nc = bacc.Bacc("TRN2", target_bir_lowering=False, num_devices=1)
    arrays, aps = {}, {}
    for name, value in given.items():
        value = np.ascontiguousarray(value)
        arrays[f"in_{name}"] = value
        aps[name] = nc.dram_tensor(f"in_{name}", value.shape, mybir.dt.from_np(value.dtype), kind="ExternalInput").ap()
    result = nc.dram_tensor("out_x", (NB, P, D), FP32, kind="ExternalOutput").ap()
    build(nc, aps, result)
    r = run_bass_kernel_spmd(nc, [arrays], core_ids=[0])
    return r.results[0]["out_x"]
```
